# Optimizing a Trainium2 kernel written in Bass

```python
import numpy as np
import jax
import jax.numpy as jnp

def _softmax(x, axis=-1):
    return jax.nn.softmax(x, axis=axis)

def _gelu(x):
    return jax.nn.gelu(x, approximate=True)

def _silu(x):
    return jax.nn.silu(x)

def _sigmoid(x):
    return jax.nn.sigmoid(x)

def _layernorm(x, axis=-1, eps=1e-05):
    m = jnp.mean(x, axis=axis, keepdims=True)
    v = jnp.var(x, axis=axis, keepdims=True)
    return (x - m) / jnp.sqrt(v + eps)

def _scatter_add(tgt, idx, src, axis=0):
    return tgt.at[idx].add(src)

def _segment_sum(src, seg, n):
    return jax.ops.segment_sum(src, seg, n)
kernel_name = 'mk_vit_tower_d4_tok_img768_r4_e803e8'

def setup_inputs(seed: int=0):
    np.random.seed(seed)
    _w = jnp.asarray

    def _rec_inputs():
        import jax
        import jax.numpy as jnp
        _rk = jax.random.key(seed)
        x = -0.00016672 + 0.999947 * jax.random.normal(jax.random.fold_in(_rk, 1), (64, 3, 96, 96), jnp.float32)
        return x
    x = _rec_inputs()

    def _L0_tok_setup():
        import math
        import jax, jax.numpy as jnp
        import numpy as np
        IMG = (96, 96)
        PATCH = (16, 16)
        CH = 3
        LEN = 192
        B = 64
        NPATCH = IMG[0] // PATCH[0] * (IMG[1] // PATCH[1])

        def _pos_encoding(n_patch, length, dtype):
            i = jnp.arange(n_patch, dtype=dtype)[:, None]
            j = jnp.arange(length)
            expo = (2 * (j // 2)).astype(dtype) / length
            angle = i / jnp.power(jnp.asarray(10000.0, dtype), expo)
            angle = angle + jnp.where(j % 2 == 1, jnp.asarray(math.pi / 2, dtype), 0.0)
            return jnp.sin(angle)
        key = jax.random.key(seed)
        k1, k2, k3 = jax.random.split(key, 3)
        x = jax.random.normal(k1, (B, CH, IMG[0], IMG[1]), dtype=jnp.float32)
        fan_in = CH * PATCH[0] * PATCH[1]
        std = math.sqrt(2.0 / fan_in)
        W = jax.random.normal(k2, (LEN, CH, PATCH[0], PATCH[1]), dtype=jnp.float32) * std
        b = jax.random.normal(k3, (LEN,), dtype=jnp.float32) * 0.01
        return {'x': x, 'W': W, 'b': b}
    _L0_tok_all = _L0_tok_setup()
    _L0_tok_in = {k: v for k, v in _L0_tok_all.items() if k in ('W', 'b')}
    del _L0_tok_all

    def _L0_attn_setup():
        import jax, jax.numpy as jnp
        import numpy as np
        B, L, D, M = (1, 512, 192, 64)
        key = jax.random.key(seed)
        ks = jax.random.split(key, 9)

        def w(k, shape):
            return jax.random.normal(k, shape, jnp.float32) * shape[0] ** (-0.5)
        x = jax.random.normal(ks[0], (B, L, D), jnp.float32)
        Wq = w(ks[1], (D, M))
        Wk = w(ks[2], (D, M))
        Wv = w(ks[3], (D, D))
        Wf = w(ks[4], (D, M))
        bf = jnp.zeros((M,), jnp.float32)
        Wo = w(ks[5], (D, D))
        gamma = jnp.ones((D,), jnp.float32)
        beta = jnp.zeros((D,), jnp.float32)
        return {'x': x, 'Wq': Wq, 'Wk': Wk, 'Wv': Wv, 'Wf': Wf, 'bf': bf, 'Wo': Wo, 'gamma': gamma, 'beta': beta}
    _L0_attn_all = _L0_attn_setup()
    _L0_attn_in = {k: v for k, v in _L0_attn_all.items() if k in ('Wq', 'Wk', 'Wv', 'Wf', 'bf', 'Wo', 'gamma', 'beta')}
    del _L0_attn_all

    def _L0_ffn_setup():
        import jax, jax.numpy as jnp
        import numpy as np
        B, L, D, H, F = (4, 512, 192, 12, 768)
        ROUTE_FRAC = 0.15
        LN_EPS = 1e-05

        def _ln(x, g, b):
            m = jnp.mean(x, axis=-1, keepdims=True)
            v = jnp.mean((x - m) ** 2, axis=-1, keepdims=True)
            return (x - m) * jax.lax.rsqrt(v + LN_EPS) * g + b
        key = jax.random.key(seed)
        ks = jax.random.split(key, 20)
        s = 0.02
        return {'hidden_states': jax.random.normal(ks[0], (B, L, D), dtype=jnp.float32), 'g1': jnp.ones((D,), jnp.float32), 'b1': jnp.zeros((D,), jnp.float32), 'g2': jnp.ones((D,), jnp.float32), 'b2': jnp.zeros((D,), jnp.float32), 'Wr': jax.random.normal(ks[1], (D,), jnp.float32) * s, 'br': jnp.zeros((), jnp.float32), 'Wq': jax.random.normal(ks[2], (D, D), jnp.float32) * s, 'bq': jnp.zeros((D,), jnp.float32), 'Wk': jax.random.normal(ks[3], (D, D), jnp.float32) * s, 'bk': jnp.zeros((D,), jnp.float32), 'Wv': jax.random.normal(ks[4], (D, D), jnp.float32) * s, 'bv': jnp.zeros((D,), jnp.float32), 'Wo': jax.random.normal(ks[5], (D, D), jnp.float32) * s, 'bo': jnp.zeros((D,), jnp.float32), 'Wm': jax.random.normal(ks[6], (D, D), jnp.float32) * s, 'bm': jnp.zeros((D,), jnp.float32), 'W1': jax.random.normal(ks[7], (D, F), jnp.float32) * s, 'bf1': jnp.zeros((F,), jnp.float32), 'W2': jax.random.normal(ks[8], (F, D), jnp.float32) * s, 'bf2': jnp.zeros((D,), jnp.float32)}
    _L0_ffn_all = _L0_ffn_setup()
    _L0_ffn_in = {k: v for k, v in _L0_ffn_all.items() if k in ('g1', 'b1', 'g2', 'b2', 'Wr', 'br', 'Wq', 'bq', 'Wk', 'bk', 'Wv', 'bv', 'Wo', 'bo', 'Wm', 'bm', 'W1', 'bf1', 'W2', 'bf2')}
    del _L0_ffn_all

    def _L1_attn_setup():
        import jax, jax.numpy as jnp
        import numpy as np
        D_MODEL = 192
        D_STATE = 16
        BATCH = 2
        SEQLEN = 512
        key = jax.random.key(seed)
        ks = jax.random.split(key, 8)
        s = 0.02
        return {'x': jax.random.normal(ks[0], (BATCH, SEQLEN, D_MODEL), dtype=jnp.float32), 'log_lambda': jax.random.uniform(ks[1], (D_MODEL, D_STATE), dtype=jnp.float32), 'Wd': jax.random.normal(ks[2], (D_MODEL, D_MODEL), dtype=jnp.float32) * s, 'bd': jax.random.normal(ks[3], (D_MODEL,), dtype=jnp.float32) * s, 'WB': jax.random.normal(ks[4], (D_STATE, D_MODEL), dtype=jnp.float32) * s, 'WC': jax.random.normal(ks[5], (D_STATE, D_MODEL), dtype=jnp.float32) * s, 'Wout': jax.random.normal(ks[6], (D_MODEL, D_MODEL * D_STATE), dtype=jnp.float32) * s, 'bout': jax.random.normal(ks[7], (D_MODEL,), dtype=jnp.float32) * s}
    _L1_attn_all = _L1_attn_setup()
    _L1_attn_in = {k: v for k, v in _L1_attn_all.items() if k in ('log_lambda', 'Wd', 'bd', 'WB', 'WC', 'Wout', 'bout')}
    del _L1_attn_all

    def _L1_ffn_setup():
        import jax, jax.numpy as jnp
        import numpy as np
        B, T, H, F, E = (128, 32, 192, 768, 3)
        key = jax.random.key(seed)
        ks = jax.random.split(key, 4)
        s = 0.02
        return {'x': jax.random.normal(ks[0], (B, T, H), jnp.float32), 'Wg': jax.random.normal(ks[1], (E, H), jnp.float32) * s, 'W1': jax.random.normal(ks[2], (E, H, F), jnp.float32) * s, 'b1': jnp.zeros((E, F), jnp.float32), 'W2': jax.random.normal(ks[3], (E, F, H), jnp.float32) * s, 'b2': jnp.zeros((E, H), jnp.float32)}
    _L1_ffn_all = _L1_ffn_setup()
    _L1_ffn_in = {k: v for k, v in _L1_ffn_all.items() if k in ('Wg', 'W1', 'b1', 'W2', 'b2')}
    del _L1_ffn_all

    def _L2_attn_setup():
        import jax, jax.numpy as jnp
        import numpy as np
        EMBED_DIM = 192
        SEQ_LEN = 256
        BATCH = 16
        ALPHA = 0.99
        key = jax.random.key(seed)
        k_x, k_w, k_b = jax.random.split(key, 3)
        d = EMBED_DIM
        x = jax.random.normal(k_x, (BATCH, SEQ_LEN, d), dtype=jnp.float32)
        lim = 1.0 / np.sqrt(d)
        W_qkv = jax.random.uniform(k_w, (3 * d, d), dtype=jnp.float32, minval=-lim, maxval=lim)
        b_qkv = jax.random.uniform(k_b, (3 * d,), dtype=jnp.float32, minval=-lim, maxval=lim)
        return {'x': x, 'W_qkv': W_qkv, 'b_qkv': b_qkv}
    _L2_attn_all = _L2_attn_setup()
    _L2_attn_in = {k: v for k, v in _L2_attn_all.items() if k in ('W_qkv', 'b_qkv')}
    del _L2_attn_all

    def _L2_ffn_setup():
        import jax, jax.numpy as jnp
        import numpy as np
        DIM = 192
        HID = 4 * DIM
        NUM_EXPERTS = 3
        TOP_K = 2
        R = 8
        ALPHA = 8
        SCALING = ALPHA / R
        key = jax.random.key(seed)
        ks = jax.random.split(key, 9)
        B, N = (64, 196)
        return {'x': jax.random.normal(ks[0], (B, N, DIM), jnp.float32), 'w1': jax.random.normal(ks[1], (DIM, HID), jnp.float32) * (1.0 / np.sqrt(DIM)), 'b1': jax.random.normal(ks[2], (HID,), jnp.float32) * 0.01, 'w2': jax.random.normal(ks[3], (HID, DIM), jnp.float32) * (1.0 / np.sqrt(HID)), 'b2': jax.random.normal(ks[4], (DIM,), jnp.float32) * 0.01, 'router_w': jax.random.normal(ks[5], (DIM, NUM_EXPERTS), jnp.float32) * (1.0 / np.sqrt(DIM)), 'router_b': jax.random.normal(ks[6], (NUM_EXPERTS,), jnp.float32) * 0.01, 'w_down': jax.random.normal(ks[7], (NUM_EXPERTS, DIM, R), jnp.float32) * (1.0 / np.sqrt(DIM)), 'w_up': jax.random.normal(ks[8], (NUM_EXPERTS, R, DIM), jnp.float32) * 0.02}
    _L2_ffn_all = _L2_ffn_setup()
    _L2_ffn_in = {k: v for k, v in _L2_ffn_all.items() if k in ('w1', 'b1', 'w2', 'b2', 'router_w', 'router_b', 'w_down', 'w_up')}
    del _L2_ffn_all

    def _L3_attn_setup():
        import jax, jax.numpy as jnp
        import numpy as np
        import math
        D_MODEL = 192
        D_STATE = 16
        D_CONV = 4
        EXPAND = 2
        N_EXP = 8
        TOP_K = 2
        D_INNER = D_MODEL * EXPAND
        D_FF = 4 * D_MODEL
        B_SZ, T_LEN = (2, 256)
        EPS = 1e-06

        def _rms(x, g):
            return x * jax.lax.rsqrt(jnp.mean(x * x, axis=-1, keepdims=True) + EPS) * g
        key = jax.random.key(seed)
        ks = jax.random.split(key, 12)
        s = 0.02
        x = jax.random.normal(ks[0], (B_SZ, T_LEN, D_MODEL), jnp.float32)
        g_mamba = jnp.ones((D_MODEL,), jnp.float32)
        w_in = jax.random.normal(ks[1], (D_MODEL, 2 * D_INNER), jnp.float32) * s
        conv_w = jax.random.normal(ks[2], (D_INNER, D_CONV), jnp.float32) * s
        conv_b = jnp.zeros((D_INNER,), jnp.float32)
        w_xproj = jax.random.normal(ks[3], (D_INNER, 2 * D_STATE + 1), jnp.float32) * s
        w_dt = jax.random.normal(ks[4], (1, D_INNER), jnp.float32) * s
        b_dt = jnp.full((D_INNER,), math.log(0.001), jnp.float32)
        A_log = jnp.log(jnp.arange(1, D_STATE + 1, dtype=jnp.float32)) * jnp.ones((D_INNER, 1), jnp.float32)
        D_skip = jnp.ones((D_INNER,), jnp.float32)
        w_out = jax.random.normal(ks[5], (D_INNER, D_MODEL), jnp.float32) * s
        g_moe = jnp.ones((D_MODEL,), jnp.float32)
        w_router = jax.random.normal(ks[6], (D_MODEL, N_EXP), jnp.float32) * s
        g_exp = jnp.ones((N_EXP, D_MODEL), jnp.float32)
        w1 = jax.random.normal(ks[7], (N_EXP, D_MODEL, D_FF), jnp.float32) * s
        w3 = jax.random.normal(ks[8], (N_EXP, D_MODEL, D_FF), jnp.float32) * s
        w2 = jax.random.normal(ks[9], (N_EXP, D_FF, D_MODEL), jnp.float32) * s
        return dict(x=x, g_mamba=g_mamba, w_in=w_in, conv_w=conv_w, conv_b=conv_b, w_xproj=w_xproj, w_dt=w_dt, b_dt=b_dt, A_log=A_log, D_skip=D_skip, w_out=w_out, g_moe=g_moe, w_router=w_router, g_exp=g_exp, w1=w1, w3=w3, w2=w2)
    _L3_attn_all = _L3_attn_setup()
    _L3_attn_in = {k: v for k, v in _L3_attn_all.items() if k in ('g_mamba', 'w_in', 'conv_w', 'conv_b', 'w_xproj', 'w_dt', 'b_dt', 'A_log', 'D_skip', 'w_out', 'g_moe', 'w_router', 'g_exp', 'w1', 'w3', 'w2')}
    del _L3_attn_all

    def _L3_ffn_setup():
        import jax, jax.numpy as jnp
        import numpy as np
        E = 128
        I = 464
        IS = 928
        K = 6
        G = 1
        TG = 1
        SCALE = 2.5
        CAP = 192

        def moe_forward(hidden_states, Wg, e_bias, W_gate_up, W_down, Wsg, Wsu, Wsd):
            B, S, H = hidden_states.shape
            x = hidden_states.reshape(-1, H)
            T = x.shape[0]
            logits = x.astype(jnp.float32) @ Wg.T
            sig = jax.nn.sigmoid(logits)
            choice = sig + e_bias[None, :]
            grp = choice.reshape(T, G, E // G)
            group_scores = jax.lax.top_k(grp, 2)[0].sum(-1)
            gidx = jax.lax.top_k(group_scores, TG)[1]
            gmask = jnp.zeros((T, G), jnp.float32).at[jnp.arange(T)[:, None], gidx].set(1.0)
            smask = jnp.repeat(gmask, E // G, axis=1)
            scores_for_choice = jnp.where(smask > 0, choice, 0.0)
            topk_idx = jax.lax.top_k(scores_for_choice, K)[1]
            topk_w = jnp.take_along_axis(sig, topk_idx, axis=1)
            topk_w = topk_w / (topk_w.sum(-1, keepdims=True) + 1e-20)
            topk_w = topk_w * SCALE
            P = T * K
            flat_e = topk_idx.reshape(-1)
            order = jnp.argsort(flat_e)
            se = flat_e[order]
            counts = jax.ops.segment_sum(jnp.ones(P, jnp.int32), flat_e, num_segments=E)
            starts = jnp.cumsum(counts) - counts
            pos = jnp.arange(P) - starts[se]
            buf_idx = jnp.where(pos < CAP, se * CAP + pos, E * CAP)
            tok_of_pair = (order // K).astype(jnp.int32)
            w_of_pair = topk_w.reshape(-1)[order]
            token_buf = jnp.zeros((E * CAP,), jnp.int32).at[buf_idx].set(tok_of_pair, mode='drop')
            w_buf = jnp.zeros((E * CAP,), x.dtype).at[buf_idx].set(w_of_pair.astype(x.dtype), mode='drop')
            xb = x[token_buf].reshape(E, CAP, H)
            gu = jnp.einsum('ech,ehf->ecf', xb, W_gate_up)
            g, u = jnp.split(gu, 2, axis=-1)
            inter = jax.nn.silu(g) * u
            yb = jnp.einsum('eci,eih->ech', inter, W_down)
            yb = yb * w_buf.reshape(E, CAP, 1)
            routed = jnp.zeros((T, H), x.dtype).at[token_buf].add(yb.reshape(E * CAP, H))
            shared = jax.nn.silu(x @ Wsg) * (x @ Wsu) @ Wsd
            return (routed + shared).reshape(B, S, H)
        key = jax.random.key(seed)
        ks = jax.random.split(key, 8)
        B, S, H = (1, 512, 192)
        sc = 0.02
        return {'hidden_states': jax.random.normal(ks[0], (B, S, H), jnp.float32), 'Wg': jax.random.normal(ks[1], (E, H), jnp.float32) * sc, 'e_bias': jnp.zeros((E,), jnp.float32), 'W_gate_up': jax.random.normal(ks[2], (E, H, 2 * I), jnp.float32) * sc, 'W_down': jax.random.normal(ks[3], (E, I, H), jnp.float32) * sc, 'Wsg': jax.random.normal(ks[4], (H, IS), jnp.float32) * sc, 'Wsu': jax.random.normal(ks[5], (H, IS), jnp.float32) * sc, 'Wsd': jax.random.normal(ks[6], (IS, H), jnp.float32) * sc}
    _L3_ffn_all = _L3_ffn_setup()
    _L3_ffn_in = {k: v for k, v in _L3_ffn_all.items() if k in ('Wg', 'e_bias', 'W_gate_up', 'W_down', 'Wsg', 'Wsu', 'Wsd')}
    del _L3_ffn_all
    return {'x': x, 'L0_tok_W': _L0_tok_in['W'], 'L0_tok_b': _L0_tok_in['b'], 'L0_attn_Wq': _L0_attn_in['Wq'], 'L0_attn_Wk': _L0_attn_in['Wk'], 'L0_attn_Wv': _L0_attn_in['Wv'], 'L0_attn_Wf': _L0_attn_in['Wf'], 'L0_attn_bf': _L0_attn_in['bf'], 'L0_attn_Wo': _L0_attn_in['Wo'], 'L0_attn_gamma': _L0_attn_in['gamma'], 'L0_attn_beta': _L0_attn_in['beta'], 'L0_ffn_g1': _L0_ffn_in['g1'], 'L0_ffn_b1': _L0_ffn_in['b1'], 'L0_ffn_g2': _L0_ffn_in['g2'], 'L0_ffn_b2': _L0_ffn_in['b2'], 'L0_ffn_Wr': _L0_ffn_in['Wr'], 'L0_ffn_br': _L0_ffn_in['br'], 'L0_ffn_Wq': _L0_ffn_in['Wq'], 'L0_ffn_bq': _L0_ffn_in['bq'], 'L0_ffn_Wk': _L0_ffn_in['Wk'], 'L0_ffn_bk': _L0_ffn_in['bk'], 'L0_ffn_Wv': _L0_ffn_in['Wv'], 'L0_ffn_bv': _L0_ffn_in['bv'], 'L0_ffn_Wo': _L0_ffn_in['Wo'], 'L0_ffn_bo': _L0_ffn_in['bo'], 'L0_ffn_Wm': _L0_ffn_in['Wm'], 'L0_ffn_bm': _L0_ffn_in['bm'], 'L0_ffn_W1': _L0_ffn_in['W1'], 'L0_ffn_bf1': _L0_ffn_in['bf1'], 'L0_ffn_W2': _L0_ffn_in['W2'], 'L0_ffn_bf2': _L0_ffn_in['bf2'], 'L1_attn_log_lambda': _L1_attn_in['log_lambda'], 'L1_attn_Wd': _L1_attn_in['Wd'], 'L1_attn_bd': _L1_attn_in['bd'], 'L1_attn_WB': _L1_attn_in['WB'], 'L1_attn_WC': _L1_attn_in['WC'], 'L1_attn_Wout': _L1_attn_in['Wout'], 'L1_attn_bout': _L1_attn_in['bout'], 'L1_ffn_Wg': _L1_ffn_in['Wg'], 'L1_ffn_W1': _L1_ffn_in['W1'], 'L1_ffn_b1': _L1_ffn_in['b1'], 'L1_ffn_W2': _L1_ffn_in['W2'], 'L1_ffn_b2': _L1_ffn_in['b2'], 'L2_attn_W_qkv': _L2_attn_in['W_qkv'], 'L2_attn_b_qkv': _L2_attn_in['b_qkv'], 'L2_ffn_w1': _L2_ffn_in['w1'], 'L2_ffn_b1': _L2_ffn_in['b1'], 'L2_ffn_w2': _L2_ffn_in['w2'], 'L2_ffn_b2': _L2_ffn_in['b2'], 'L2_ffn_router_w': _L2_ffn_in['router_w'], 'L2_ffn_router_b': _L2_ffn_in['router_b'], 'L2_ffn_w_down': _L2_ffn_in['w_down'], 'L2_ffn_w_up': _L2_ffn_in['w_up'], 'L3_attn_g_mamba': _L3_attn_in['g_mamba'], 'L3_attn_w_in': _L3_attn_in['w_in'], 'L3_attn_conv_w': _L3_attn_in['conv_w'], 'L3_attn_conv_b': _L3_attn_in['conv_b'], 'L3_attn_w_xproj': _L3_attn_in['w_xproj'], 'L3_attn_w_dt': _L3_attn_in['w_dt'], 'L3_attn_b_dt': _L3_attn_in['b_dt'], 'L3_attn_A_log': _L3_attn_in['A_log'], 'L3_attn_D_skip': _L3_attn_in['D_skip'], 'L3_attn_w_out': _L3_attn_in['w_out'], 'L3_attn_g_moe': _L3_attn_in['g_moe'], 'L3_attn_w_router': _L3_attn_in['w_router'], 'L3_attn_g_exp': _L3_attn_in['g_exp'], 'L3_attn_w1': _L3_attn_in['w1'], 'L3_attn_w3': _L3_attn_in['w3'], 'L3_attn_w2': _L3_attn_in['w2'], 'L3_ffn_Wg': _L3_ffn_in['Wg'], 'L3_ffn_e_bias': _L3_ffn_in['e_bias'], 'L3_ffn_W_gate_up': _L3_ffn_in['W_gate_up'], 'L3_ffn_W_down': _L3_ffn_in['W_down'], 'L3_ffn_Wsg': _L3_ffn_in['Wsg'], 'L3_ffn_Wsu': _L3_ffn_in['Wsu'], 'L3_ffn_Wsd': _L3_ffn_in['Wsd']}

def reference(x, L0_tok_W, L0_tok_b, L0_attn_Wq, L0_attn_Wk, L0_attn_Wv, L0_attn_Wf, L0_attn_bf, L0_attn_Wo, L0_attn_gamma, L0_attn_beta, L0_ffn_g1, L0_ffn_b1, L0_ffn_g2, L0_ffn_b2, L0_ffn_Wr, L0_ffn_br, L0_ffn_Wq, L0_ffn_bq, L0_ffn_Wk, L0_ffn_bk, L0_ffn_Wv, L0_ffn_bv, L0_ffn_Wo, L0_ffn_bo, L0_ffn_Wm, L0_ffn_bm, L0_ffn_W1, L0_ffn_bf1, L0_ffn_W2, L0_ffn_bf2, L1_attn_log_lambda, L1_attn_Wd, L1_attn_bd, L1_attn_WB, L1_attn_WC, L1_attn_Wout, L1_attn_bout, L1_ffn_Wg, L1_ffn_W1, L1_ffn_b1, L1_ffn_W2, L1_ffn_b2, L2_attn_W_qkv, L2_attn_b_qkv, L2_ffn_w1, L2_ffn_b1, L2_ffn_w2, L2_ffn_b2, L2_ffn_router_w, L2_ffn_router_b, L2_ffn_w_down, L2_ffn_w_up, L3_attn_g_mamba, L3_attn_w_in, L3_attn_conv_w, L3_attn_conv_b, L3_attn_w_xproj, L3_attn_w_dt, L3_attn_b_dt, L3_attn_A_log, L3_attn_D_skip, L3_attn_w_out, L3_attn_g_moe, L3_attn_w_router, L3_attn_g_exp, L3_attn_w1, L3_attn_w3, L3_attn_w2, L3_ffn_Wg, L3_ffn_e_bias, L3_ffn_W_gate_up, L3_ffn_W_down, L3_ffn_Wsg, L3_ffn_Wsu, L3_ffn_Wsd):
    import jax
    import jax.numpy as jnp

    def _L0_tok_ref(x, W, b):
        import math
        import jax, jax.numpy as jnp
        import numpy as np
        IMG = (96, 96)
        PATCH = (16, 16)
        CH = 3
        LEN = 192
        B = 64
        NPATCH = IMG[0] // PATCH[0] * (IMG[1] // PATCH[1])

        def _pos_encoding(n_patch, length, dtype):
            i = jnp.arange(n_patch, dtype=dtype)[:, None]
            j = jnp.arange(length)
            expo = (2 * (j // 2)).astype(dtype) / length
            angle = i / jnp.power(jnp.asarray(10000.0, dtype), expo)
            angle = angle + jnp.where(j % 2 == 1, jnp.asarray(math.pi / 2, dtype), 0.0)
            return jnp.sin(angle)
        y = jax.lax.conv_general_dilated(x, W, window_strides=PATCH, padding='VALID', dimension_numbers=('NCHW', 'OIHW', 'NCHW'))
        y = y + b[None, :, None, None]
        Bn, L, Hp, Wp = y.shape
        y = y.reshape(Bn, L, Hp * Wp).transpose(0, 2, 1)
        pos = _pos_encoding(Hp * Wp, L, y.dtype)
        return y + pos[None, :, :]

    def _L0_attn_ref(x, Wq, Wk, Wv, Wf, bf, Wo, gamma, beta):
        import jax, jax.numpy as jnp
        import numpy as np
        B, L, D, M = (1, 512, 192, 64)
        m_dim = Wq.shape[1]
        scale = m_dim ** (-0.5)
        q = (jax.nn.elu(x @ Wq) + 1.0) * scale
        k = jax.nn.elu(x @ Wk) + 1.0
        v = x @ Wv
        forget = jax.nn.sigmoid(x @ Wf + bf)
        log_f = jnp.log(jnp.clip(forget, 1e-06, None))
        log_f_cum = jnp.clip(jnp.cumsum(log_f, axis=1), -20.0, 20.0)
        exp_neg = jnp.exp(-log_f_cum)
        exp_pos = jnp.exp(log_f_cum)
        kv = k[..., :, None] * v[..., None, :]
        cum_kv = jnp.cumsum(exp_neg[..., None] * kv, axis=1)
        Mstate = exp_pos[..., None] * cum_kv
        z = exp_pos * jnp.cumsum(exp_neg * k, axis=1)
        numerator = jnp.einsum('blm,blmd->bld', q, Mstate)
        denominator = jnp.einsum('blm,blm->bl', q, z)[..., None] + 1e-06
        h = numerator / denominator
        mu = jnp.mean(h, axis=-1, keepdims=True)
        var = jnp.var(h, axis=-1, keepdims=True)
        normed = (h - mu) / jnp.sqrt(var + 1e-05) * gamma + beta
        return normed @ Wo

    def _L0_ffn_ref(hidden_states, g1, b1, g2, b2, Wr, br, Wq, bq, Wk, bk, Wv, bv, Wo, bo, Wm, bm, W1, bf1, W2, bf2):
        import jax, jax.numpy as jnp
        import numpy as np
        B, L, D, H, F = (4, 512, 192, 12, 768)
        ROUTE_FRAC = 0.15
        LN_EPS = 1e-05

        def _ln(x, g, b):
            m = jnp.mean(x, axis=-1, keepdims=True)
            v = jnp.mean((x - m) ** 2, axis=-1, keepdims=True)
            return (x - m) * jax.lax.rsqrt(v + LN_EPS) * g + b
        b, l, d = hidden_states.shape
        dh = d // H
        normed = _ln(hidden_states, g1, b1)
        scores = jax.nn.sigmoid(jnp.einsum('bld,d->bl', normed, Wr) + br)
        k = max(1, int(round(ROUTE_FRAC * l)))
        _, idx = jax.lax.top_k(-scores, k)
        attn_mask = jnp.zeros((b, l), bool).at[jnp.arange(b)[:, None], idx].set(True)
        q = (normed @ Wq + bq).reshape(b, l, H, dh)
        kk = (normed @ Wk + bk).reshape(b, l, H, dh)
        v = (normed @ Wv + bv).reshape(b, l, H, dh)
        logits = jnp.einsum('blhd,bmhd->bhlm', q, kk) / jnp.sqrt(jnp.float32(dh))
        probs = jax.nn.softmax(logits, axis=-1)
        ctx = jnp.einsum('bhlm,bmhd->blhd', probs, v).reshape(b, l, d)
        attn_out = ctx @ Wo + bo
        w = scores / (jnp.sum(scores, axis=1, keepdims=True) + 1e-06)
        pooled = jnp.einsum('bl,bld->bd', w, normed)
        mix_out = (normed + scores[..., None] * pooled[:, None, :]) @ Wm + bm
        merged = jnp.where(attn_mask[..., None], attn_out, mix_out)
        h = hidden_states + merged
        n2 = _ln(h, g2, b2)
        ffn = jax.nn.gelu(n2 @ W1 + bf1, approximate=False) @ W2 + bf2
        return h + ffn

    def _L1_attn_ref(x, log_lambda, Wd, bd, WB, WC, Wout, bout):
        import jax, jax.numpy as jnp
        import numpy as np
        D_MODEL = 192
        D_STATE = 16
        BATCH = 2
        SEQLEN = 512
        B, L, D = x.shape
        N = log_lambda.shape[1]
        lam = jax.nn.softplus(log_lambda)
        delta = jax.nn.softplus(jnp.einsum('bld,ed->ble', x, Wd) + bd)
        Bt = jnp.einsum('bld,nd->bln', x, WB)
        Ct = jnp.einsum('bld,nd->bln', x, WC)
        A_d = jnp.exp(-delta[..., None] * lam)
        B_d = delta[..., None] * Bt[:, :, None, :]

        def step(h, inp):
            a, b, c = inp
            h = a * h + b
            y = h * c[:, None, :]
            return (h, y)
        h0 = jnp.zeros((B, D, N), dtype=x.dtype)
        xs = (jnp.swapaxes(A_d, 0, 1), jnp.swapaxes(B_d, 0, 1), jnp.swapaxes(Ct, 0, 1))
        _, ys = jax.lax.scan(step, h0, xs)
        flat = jnp.swapaxes(ys, 0, 1).reshape(B, L, D * N)
        out = jnp.einsum('blk,dk->bld', flat, Wout) + bout
        return out

    def _L1_ffn_ref(x, Wg, W1, b1, W2, b2):
        import jax, jax.numpy as jnp
        import numpy as np
        B, T, H, F, E = (128, 32, 192, 768, 3)
        scores = jax.nn.softmax(jnp.mean(x, axis=1) @ Wg.T, axis=-1)
        _, idx = jax.lax.top_k(scores, 1)
        sel = idx[:, 0]
        h = jax.nn.gelu(jnp.einsum('bth,ehf->betf', x, W1) + b1[None, :, None, :], approximate=False)
        y = jnp.einsum('betf,efh->beth', h, W2) + b2[None, :, None, :]
        w = scores * jax.nn.one_hot(sel, E, dtype=scores.dtype)
        out = jnp.einsum('beth,be->bth', y, w)
        return out

    def _L2_attn_ref(x, W_qkv, b_qkv):
        import jax, jax.numpy as jnp
        import numpy as np
        EMBED_DIM = 192
        SEQ_LEN = 256
        BATCH = 16
        ALPHA = 0.99
        bs, sl, d = x.shape
        qkv = x @ W_qkv.T + b_qkv
        q, k, v = jnp.split(qkv, 3, axis=-1)
        idx = jnp.arange(sl)
        diff = idx[:, None] - idx[None, :]
        M = jnp.where(diff >= 0, jnp.float32(ALPHA) ** diff.astype(jnp.float32), 0.0)
        dim_sqrt = jnp.asarray(d, jnp.float32) ** 0.5
        scores = jnp.einsum('bsd,btd->bst', q, k) / dim_sqrt * M
        out = jnp.einsum('bst,btd->bsd', scores, v)
        return out

    def _L2_ffn_ref(x, w1, b1, w2, b2, router_w, router_b, w_down, w_up):
        import jax, jax.numpy as jnp
        import numpy as np
        DIM = 192
        HID = 4 * DIM
        NUM_EXPERTS = 3
        TOP_K = 2
        R = 8
        ALPHA = 8
        SCALING = ALPHA / R
        orig_out = jax.nn.gelu(x @ w1 + b1, approximate=False) @ w2 + b2
        orig_shape = x.shape
        xf = x.reshape(-1, orig_shape[-1])
        gate_probs = jax.nn.softmax(xf @ router_w + router_b, axis=-1)
        topk_probs, topk_idx = jax.lax.top_k(gate_probs, TOP_K)
        topk_probs = topk_probs / (topk_probs.sum(axis=-1, keepdims=True) + 1e-06)
        onehot = jax.nn.one_hot(topk_idx, NUM_EXPERTS, dtype=xf.dtype)
        comb_w = (onehot * topk_probs[..., None]).sum(axis=1)
        down = jnp.einsum('td,edr->ter', xf, w_down)
        act = jax.nn.gelu(down, approximate=False)
        up = jnp.einsum('ter,erd->ted', act, w_up) * SCALING
        moe_out = jnp.einsum('ted,te->td', up, comb_w)
        return orig_out + moe_out.reshape(orig_shape)

    def _L3_attn_ref(x, g_mamba, w_in, conv_w, conv_b, w_xproj, w_dt, b_dt, A_log, D_skip, w_out, g_moe, w_router, g_exp, w1, w3, w2):
        import jax, jax.numpy as jnp
        import numpy as np
        import math
        D_MODEL = 192
        D_STATE = 16
        D_CONV = 4
        EXPAND = 2
        N_EXP = 8
        TOP_K = 2
        D_INNER = D_MODEL * EXPAND
        D_FF = 4 * D_MODEL
        B_SZ, T_LEN = (2, 256)
        EPS = 1e-06

        def _rms(x, g):
            return x * jax.lax.rsqrt(jnp.mean(x * x, axis=-1, keepdims=True) + EPS) * g
        B, T, _ = x.shape
        residual = x
        h = _rms(x, g_mamba)
        xz = h @ w_in
        x_s, z = jnp.split(xz, 2, axis=-1)
        xpad = jnp.pad(x_s, ((0, 0), (D_CONV - 1, 0), (0, 0)))
        xc = conv_b + sum((xpad[:, k:k + T, :] * conv_w[:, k] for k in range(D_CONV)))
        xc = jax.nn.silu(xc)
        params = xc @ w_xproj
        B_coef = params[..., :D_STATE]
        C_coef = params[..., D_STATE:2 * D_STATE]
        log_dt = params[..., -1:]
        dt = jax.nn.softplus(log_dt @ w_dt + b_dt)
        A = -jnp.exp(A_log)
        dt_e = dt[..., None]
        A_bar = jnp.exp(dt_e * A)
        Bu = dt_e * B_coef[:, :, None, :] * xc[..., None]

        def step(hst, inp):
            Ab, bu, c = inp
            hst = Ab * hst + bu
            return (hst, jnp.einsum('bds,bs->bd', hst, c))
        h0 = jnp.zeros((B, D_INNER, D_STATE), x.dtype)
        _, ys = jax.lax.scan(step, h0, (jnp.swapaxes(A_bar, 0, 1), jnp.swapaxes(Bu, 0, 1), jnp.swapaxes(C_coef, 0, 1)))
        y = jnp.swapaxes(ys, 0, 1)
        y = y + xc * D_skip
        y = y * jax.nn.silu(z)
        x = residual + y @ w_out
        N = B * T
        x_flat = x.reshape(N, D_MODEL)
        h_flat = _rms(x_flat, g_moe)
        scores = h_flat @ w_router
        topk_vals, topk_idx = jax.lax.top_k(scores, TOP_K)
        weights = jax.nn.softmax(topk_vals, axis=-1)
        w_dense = jnp.sum(jax.nn.one_hot(topk_idx, N_EXP, dtype=x.dtype) * weights[..., None], axis=1)
        rms_x = x_flat * jax.lax.rsqrt(jnp.mean(x_flat * x_flat, axis=-1, keepdims=True) + EPS)
        he = rms_x[:, None, :] * g_exp
        a = jnp.einsum('ned,edf->nef', he, w1)
        b = jnp.einsum('ned,edf->nef', he, w3)
        ffn = jnp.einsum('nef,efd->ned', jax.nn.silu(a) * b, w2)
        tok_out = x_flat[:, None, :] + ffn
        out = jnp.einsum('ne,ned->nd', w_dense, tok_out)
        return out.reshape(B, T, D_MODEL)

    def _L3_ffn_ref(hidden_states, Wg, e_bias, W_gate_up, W_down, Wsg, Wsu, Wsd):
        import jax, jax.numpy as jnp
        import numpy as np
        E = 128
        I = 464
        IS = 928
        K = 6
        G = 1
        TG = 1
        SCALE = 2.5
        CAP = 192

        def moe_forward(hidden_states, Wg, e_bias, W_gate_up, W_down, Wsg, Wsu, Wsd):
            B, S, H = hidden_states.shape
            x = hidden_states.reshape(-1, H)
            T = x.shape[0]
            logits = x.astype(jnp.float32) @ Wg.T
            sig = jax.nn.sigmoid(logits)
            choice = sig + e_bias[None, :]
            grp = choice.reshape(T, G, E // G)
            group_scores = jax.lax.top_k(grp, 2)[0].sum(-1)
            gidx = jax.lax.top_k(group_scores, TG)[1]
            gmask = jnp.zeros((T, G), jnp.float32).at[jnp.arange(T)[:, None], gidx].set(1.0)
            smask = jnp.repeat(gmask, E // G, axis=1)
            scores_for_choice = jnp.where(smask > 0, choice, 0.0)
            topk_idx = jax.lax.top_k(scores_for_choice, K)[1]
            topk_w = jnp.take_along_axis(sig, topk_idx, axis=1)
            topk_w = topk_w / (topk_w.sum(-1, keepdims=True) + 1e-20)
            topk_w = topk_w * SCALE
            P = T * K
            flat_e = topk_idx.reshape(-1)
            order = jnp.argsort(flat_e)
            se = flat_e[order]
            counts = jax.ops.segment_sum(jnp.ones(P, jnp.int32), flat_e, num_segments=E)
            starts = jnp.cumsum(counts) - counts
            pos = jnp.arange(P) - starts[se]
            buf_idx = jnp.where(pos < CAP, se * CAP + pos, E * CAP)
            tok_of_pair = (order // K).astype(jnp.int32)
            w_of_pair = topk_w.reshape(-1)[order]
            token_buf = jnp.zeros((E * CAP,), jnp.int32).at[buf_idx].set(tok_of_pair, mode='drop')
            w_buf = jnp.zeros((E * CAP,), x.dtype).at[buf_idx].set(w_of_pair.astype(x.dtype), mode='drop')
            xb = x[token_buf].reshape(E, CAP, H)
            gu = jnp.einsum('ech,ehf->ecf', xb, W_gate_up)
            g, u = jnp.split(gu, 2, axis=-1)
            inter = jax.nn.silu(g) * u
            yb = jnp.einsum('eci,eih->ech', inter, W_down)
            yb = yb * w_buf.reshape(E, CAP, 1)
            routed = jnp.zeros((T, H), x.dtype).at[token_buf].add(yb.reshape(E * CAP, H))
            shared = jax.nn.silu(x @ Wsg) * (x @ Wsu) @ Wsd
            return (routed + shared).reshape(B, S, H)
        return moe_forward(hidden_states, Wg, e_bias, W_gate_up, W_down, Wsg, Wsu, Wsd)
    h = _L0_tok_ref(x, L0_tok_W, L0_tok_b)
    h = h + _L0_attn_ref(_layernorm(h, axis=-1), L0_attn_Wq, L0_attn_Wk, L0_attn_Wv, L0_attn_Wf, L0_attn_bf, L0_attn_Wo, L0_attn_gamma, L0_attn_beta)
    h = h + _L0_ffn_ref(_layernorm(h, axis=-1), L0_ffn_g1, L0_ffn_b1, L0_ffn_g2, L0_ffn_b2, L0_ffn_Wr, L0_ffn_br, L0_ffn_Wq, L0_ffn_bq, L0_ffn_Wk, L0_ffn_bk, L0_ffn_Wv, L0_ffn_bv, L0_ffn_Wo, L0_ffn_bo, L0_ffn_Wm, L0_ffn_bm, L0_ffn_W1, L0_ffn_bf1, L0_ffn_W2, L0_ffn_bf2)
    h = h + _L1_attn_ref(_layernorm(h, axis=-1), L1_attn_log_lambda, L1_attn_Wd, L1_attn_bd, L1_attn_WB, L1_attn_WC, L1_attn_Wout, L1_attn_bout)
    h = h + _L1_ffn_ref(_layernorm(h, axis=-1), L1_ffn_Wg, L1_ffn_W1, L1_ffn_b1, L1_ffn_W2, L1_ffn_b2)
    h = h + _L2_attn_ref(_layernorm(h, axis=-1), L2_attn_W_qkv, L2_attn_b_qkv)
    h = h + _L2_ffn_ref(_layernorm(h, axis=-1), L2_ffn_w1, L2_ffn_b1, L2_ffn_w2, L2_ffn_b2, L2_ffn_router_w, L2_ffn_router_b, L2_ffn_w_down, L2_ffn_w_up)
    h = h + _L3_attn_ref(_layernorm(h, axis=-1), L3_attn_g_mamba, L3_attn_w_in, L3_attn_conv_w, L3_attn_conv_b, L3_attn_w_xproj, L3_attn_w_dt, L3_attn_b_dt, L3_attn_A_log, L3_attn_D_skip, L3_attn_w_out, L3_attn_g_moe, L3_attn_w_router, L3_attn_g_exp, L3_attn_w1, L3_attn_w3, L3_attn_w2)
    h = h + _L3_ffn_ref(_layernorm(h, axis=-1), L3_ffn_Wg, L3_ffn_e_bias, L3_ffn_W_gate_up, L3_ffn_W_down, L3_ffn_Wsg, L3_ffn_Wsu, L3_ffn_Wsd)
    return h

_drawn_inputs = setup_inputs


def setup_inputs(seed=0):
    import zlib

    import numpy as np

    out = dict(_drawn_inputs(seed))
    spreads = {'L0_attn_bf': (0.0, 0.612),
     'L0_attn_gamma': (1.0, 0.2),
     'L0_attn_beta': (0.0, 0.1),
     'L0_ffn_g1': (1.0, 0.2),
     'L0_ffn_b1': (0.0, 0.463),
     'L0_ffn_g2': (1.0, 0.6),
     'L0_ffn_b2': (0.0, 0.8),
     'L0_ffn_bq': (0.0, 0.8),
     'L0_ffn_bk': (0.0, 0.8),
     'L0_ffn_bv': (0.0, 0.8),
     'L0_ffn_bo': (0.0, 0.58),
     'L0_ffn_bm': (0.0, 0.1),
     'L0_ffn_bf1': (0.0, 0.599),
     'L0_ffn_bf2': (0.0, 0.1),
     'L1_ffn_b1': (0.0, 0.8),
     'L1_ffn_b2': (0.0, 0.431),
     'L3_attn_g_mamba': (1.0, 0.6),
     'L3_attn_conv_b': (0.0, 0.8),
     'L3_attn_b_dt': (-6.907755374908447, 0.6),
     'L3_attn_D_skip': (1.0, 0.6),
     'L3_attn_g_moe': (1.0, 0.6),
     'L3_attn_g_exp': (1.0, 0.6),
     'L3_ffn_e_bias': (0.0, 0.8)}
    factors = {'L0_tok_b': 3.995,
     'L0_ffn_Wq': 8.0,
     'L0_ffn_Wk': 8.0,
     'L0_ffn_Wv': 8.0,
     'L0_ffn_Wo': 8.0,
     'L1_attn_log_lambda': 8.0,
     'L1_attn_Wd': 8.0,
     'L1_attn_bd': 8.0,
     'L1_attn_bout': 6.316,
     'L1_ffn_W1': 4.468,
     'L1_ffn_W2': 3.92,
     'L2_ffn_b1': 8.0,
     'L2_ffn_b2': 8.0,
     'L2_ffn_router_w': 8.0,
     'L2_ffn_router_b': 8.0,
     'L2_ffn_w_down': 7.08,
     'L2_ffn_w_up': 6.248,
     'L3_attn_w_in': 8.0,
     'L3_attn_conv_w': 8.0,
     'L3_attn_w_xproj': 8.0,
     'L3_attn_w_dt': 8.0,
     'L3_attn_A_log': 8.0,
     'L3_attn_w_out': 8.0,
     'L3_attn_w_router': 8.0,
     'L3_attn_w1': 8.0,
     'L3_attn_w3': 8.0,
     'L3_attn_w2': 8.0,
     'L3_ffn_Wg': 8.0,
     'L3_ffn_W_gate_up': 8.0,
     'L3_ffn_W_down': 8.0,
     'L3_ffn_Wsg': 8.0,
     'L3_ffn_Wsu': 8.0,
     'L3_ffn_Wsd': 8.0}
    for name, (base, spread) in spreads.items():
        noise = np.random.default_rng([zlib.crc32(name.encode()), seed]).standard_normal(out[name].shape)
        drawn = base * np.exp(spread * noise) if base else spread * noise
        out[name] = jnp.asarray(drawn.astype(out[name].dtype))
    for name, factor in factors.items():
        out[name] = (out[name] * factor).astype(out[name].dtype)
    return out
```

```python
from contextlib import ExitStack

import numpy as np

import concourse.bass as bass
from concourse import mybir

F32 = mybir.dt.float32
BF16 = mybir.dt.bfloat16
I32 = mybir.dt.int32
U32 = mybir.dt.uint32
ALU = mybir.AluOpType
ACT = mybir.ActivationFunctionType
AXX = mybir.AxisListType.X
SILU, SIGMOID, GELU = "silu_and_others", "sigmoid_and_others", "gelu_and_others"
LOG_EXP = "natural_log_exp_and_others"

B, L, D = 64, 36, 192
T = B * L
P = 96
GB = 8
N = GB * L
GROUPS = T // N
WIDE = 384
PAIR = 2 * L
ROWS = 128
RT = T // ROWS
HEADS, DH = 12, 16
HID = 768
PD = 768
STATES = 16
DI = 384
TILE = 192
HALF = TILE // 2

E1, K1, STRIDE1 = 8, 2, T
E2, K2, STRIDE2 = 128, 6, 192
F2 = 464
SHARED = 928


def signals(nc, block, *names):
    return [nc.alloc_semaphore(f"{block}_{n}") for n in names]


def finish(nc, sems):
    nc.clear_and_free_semaphores(sems)
    nc.all_engine_barrier()


def own_wait(engine, turn):
    engine.sem_inc(turn, 1)


def span(g, n):
    return bass.ds(g * n, n)


class Memory:

    WEIGHTS = 4800

    def __init__(self, nc, ctx):
        self.nc, self.ctx = nc, ctx
        sb = lambda name, shape, dt=F32: ctx.enter_context(nc.sbuf_tensor(name, shape, dt))
        self.sb = sb
        self.h = sb("residual", [P, 2, T])
        self.full = sb("full", [128, 11, T])
        self.half = [sb(f"weights{n}", [128, self.WEIGHTS]) for n in range(2)]
        self.scratch = sb("scratch", [128, self.SCRATCH])
        self.psum = ctx.enter_context(nc.psum_tensor("psum", [128, 8, 512], F32))
        self.ones = sb("ones", [128, 128])
        self.mean = sb("mean_weights", [P, P])
        self.eps = sb("eps", [128, 2])
        self.identity = sb("identity", [128, 128])
        self.coef = sb("coef", [96, T], BF16)
        self.rates = sb("rates", [128, 3 * STATES])
        self.arrived = [nc.alloc_semaphore(f"weights_loaded{n}") for n in range(2)]
        self.setup = nc.alloc_semaphore("constants_set")
        self.zeros = sb("zeros", [128, self.FILL // 2])
        self.fills = []
        self.filled = nc.alloc_semaphore("tables_zeroed")

    FILL = 2304
    SCRATCH = 10496

    def zeroing(self, rows, words):
        if words == 1:
            n = rows.shape[0] // 128
            self.fills.append((rows.rearrange("(p n) a -> p (n a)", p=128), self.zeros[:, 0:n].bitcast(U32)))
        else:
            parts = rows.rearrange("(n p b a) d -> n p b (a d)", p=128, b=2, a=self.FILL // words // 2)
            zeros = self.zeros[:].rearrange("p (b f) -> p b f", b=1).broadcast_to([128, 2, self.FILL // 2])
            self.fills += [(parts[n], zeros) for n in range(rows.shape[0] * words // (128 * self.FILL))]

    def act(self, first, n=2, parts=P):
        return self.full[0:parts, first:first + n, :]


def carve(base, specs):
    at, tiles = 0, {}
    for name, (parts, shape, dt) in specs.items():
        count = int(np.prod(shape))
        words = count if dt in (F32, I32, U32) else (count + 1) // 2
        flat = base[0:parts, at:at + words]
        if dt is not F32:
            flat = flat.bitcast(dt)
        names = " ".join(f"a{k}" for k in range(len(shape)))
        sizes = {f"a{k}": s for k, s in enumerate(shape)}
        tiles[name] = flat.rearrange(f"p ({names}) -> p {names}", **sizes) if len(shape) > 1 else flat
        at += words + (-words) % 8
    assert at <= base.shape[1], (at, base.shape)
    return tiles



class Routing:

    def __init__(self, m, experts, picks, stride, capacity, steps, sigmoid, factor):
        self.experts, self.picks, self.stride, self.capacity = experts, picks, stride, capacity
        self.steps, self.sigmoid, self.factor = steps, sigmoid, factor
        self.bias, self.scaled = sigmoid, not sigmoid
        self.slots = experts * stride + m.FILL * 128 // D
        data = m.full[:, 10, :]
        self.weight = data[:, 0:RT * picks].rearrange("p (t k) -> p t k", k=picks)
        self.slot = data[:, 128:128 + RT * picks].bitcast(U32).rearrange("p (t k) -> p t k", k=picks)
        self.scatter = data[:, 640:640 + RT * picks].bitcast(U32).rearrange("p (t k) -> p t k", k=picks)
        self.ids = data[:, 768:768 + RT].bitcast(U32).rearrange("p (t a) -> p t a", a=1)
        self.table = data[0:1, 256:256 + 2 * steps + 1].bitcast(I32)


def start_block(nc, m, load):
    with nc.Block() as block:
        @block.vector
        def _(dve):
            nc.vector.memset(m.ones[:], 1.0)
            nc.vector.memset(m.mean[:], 1.0 / D)
            nc.vector.memset(m.eps[:, 0:1], 1e-5)
            nc.vector.memset(m.eps[:, 1:2], 1e-6)
            nc.vector.memset(m.psum[:], 0.0)
            nc.vector.memset(m.zeros[:], 0.0)

        @block.sync
        def _(sp):
            load(sp)


def norm_block(nc, m, name, load, src, dst, eps, centre=True, gamma=None, beta=None):
    n, steps = WIDE, T // WIDE
    s = carve(m.scratch[:], {f"{k}{j}": v for j in range(2) for k, v in (
        ("centred", (P, (2, n), F32)), ("square", (P, (2, n), F32)), ("rstd", (P, (n,), F32)))})
    mean = [m.psum[0:P, j, 0:n] for j in range(2)]
    var = [m.psum[0:P, 2 + j, 0:n] for j in range(2)]
    sems = signals(nc, name, "mean", "centred", "squared", "var", "log", "rstd", "scaled", "shifted")
    s_mean, s_centred, s_squared, s_var, s_log, s_rstd, s_scaled, s_shifted = sems
    e = m.eps[0:P, 0:1] if eps == 1e-5 else m.eps[0:P, 1:2]
    with nc.Block() as block:
        @block.sync
        def _(sp):
            load(sp)

        @block.tensor
        def _(pe):
            with pe.Fori(0, steps // 2) as i:
                if centre:
                    for j in range(2):
                        g = 2 * i + j
                        for c in range(2):
                            last = nc.tensor.matmul(mean[j], m.mean[:], src[:, c, span(g, n)],
                                                    start=c == 0, stop=c == 1)
                        last.then_inc(s_mean, 1)
                for j in range(2):
                    pe.wait_ge(s_squared, 2 * i + j + 1)
                    for c in range(2):
                        last = nc.tensor.matmul(var[j], m.mean[:], s[f"square{j}"][:, c, :],
                                                start=c == 0, stop=c == 1)
                    last.then_inc(s_var, 1)

        @block.scalar
        def _(act):
            nc.scalar.preload_act_table_set(LOG_EXP)
            if gamma is not None:
                act.wait_ge(m.loaded, m.due)
            with act.Fori(0, steps // 2) as i:
                for j in range(2):
                    g = 2 * i + j
                    if centre:
                        act.wait_ge(s_centred, g + 1)
                        x = s[f"centred{j}"]
                    else:
                        x = src[:, :, span(g, n)]
                    nc.scalar.activation(s[f"square{j}"], x, ACT.Square).then_inc(s_squared, 1)
                for j in range(2):
                    g = 2 * i + j
                    act.wait_ge(s_var, g + 1)
                    act.wait_ge(s_scaled, g + 1)
                    nc.scalar.activation(s[f"rstd{j}"], var[j], ACT.Ln, bias=e).then_inc(s_log, 1)
                    act.wait_ge(s_log, g + 1)
                    nc.scalar.activation(s[f"rstd{j}"], s[f"rstd{j}"], ACT.Exp, scale=-0.5).then_inc(s_rstd, 1)
                if beta is not None:
                    for j in range(2):
                        g = 2 * i + j
                        act.wait_ge(s_scaled, g + 3)
                        for c in range(2):
                            nc.scalar.activation(dst[:, c, span(g, n)], dst[:, c, span(g, n)], ACT.Identity,
                                                 bias=beta[:, c:c + 1]).then_inc(s_shifted, 1)

        @block.vector
        def _(dve):
            if gamma is not None:
                dve.wait_ge(m.loaded, m.due)
            dve.sem_inc(s_scaled, 2)
            with dve.Fori(0, steps // 2) as i:
                if centre:
                    for j in range(2):
                        g = 2 * i + j
                        dve.wait_ge(s_mean, g + 1)
                        dve.wait_ge(s_scaled, g + 1)
                        nc.vector.tensor_tensor(s[f"centred{j}"], src[:, :, span(g, n)],
                                                m.psum[0:P, j:j + 1, 0:n].broadcast_to([P, 2, n]),
                                                ALU.subtract).then_inc(s_centred, 1)
                for j in range(2):
                    g = 2 * i + j
                    dve.wait_ge(s_rstd, g + 1)
                    if centre:
                        dve.wait_ge(s_centred, g + 1)
                    for c in range(2):
                        x = s[f"centred{j}"][:, c, :] if centre else src[:, c, span(g, n)]
                        if gamma is None:
                            last = nc.vector.tensor_tensor(dst[:, c, span(g, n)], x, s[f"rstd{j}"], ALU.mult)
                        else:
                            last = nc.vector.scalar_tensor_tensor(
                                out=dst[:, c, span(g, n)], in0=x, scalar=gamma[:, c:c + 1],
                                in1=s[f"rstd{j}"], op0=ALU.mult, op1=ALU.mult)
                    last.then_inc(s_scaled, 1)
    finish(nc, sems)


def patch_block(nc, m, w, load, patches):
    s = carve(m.scratch[:], {f"patch{j}": (128, (PD // 128, N), F32) for j in range(2)})
    sems = signals(nc, "patch", "loaded0", "loaded1", "product", "evacuated")
    s_in, (s_prod, s_out) = sems[:2], sems[2:]
    with nc.Block() as block:
        @block.sync
        def _(sp):
            load(sp)
            with sp.Fori(0, GROUPS // 2) as i:
                for j in range(2):
                    g = 2 * i + j
                    sp.wait_ge(s_prod, 2 * g + 2)
                    sp.dma_start(s[f"patch{j}"], patches[g]).then_inc(s_in[j], 16)

        @block.tensor
        def _(pe):
            pe.sem_inc(s_prod, 4)
            pe.wait_ge(m.loaded, m.due)
            with pe.Fori(0, GROUPS // 2) as i:
                for j in range(2):
                    g = 2 * i + j
                    pe.wait_ge(s_in[j], 16 * i + 16)
                    pe.wait_ge(s_out, g + 1)
                    for c in range(2):
                        for k in range(PD // 128):
                            last = nc.tensor.matmul(m.psum[0:P, 2 * j + c, 0:N], w["W"][:, k, c * P:c * P + P],
                                                    s[f"patch{j}"][:, k, :], start=k == 0, stop=k == PD // 128 - 1)
                        last.then_inc(s_prod, 1)

        @block.vector
        def _(dve):
            dve.sem_inc(s_out, 2)
            dve.wait_ge(m.loaded, m.due)
            with dve.Fori(0, GROUPS // 2) as i:
                for j in range(2):
                    g = 2 * i + j
                    for c in range(2):
                        dve.wait_ge(s_prod, 2 * g + c + 5)
                        last = nc.vector.scalar_tensor_tensor(
                            out=m.h[:, c, span(g, N)].rearrange("p (b l) -> p b l", l=L),
                            in0=m.psum[0:P, 2 * j + c, 0:N].rearrange("p (b l) -> p b l", l=L),
                            scalar=w["b"][:, c:c + 1], in1=w["pos"][:, c:c + 1, :].broadcast_to([P, GB, L]),
                            op0=ALU.add, op1=ALU.add)
                    last.then_inc(s_out, 1)
    finish(nc, sems)


def mlp_block(nc, m, name, load, x, w1, b1, w2, evacuate, func, extra=None, n=WIDE,
              scale=None):
    chunks = HID // 128
    s = carve(m.scratch[:], {f"hidden{j}": (128, (chunks, n), F32) for j in range(2)}
              | {f"scaled{j}": (P, (2, n), F32) for j in range(2)})
    sems = signals(nc, name, "up", "hidden", "down", "evacuated", "scaled")
    s_up, s_hidden, s_down, s_out, s_scaled = sems
    up = lambda k: m.psum[:, k % 4, 0:n]
    with nc.Block() as block:
        @block.sync
        def _(sp):
            load(sp)

        @block.tensor
        def _(pe):
            pe.sem_inc(s_down, 4)
            pe.wait_ge(m.loaded, m.due)
            with pe.Fori(0, T // n // 2) as i:
                for j in range(2):
                    g = 2 * i + j
                    for k in range(chunks):
                        pe.wait_ge(s_hidden, chunks * g + k + 1)
                        for c in range(2):
                            last = nc.tensor.matmul(up(j * chunks + k), w1[:, c, k * 128:k * 128 + 128],
                                                    x[:, c, span(g, n)], start=c == 0, stop=c == 1)
                        last.then_inc(s_up, 1)
                for j in range(2):
                    g = 2 * i + j
                    pe.wait_ge(s_hidden, chunks * g + chunks + 4)
                    pe.wait_ge(s_out, 2 * g + 2)
                    for c in range(2):
                        out = m.psum[0:P, 4 + 2 * j + c, 0:n]
                        for k in range(chunks):
                            last = nc.tensor.matmul(out, w2[:, k, c * P:c * P + P], s[f"hidden{j}"][:, k, :],
                                                    start=k == 0, stop=k == chunks - 1 and extra is None)
                        if extra is not None:
                            last = nc.tensor.matmul(out, extra[0][:, c * P:c * P + P],
                                                    extra[1][:, span(g, n)], start=False, stop=True)
                        last.then_inc(s_down, 1)

        @block.scalar
        def _(act):
            nc.scalar.preload_act_table_set(GELU)
            act.sem_inc(s_hidden, 4)
            act.wait_ge(m.loaded, m.due)
            with act.Fori(0, T // n // 2) as i:
                for j in range(2):
                    g = 2 * i + j
                    act.wait_ge(s_down, 2 * g + 2)
                    for k in range(chunks):
                        act.wait_ge(s_up, chunks * g + k + 1)
                        nc.scalar.activation(s[f"hidden{j}"][:, k, :], up(j * chunks + k), func,
                                             bias=b1[:, k:k + 1]).then_inc(s_hidden, 1)

        @block.vector
        def _(dve):
            dve.sem_inc(s_out, 4)
            dve.wait_ge(m.loaded, m.due)
            with dve.Fori(0, T // n // 2) as i:
                for j in range(2):
                    g = 2 * i + j
                    for c in range(2):
                        dve.wait_ge(s_down, 2 * g + c + 5)
                        product = m.psum[0:P, 4 + 2 * j + c, 0:n]
                        if scale is not None:
                            dve.wait_ge(s_out, 2 * g + 2)
                            bias, factor = scale
                            factor = factor[:, span(g, n // L)].rearrange("p (b a) -> p b a", a=1)
                            nc.vector.scalar_tensor_tensor(
                                out=s[f"scaled{j}"][:, c, :].rearrange("p (b l) -> p b l", l=L),
                                in0=product.rearrange("p (b l) -> p b l", l=L), scalar=bias[:, c:c + 1],
                                in1=factor.broadcast_to([P, n // L, L]), op0=ALU.add, op1=ALU.mult
                            ).then_inc(s_scaled, 1)
                            dve.wait_ge(s_scaled, 2 * g + c + 1)
                            product = s[f"scaled{j}"][:, c, :]
                        evacuate(dve, c, g, product).then_inc(s_out, 1)
    finish(nc, sems)


def gated_block(nc, m, name, load, x, wg, wu, wd, chunk, chunks, side):
    n = WIDE
    s = carve(m.scratch[:], {f"hidden{j}": (chunk, (chunks, n), F32) for j in range(2)}
              | {f"silu{j}": (chunk, (n,), F32) for j in range(2)})
    sems = signals(nc, name, "up", "silu", "hidden", "down", "evacuated")
    s_up, s_silu, s_hidden, s_down, s_out = sems
    up = lambda k, q: m.psum[0:chunk, 2 * (k % 2) + q, 0:n]
    with nc.Block() as block:
        @block.sync
        def _(sp):
            load(sp)
            side.sync(sp)

        @block.gpsimd
        def _(pool):
            side.gpsimd(pool)

        @block.tensor
        def _(pe):
            pe.sem_inc(s_down, 4)
            pe.wait_ge(m.loaded, m.due)
            with pe.Fori(0, T // n // 2) as i:
                for j in range(2):
                    g = 2 * i + j
                    for k in range(chunks):
                        pe.wait_ge(s_hidden, chunks * g + k + 1)
                        for q, w in enumerate((wg, wu)):
                            for c in range(2):
                                last = nc.tensor.matmul(up(j * chunks + k, q), w[:, c, k * chunk:k * chunk + chunk],
                                                        x[:, c, span(g, n)], start=c == 0, stop=c == 1)
                        last.then_inc(s_up, 1)
                for j in range(2):
                    g = 2 * i + j
                    pe.wait_ge(s_hidden, chunks * g + chunks + 2)
                    pe.wait_ge(s_out, 2 * g + 2)
                    for c in range(2):
                        for k in range(chunks):
                            last = nc.tensor.matmul(m.psum[0:P, 4 + 2 * j + c, 0:n], wd[:, k, c * P:c * P + P],
                                                    s[f"hidden{j}"][:, k, :], start=k == 0, stop=k == chunks - 1)
                        last.then_inc(s_down, 1)

        @block.scalar
        def _(act):
            nc.scalar.preload_act_table_set(SILU)
            with act.Fori(0, T // n // 2) as i:
                for j in range(2):
                    g = 2 * i + j
                    for k in range(chunks):
                        act.wait_ge(s_up, chunks * g + k + 1)
                        act.wait_ge(s_hidden, chunks * g + k + 1)
                        nc.scalar.activation(s[f"silu{(j * chunks + k) % 2}"], up(j * chunks + k, 0),
                                             ACT.Silu).then_inc(s_silu, 1)

        @block.vector
        def _(dve):
            dve.sem_inc(s_out, 4)
            dve.sem_inc(s_hidden, 2)
            with dve.Fori(0, T // n // 2) as i:
                for j in range(2):
                    g = 2 * i + j
                    dve.wait_ge(s_down, 2 * g + 2)
                    for k in range(chunks):
                        dve.wait_ge(s_silu, chunks * g + k + 1)
                        nc.vector.tensor_tensor(s[f"hidden{j}"][:, k, :], s[f"silu{(j * chunks + k) % 2}"],
                                                up(j * chunks + k, 1), ALU.mult).then_inc(s_hidden, 1)
                for j in range(2):
                    g = 2 * i + j
                    for c in range(2):
                        dve.wait_ge(s_down, 2 * g + c + 5)
                        h = m.h[:, c, span(g, n)]
                        nc.vector.tensor_tensor(h, m.psum[0:P, 4 + 2 * j + c, 0:n], h, ALU.add).then_inc(s_out, 1)
                    side.vector(dve, i, j)
    finish(nc, sems + side.sems)


def project_block(nc, m, name, load, x, w, dst):
    n = WIDE
    sems = signals(nc, name, "product", "evacuated")
    s_prod, s_out = sems
    with nc.Block() as block:
        @block.sync
        def _(sp):
            load(sp)

        @block.tensor
        def _(pe):
            pe.wait_ge(m.loaded, m.due)
            with pe.Fori(0, T // n // 2) as i:
                for j in range(2):
                    g = 2 * i + j
                    pe.wait_ge(s_out, 2 * g + 2)
                    for c in range(2):
                        for k in range(2):
                            last = nc.tensor.matmul(m.psum[0:P, 2 * j + c, 0:n], w[:, k, c * P:c * P + P],
                                                    x[:, k, span(g, n)], start=k == 0, stop=k == 1)
                        last.then_inc(s_prod, 1)

        @block.vector
        def _(dve):
            dve.sem_inc(s_out, 4)
            with dve.Fori(0, T // n // 2) as i:
                for j in range(2):
                    g = 2 * i + j
                    for c in range(2):
                        dve.wait_ge(s_prod, 2 * g + c + 1)
                        d = dst[:, c, span(g, n)]
                        nc.vector.tensor_tensor(d, m.psum[0:P, 2 * j + c, 0:n], d, ALU.add).then_inc(s_out, 1)
    finish(nc, sems)


def decay_attention_block(nc, m, w, load, x, dst):
    F = (N,)
    s = carve(m.scratch[:], {f"{k}{j}": v for j in range(2) for k, v in (
        ("x", (P, (2, N), F32)), ("forget", (128, F, F32)), ("cum", (128, F, F32)),
        ("neg", (128, F, F32)), ("elu", (128, F, F32)), ("q", (64, F, F32)), ("k", (64, F, F32)),
        ("v", (PAIR, (4, D), F32)), ("score", (PAIR, (4, PAIR), F32)), ("den", (P, F, F32)))}
        | {"negb": (128, (1,), F32)})
    ps = lambda j, q: m.psum[:, 4 * j + q, :]
    names = ("copied", "products", "values", "v_copied", "e", "u", "log", "scan", "clip", "decay", "min", "exp",
             "elu", "qk", "scores", "masked", "sums", "den", "recip", "out", "negb")
    sems = signals(nc, "decay", *names)
    S = dict(zip(names, sems))
    r4 = lambda a, k: a.rearrange("p (a b) -> p a b", a=k)
    with nc.Block() as block:
        @block.sync
        def _(sp):
            load(sp)

        @block.gpsimd
        def _(pool):
            with pool.Fori(0, GROUPS // 2) as i:
                for j in range(2):
                    g = 2 * i + j
                    pool.wait_ge(S["values"], g + 1)
                    nc.gpsimd.tensor_copy(s[f"x{j}"], x[:, :, span(g, N)]).then_inc(S["copied"], 1)

        @block.tensor
        def _(pe):
            pe.sem_inc(S["values"], 2)
            pe.wait_ge(m.loaded, m.due)
            with pe.Fori(0, GROUPS // 2) as i:
                for j in range(2):
                    g = 2 * i + j
                    pe.wait_ge(S["out"], g + 1)
                    for q, wt in enumerate((w["Wqk"], w["Wff"])):
                        for c in range(2):
                            last = nc.tensor.matmul(ps(j, q)[:, 0:N], wt[:, c, :], x[:, c, span(g, N)],
                                                    start=c == 0, stop=c == 1)
                    last.then_inc(S["products"], 1)
                    pe.wait_ge(S["copied"], g + 1)
                    for p in range(4):
                        for c in range(2):
                            last = nc.tensor.matmul(ps(j, 2 + p // 2)[0:PAIR, (p % 2) * D:(p % 2) * D + D],
                                                    s[f"x{j}"][:, c, p * PAIR:p * PAIR + PAIR], w["Wv"][:, c, :],
                                                    start=c == 0, stop=c == 1)
                    last.then_inc(S["values"], 1)
                for j in range(2):
                    g = 2 * i + j
                    pe.wait_ge(S["qk"], g + 1)
                    for p in range(4):
                        last = nc.tensor.matmul(ps(j, 0)[0:PAIR, p * PAIR:p * PAIR + PAIR],
                                                s[f"k{j}"][:, p * PAIR:p * PAIR + PAIR],
                                                s[f"q{j}"][:, p * PAIR:p * PAIR + PAIR], start=True, stop=True)
                    last.then_inc(S["scores"], 1)
                for j in range(2):
                    g = 2 * i + j
                    pe.wait_ge(S["masked"], g + 1)
                    pe.wait_ge(S["v_copied"], g + 1)
                    nc.tensor.matmul(ps(j, 3)[0:P, 0:N], m.ones[0:PAIR, 0:P],
                                     s[f"score{j}"].rearrange("p a b -> p (a b)"), start=True, stop=True)
                    for c in range(2):
                        for p in range(4):
                            last = nc.tensor.matmul(ps(j, 1 + c)[0:P, p * PAIR:p * PAIR + PAIR],
                                                    s[f"v{j}"][:, p, c * P:c * P + P], s[f"score{j}"][:, p, :],
                                                    start=True, stop=True)
                    last.then_inc(S["sums"], 1)

        @block.scalar
        def _(act):
            nc.scalar.preload_act_table_set(LOG_EXP)
            act.wait_ge(S["negb"], 1)
            with act.Fori(0, GROUPS // 2) as i:
                for j in range(2):
                    g = 2 * i + j
                    act.wait_ge(S["products"], g + 1)
                    nc.scalar.activation(s[f"forget{j}"], ps(j, 1)[:, 0:N], ACT.Exp, bias=s["negb"],
                                         scale=-1.0).then_inc(S["e"], 1)
                    act.wait_ge(S["min"], g + 1)
                    nc.scalar.activation(s[f"neg{j}"], s[f"neg{j}"], ACT.Exp).then_inc(S["exp"], 1)
                    act.wait_ge(S["values"], g + 3)
                    for q in range(2):
                        last = nc.scalar.activation(s[f"v{j}"][:, 2 * q:2 * q + 2, :],
                                                    r4(ps(j, 2 + q)[0:PAIR, 0:2 * D], 2), ACT.Copy)
                    last.then_inc(S["v_copied"], 1)
                for j in range(2):
                    g = 2 * i + j
                    act.wait_ge(S["u"], g + 1)
                    nc.scalar.activation(s[f"forget{j}"], s[f"forget{j}"], ACT.Ln).then_inc(S["log"], 1)
                for j in range(2):
                    g = 2 * i + j
                    act.wait_ge(S["clip"], g + 1)
                    nc.scalar.activation(s[f"cum{j}"], s[f"cum{j}"], ACT.Exp,
                                         scale=w["sign"]).then_inc(S["decay"], 1)

        @block.vector
        def _(dve):
            dve.sem_inc(S["out"], 2)
            dve.wait_ge(m.loaded, m.due)
            nc.vector.tensor_scalar(s["negb"], w["bf"], -1.0, None, ALU.mult).then_inc(S["negb"], 1)
            with dve.Fori(0, GROUPS // 2) as i:
                for j in range(2):
                    g = 2 * i + j
                    dve.wait_ge(S["products"], g + 1)
                    nc.vector.tensor_scalar(s[f"neg{j}"], ps(j, 0)[:, 0:N], 0.0, None,
                                            ALU.min).then_inc(S["min"], 1)
                    dve.wait_ge(S["e"], g + 1)
                    nc.vector.tensor_scalar(s[f"forget{j}"], s[f"forget{j}"], 1.0, 1e6, ALU.add,
                                            ALU.min).then_inc(S["u"], 1)
                    dve.wait_ge(S["exp"], g + 1)
                    nc.vector.scalar_tensor_tensor(out=s[f"elu{j}"], in0=ps(j, 0)[:, 0:N], scalar=0.0,
                                                   in1=s[f"neg{j}"], op0=ALU.max, op1=ALU.add).then_inc(S["elu"], 1)
                for j in range(2):
                    g = 2 * i + j
                    dve.wait_ge(S["log"], g + 1)
                    nc.vector.tensor_tensor_scan(s[f"cum{j}"], w["carry"], s[f"forget{j}"], 0.0, ALU.mult,
                                                 ALU.add).then_inc(S["scan"], 1)
                    dve.wait_ge(S["scan"], g + 1)
                    nc.vector.tensor_scalar(s[f"cum{j}"], s[f"cum{j}"], 20.0, -20.0, ALU.min,
                                            ALU.max).then_inc(S["clip"], 1)
                for j in range(2):
                    g = 2 * i + j
                    dve.wait_ge(S["decay"], g + 1)
                    dve.wait_ge(S["elu"], g + 1)
                    nc.vector.scalar_tensor_tensor(out=s[f"q{j}"], in0=s[f"elu{j}"][0:64, :], scalar=64 ** -0.5,
                                                   in1=s[f"cum{j}"][0:64, :], op0=ALU.mult, op1=ALU.mult)
                    nc.vector.tensor_tensor(s[f"k{j}"], s[f"elu{j}"][64:128, :], s[f"cum{j}"][64:128, :],
                                            ALU.mult).then_inc(S["qk"], 1)
                for j in range(2):
                    g = 2 * i + j
                    dve.wait_ge(S["scores"], g + 1)
                    nc.vector.tensor_tensor(s[f"score{j}"], r4(ps(j, 0)[0:PAIR, 0:N], 4),
                                            w["causal"].rearrange("p (a b) -> p a b", a=1)
                                            .broadcast_to([PAIR, 4, PAIR]), ALU.mult).then_inc(S["masked"], 1)
                for j in range(2):
                    g = 2 * i + j
                    dve.wait_ge(S["sums"], g + 1)
                    nc.vector.tensor_scalar(s[f"den{j}"], ps(j, 3)[0:P, 0:N], 1e-6, None,
                                            ALU.add).then_inc(S["den"], 1)
                    dve.wait_ge(S["den"], g + 1)
                    nc.vector.reciprocal(s[f"den{j}"], s[f"den{j}"]).then_inc(S["recip"], 1)
                    dve.wait_ge(S["recip"], g + 1)
                    for c in range(2):
                        last = nc.vector.tensor_tensor(dst[:, c, span(g, N)], ps(j, 1 + c)[0:P, 0:N],
                                                       s[f"den{j}"], ALU.mult)
                    last.then_inc(S["out"], 1)
    finish(nc, sems)


def mix_block(nc, m, w, load, x, mix, work, score, mask, mask_rows, dram_score, dram_mask):
    few = max(1, int(round(0.15 * L)))
    n = WIDE
    s = carve(m.scratch[:], {"row": (B, (L,), F32), "less": (B, (L, L), F32), "equal": (B, (L, L), F32),
                             "rank": (B, (L,), F32), "low": (B, (2, L), F32), "sum": (P, (B,), F32),
                             "pooled": (P, (2, B), F32)})
    names = ("product", "score", "stored", "rows", "step", "mask", "mask_stored", "mask_loaded")
    sems = signals(nc, "mix", *names)
    S = dict(zip(names, sems))
    bl = lambda a: a.rearrange("p (b l) -> p b l", l=L)
    with nc.Block() as block:
        @block.sync
        def _(sp):
            load(sp)
            sp.wait_ge(S["score"], T // n + 4)
            sp.dma_start(dram_score, score[0:1, :]).then_inc(S["stored"], 16)
            sp.wait_ge(S["stored"], 16)
            sp.dma_start(s["row"], dram_score.rearrange("a (b l) -> (a b) l", l=L)).then_inc(S["rows"], 16)
            sp.wait_ge(S["mask"], 1)
            for k in range(2):
                sp.dma_start(dram_mask[k].rearrange("(b l) -> b l", l=L), s["low"][:, k, :]
                             ).then_inc(S["mask_stored"], 16)
            sp.wait_ge(S["mask_stored"], 32)
            sp.dma_start(mask, dram_mask[0:1, :].broadcast_to([P, T])).then_inc(S["mask_loaded"], 16)
            sp.dma_start(mask_rows, dram_mask).then_inc(S["mask_loaded"], 16)

        @block.tensor
        def _(pe):
            pe.wait_ge(m.loaded, m.due)
            with pe.Fori(0, T // n // 2) as i:
                for j in range(2):
                    g = 2 * i + j
                    pe.wait_ge(S["score"], g + 3)
                    for c in range(2):
                        last = nc.tensor.matmul(m.psum[0:P, j, 0:n], w["Wr"][:, c:c + 1].broadcast_to([P, P]),
                                                x[:, c, span(g, n)], start=c == 0, stop=c == 1)
                    last.then_inc(S["product"], 1)

        @block.scalar
        def _(act):
            act.sem_inc(S["score"], 4)
            act.wait_ge(m.loaded, m.due)
            with act.Fori(0, T // n // 2) as i:
                for j in range(2):
                    g = 2 * i + j
                    act.wait_ge(S["product"], g + 1)
                    nc.scalar.activation(score[:, span(g, n)], m.psum[0:P, j, 0:n], ACT.Sigmoid,
                                         bias=w["br"]).then_inc(S["score"], 1)

        @block.vector
        def _(dve):
            done = [0]

            def step(ins):
                done[0] += 1
                ins.then_inc(S["step"], 1)
                dve.wait_ge(S["step"], done[0])

            dve.wait_ge(m.loaded, m.due)
            dve.wait_ge(S["rows"], 16)
            si = s["row"].rearrange("p (a l) -> p l a", a=1).broadcast_to([B, L, L])
            sj = s["row"].rearrange("p (a l) -> p a l", a=1).broadcast_to([B, L, L])
            nc.vector.tensor_tensor(s["less"], sj, si, ALU.is_lt)
            step(nc.vector.tensor_tensor(s["equal"], sj, si, ALU.is_equal))
            step(nc.vector.tensor_tensor(s["equal"], s["equal"], w["before"], ALU.mult))
            step(nc.vector.tensor_tensor(s["less"], s["less"], s["equal"], ALU.add))
            step(nc.vector.tensor_reduce(s["rank"], s["less"], AXX, ALU.add))
            nc.vector.tensor_scalar(s["low"][:, 0, :], s["rank"], few - 0.5, None, ALU.is_lt)
            nc.vector.tensor_scalar(s["low"][:, 1, :], s["rank"], few - 0.5, None, ALU.is_gt).then_inc(S["mask"], 1)
            step(nc.vector.tensor_reduce(s["sum"], bl(score), AXX, ALU.add))
            step(nc.vector.tensor_scalar(s["sum"], s["sum"], 1e-6, None, ALU.add))
            step(nc.vector.reciprocal(s["sum"], s["sum"]))
            step(nc.vector.tensor_tensor(bl(mix[:, 0, :]), bl(score),
                                         s["sum"].rearrange("p (b a) -> p b a", a=1).broadcast_to([P, B, L]),
                                         ALU.mult))
            step(nc.vector.tensor_tensor(work, x, mix[:, 0:1, :].broadcast_to([P, 2, T]), ALU.mult))
            step(nc.vector.tensor_reduce(s["pooled"], work.rearrange("p c (b l) -> p c b l", l=L), AXX, ALU.add))
            for c in range(2):
                step(nc.vector.tensor_tensor(bl(mix[:, c, :]), bl(score),
                                             s["pooled"][:, c, :].rearrange("p (b a) -> p b a", a=1)
                                             .broadcast_to([P, B, L]), ALU.mult))
            step(nc.vector.tensor_tensor(mix, mix, x, ALU.add))
            dve.wait_ge(S["mask_loaded"], 32)
            step(nc.vector.tensor_tensor(work, mix, mask.rearrange("p (a t) -> p a t", a=1)
                                         .broadcast_to([P, 2, T]), ALU.mult))
            nc.vector.tensor_tensor(mix, mix, work, ALU.subtract)
    finish(nc, sems)


def softmax_attention_block(nc, m, w, load, x, x0, mix, mask, mask_rows, dst):
    H3 = 3 * L
    s = carve(m.scratch[:], {"x3": (P, (2, GB, 3, L), F32), "q": (P, (2, N), F32), "k": (P, (2, N), F32),
                             "context": (P, (2, N), F32)}
              | {f"{k}{j}": v for j in range(2) for k, v in (
                  ("max", (100, (HEADS,), F32)), ("sum", (100, (HEADS,), F32)),
                  ("prob", (100, (HEADS, L), F32)), ("turned", (H3, (4, 100), F32)),
                  ("v", (H3, (2, 4, P), F32)))} | {"bq": (P, (2,), F32), "apart": (P, (2, GB, 6, L), F32)})
    names = ("copied", "q", "k", "qk_out", "apart", "logits", "values", "v_apart", "max", "sub", "exp", "sum",
             "recip", "prob", "turned", "turned_out", "ctx", "ctx_out", "product", "out", "bq")
    sems = signals(nc, "attention", *names)
    S = dict(zip(names, sems))
    kx = s["apart"]
    PAIRS = GB // 2
    with nc.Block() as block:
        @block.sync
        def _(sp):
            load(sp)

        @block.gpsimd
        def _(pool):
            with pool.Fori(0, GROUPS) as i:
                pool.wait_ge(S["values"], PAIRS * i + 4)
                for c in range(2):
                    nc.gpsimd.tensor_copy(s["x3"][:, c, :, :, :],
                                          x[:, c, span(i, N)].rearrange("p (b a l) -> p b a l", a=1, l=L)
                                          .broadcast_to([P, GB, 3, L])).then_inc(S["copied"], 1)

        @block.tensor
        def _(pe):
            pe.sem_inc(S["values"], 4)
            pe.wait_ge(m.loaded, m.due)

            def projections(i):
                pe.wait_ge(S["turned_out"], PAIRS * i + 2)
                for q, wt in enumerate((w["Wq"], w["Wk"])):
                    if q == 1:
                        pe.wait_ge(S["qk_out"], 4 * i + 2)
                    for c in range(2):
                        for k in range(2):
                            last = nc.tensor.matmul(m.psum[0:P, 4 + c, 0:N], wt[:, k, c * P:c * P + P],
                                                    x[:, k, span(i, N)], start=k == 0, stop=k == 1)
                        last.then_inc(S["q"], 1)

            def group(i, final):

                def front(p):
                    r = p % 2
                    if p == 0:
                        pe.wait_ge(S["copied"], 2 * i + 2)
                    pe.wait_ge(S["v_apart"], PAIRS * i + p + 1)
                    for b in range(2):
                        for c in range(2):
                            rep = s["x3"][:, c, 2 * p + b, :, :].rearrange("p a l -> p (a l)")
                            last = nc.tensor.matmul(m.psum[0:H3, 2 + r, b * D:b * D + D], rep, w["Wv"][:, c, :],
                                                    start=c == 0, stop=c == 1)
                    last.then_inc(S["values"], 1)
                    if p == 0:
                        pe.wait_ge(S["apart"], 2 * i + 2)
                    pe.wait_ge(S["sub"], PAIRS * i + p + 1)
                    for b in range(2):
                        at = (2 * p + b) * L
                        for c in range(2):
                            last = nc.tensor.matmul(m.psum[64 * b:64 * b + L, r, c * 216:c * 216 + 216],
                                                    s["q"][:, c, at:at + L],
                                                    kx[:, c, 2 * p + b, :, :].rearrange("p h l -> p (h l)"),
                                                    start=True, stop=True)
                    last.then_inc(S["logits"], 1)

                def turn(p):
                    r = p % 2
                    pe.wait_ge(S["prob"], PAIRS * i + p + 1)
                    pe.wait_ge(S["turned_out"], PAIRS * i + p + 1)
                    for q in range(4):
                        last = nc.tensor.transpose(m.psum[0:H3, 4 + r, q * 100:q * 100 + 100],
                                                   s[f"prob{r}"][:, 3 * q:3 * q + 3, :].rearrange("p h l -> p (h l)"),
                                                   m.identity[0:100, 0:100])
                    last.then_inc(S["turned"], 1)

                def context(p):
                    r = p % 2
                    pe.wait_ge(S["turned_out"], PAIRS * i + p + 3)
                    pe.wait_ge(S["v_apart"], PAIRS * i + p + 3)
                    for b in range(2):
                        at = (2 * p + b) * L
                        for c in range(2):
                            for q in range(2):
                                last = nc.tensor.matmul(m.psum[0:P, 6 + c, at:at + L],
                                                        s[f"v{r}"][:, b, 2 * c + q, :],
                                                        s[f"turned{r}"][:, 2 * c + q, 64 * b:64 * b + L],
                                                        start=q == 0, stop=q == 1)
                    last.then_inc(S["ctx"], 1)

                front(0)
                front(1)
                pe.wait_ge(S["qk_out"], 4 * i + 4)
                for p in range(PAIRS):
                    turn(p)
                    if p + 2 < PAIRS:
                        front(p + 2)
                    if p == 0:
                        pe.wait_ge(S["out"], 2 * i + 2)
                    context(p)
                if not final:
                    projections(i + 1)
                pe.wait_ge(S["ctx_out"], 2 * i + 2)
                for c in range(2):
                    out = m.psum[0:P, 6 + c, 0:N]
                    for k in range(2):
                        nc.tensor.matmul(out, w["Wo"][:, k, c * P:c * P + P], s["context"][:, k, :],
                                         start=k == 0, stop=False)
                        nc.tensor.matmul(out, w["Wm"][:, k, c * P:c * P + P], mix[:, k, span(i, N)],
                                         start=False, stop=False)
                    nc.tensor.matmul(out, w["bom"][:, c * P:c * P + P], mask_rows[:, span(i, N)],
                                     start=False, stop=True).then_inc(S["product"], 1)

            projections(0)
            with pe.Fori(0, GROUPS - 1) as i:
                group(i, False)
            group(GROUPS - 1, True)

        @block.scalar
        def _(act):
            act.sem_inc(S["turned_out"], 2)
            act.wait_ge(m.loaded, m.due)
            act.wait_ge(S["bq"], 1)

            def projections(i):
                for q in range(2):
                    for c in range(2):
                        act.wait_ge(S["q"], 4 * i + 2 * q + c + 1)
                        if q == 0:
                            nc.scalar.activation(s["q"][:, c, :], m.psum[0:P, 4 + c, 0:N], ACT.Identity,
                                                 bias=s["bq"][:, c:c + 1], scale=DH ** -0.5).then_inc(S["qk_out"], 1)
                        else:
                            nc.scalar.activation(s["k"][:, c, :], m.psum[0:P, 4 + c, 0:N], ACT.Identity,
                                                 bias=w["bk"][:, c:c + 1]).then_inc(S["qk_out"], 1)

            def group(i, final):
                def turned(p):
                    r = p % 2
                    act.wait_ge(S["turned"], PAIRS * i + p + 1)
                    nc.scalar.activation(s[f"turned{r}"],
                                         m.psum[0:H3, 4 + r, 0:400].rearrange("p (a b) -> p a b", a=4),
                                         ACT.Copy).then_inc(S["turned_out"], 1)

                def exponential(p):
                    r = p % 2
                    act.wait_ge(S["sub"], PAIRS * i + p + 3)
                    nc.scalar.activation(s[f"prob{r}"], s[f"prob{r}"], ACT.Exp).then_inc(S["exp"], 1)

                exponential(0)
                exponential(1)
                for p in range(PAIRS):
                    turned(p)
                    if p + 2 < PAIRS:
                        exponential(p + 2)
                if not final:
                    projections(i + 1)

            projections(0)
            with act.Fori(0, GROUPS - 1) as i:
                group(i, False)
            group(GROUPS - 1, True)

        @block.vector
        def _(dve):
            dve.sem_inc(S["out"], 2)
            dve.sem_inc(S["v_apart"], 2)
            dve.sem_inc(S["sub"], 2)
            dve.wait_ge(m.loaded, m.due)
            nc.vector.tensor_scalar(s["bq"], w["bq"], DH ** -0.5, None, ALU.mult).then_inc(S["bq"], 1)

            def keys_apart(i):
                for c in range(2):
                    dve.wait_ge(S["qk_out"], 4 * i + 3 + c)
                    for h in range(6):
                        last = nc.vector.tensor_scalar(kx[:, c, :, h, :],
                                                       s["k"][:, c, :].rearrange("p (b l) -> p b l", l=L),
                                                       w["head"][:, h:h + 1], None, ALU.mult)
                    last.then_inc(S["apart"], 1)

            def group(i, final):
                def top(p):
                    r = p % 2
                    dve.wait_ge(S["logits"], PAIRS * i + p + 1)
                    lg = m.psum[0:100, r, 0:432].rearrange("p (h l) -> p h l", l=L)
                    nc.vector.tensor_reduce(s[f"max{r}"], lg, AXX, ALU.max).then_inc(S["max"], 1)
                    dve.wait_ge(S["max"], PAIRS * i + p + 1)
                    if p >= 2:
                        dve.wait_ge(S["turned"], PAIRS * i + p - 1)
                    nc.vector.tensor_tensor(s[f"prob{r}"], lg,
                                            s[f"max{r}"].rearrange("p (h a) -> p h a", a=1)
                                            .broadcast_to([100, HEADS, L]), ALU.subtract).then_inc(S["sub"], 1)
                    dve.wait_ge(S["values"], PAIRS * i + p + 5)
                    if p >= 2:
                        dve.wait_ge(S["ctx"], PAIRS * i + p - 1)
                    for b in range(2):
                        v = m.psum[0:H3, 2 + r, b * D:b * D + D].rearrange("p (c a f) -> p c a f", c=2, a=1)
                        last = nc.vector.tensor_tensor(
                            s[f"v{r}"][:, b, :, :].rearrange("p (c q) f -> p c q f", c=2),
                            v.broadcast_to([H3, 2, 2, P]),
                            w["rows"].rearrange("p (a q) f -> p a q f", a=1).broadcast_to([H3, 2, 2, P]),
                            ALU.mult)
                    last.then_inc(S["v_apart"], 1)

                def norm(p):
                    r = p % 2
                    dve.wait_ge(S["exp"], PAIRS * i + p + 1)
                    nc.vector.tensor_reduce(s[f"sum{r}"], s[f"prob{r}"], AXX, ALU.add).then_inc(S["sum"], 1)
                    dve.wait_ge(S["sum"], PAIRS * i + p + 1)
                    nc.vector.reciprocal(s[f"sum{r}"], s[f"sum{r}"]).then_inc(S["recip"], 1)
                    dve.wait_ge(S["recip"], PAIRS * i + p + 1)
                    nc.vector.tensor_tensor(s[f"prob{r}"], s[f"prob{r}"],
                                            s[f"sum{r}"].rearrange("p (h a) -> p h a", a=1)
                                            .broadcast_to([100, HEADS, L]), ALU.mult).then_inc(S["prob"], 1)

                top(0)
                top(1)
                for p in range(PAIRS):
                    norm(p)
                    if 1 <= p < PAIRS - 1:
                        top(p + 1)
                dve.wait_ge(S["ctx"], PAIRS * i + PAIRS)
                for c in range(2):
                    nc.vector.scalar_tensor_tensor(out=s["context"][:, c, :], in0=m.psum[0:P, 6 + c, 0:N],
                                                   scalar=w["bv"][:, c:c + 1], in1=mask[:, span(i, N)],
                                                   op0=ALU.add, op1=ALU.mult).then_inc(S["ctx_out"], 1)
                if not final:
                    keys_apart(i + 1)
                for c in range(2):
                    dve.wait_ge(S["product"], 2 * i + c + 1)
                    nc.vector.tensor_tensor(dst[:, c, span(i, N)], m.psum[0:P, 6 + c, 0:N],
                                            x0[:, c, span(i, N)], ALU.add).then_inc(S["out"], 1)

            keys_apart(0)
            with dve.Fori(0, GROUPS - 1) as i:
                group(i, False)
            group(GROUPS - 1, True)
    finish(nc, sems)


def rates_block(nc, m, w, load, x, delta, coef, rates):
    n = WIDE
    s = carve(m.scratch[:], {f"{k}{j}": v for j in range(2) for k, v in (
        ("mag", (128, (2, n), F32)), ("rest", (32, (n,), F32)), ("high", (32, (n,), BF16)),
        ("mid", (32, (n,), BF16)))} | {"lmag": (128, (24,), F32)})
    names = ("product", "mag", "exp", "log", "max", "out", "high", "rest", "mid", "low", "rates",
             "negated")
    sems = signals(nc, "rates", *names)
    S = dict(zip(names, sems))
    with nc.Block() as block:
        @block.sync
        def _(sp):
            load(sp)

        @block.tensor
        def _(pe):
            pe.wait_ge(m.loaded, m.due)
            with pe.Fori(0, T // n // 2) as i:
                for j in range(2):
                    g = 2 * i + j
                    pe.wait_ge(S["out"], g + 1)
                    pe.wait_ge(S["low"], g + 1)
                    for c in range(2):
                        for k in range(2):
                            nc.tensor.matmul(m.psum[:, 3 * j + c, 0:n], w["Wd"][:, k, c * 128:c * 128 + 128],
                                             x[:, k, span(g, n)], start=k == 0, stop=k == 1)
                    for k in range(2):
                        last = nc.tensor.matmul(m.psum[0:32, 3 * j + 2, 0:n], w["WBC"][:, k, :],
                                                x[:, k, span(g, n)], start=k == 0, stop=k == 1)
                    last.then_inc(S["product"], 1)

        @block.scalar
        def _(act):
            nc.scalar.preload_act_table_set(LOG_EXP)
            act.wait_ge(m.loaded, m.due)
            nc.scalar.activation(s["lmag"], w["loglam"], ACT.Abs).then_inc(S["rates"], 1)
            act.wait_ge(S["rates"], 1)
            nc.scalar.activation(s["lmag"], s["lmag"], ACT.Exp, scale=-1.0).then_inc(S["rates"], 1)
            act.wait_ge(S["rates"], 2)
            nc.scalar.activation(s["lmag"], s["lmag"], ACT.Ln, bias=m.ones[:, 0:1]).then_inc(S["rates"], 1)
            with act.Fori(0, T // n // 2) as i:
                for j in range(2):
                    g = 2 * i + j
                    act.wait_ge(S["product"], g + 1)
                    act.wait_ge(S["out"], g + 1)
                    act.wait_ge(S["low"], g + 1)
                    nc.scalar.activation(s[f"high{j}"], m.psum[0:32, 3 * j + 2, 0:n], ACT.Copy)
                    nc.scalar.activation(coef[0:32, span(g, n)], m.psum[0:32, 3 * j + 2, 0:n],
                                         ACT.Copy).then_inc(S["high"], 1)
                    for c in range(2):
                        last = nc.scalar.activation(s[f"mag{j}"][:, c, :], m.psum[:, 3 * j + c, 0:n], ACT.Abs,
                                                    bias=w["bd"][:, c:c + 1])
                    last.then_inc(S["mag"], 1)
                for j in range(2):
                    g = 2 * i + j
                    act.wait_ge(S["mag"], g + 1)
                    nc.scalar.activation(s[f"mag{j}"], s[f"mag{j}"], ACT.Exp, scale=-1.0).then_inc(S["exp"], 1)
                    act.wait_ge(S["exp"], g + 1)
                    nc.scalar.activation(s[f"mag{j}"], s[f"mag{j}"], ACT.Ln, bias=m.ones[:, 0:1]
                                         ).then_inc(S["log"], 1)
                    act.wait_ge(S["rest"], g + 1)
                    nc.scalar.activation(s[f"mid{j}"], s[f"rest{j}"], ACT.Copy)
                    nc.scalar.activation(coef[32:64, span(g, n)], s[f"rest{j}"], ACT.Copy).then_inc(S["mid"], 1)

        @block.vector
        def _(dve):
            dve.sem_inc(S["out"], 2)
            dve.sem_inc(S["low"], 2)
            dve.wait_ge(m.loaded, m.due)
            nc.vector.tensor_scalar(rates, w["loglam"], 0.0, None, ALU.max).then_inc(S["negated"], 1)
            dve.wait_ge(S["rates"], 3)
            dve.wait_ge(S["negated"], 1)
            nc.vector.tensor_tensor(rates, rates, s["lmag"], ALU.add).then_inc(S["negated"], 1)
            dve.wait_ge(S["negated"], 2)
            nc.vector.tensor_scalar(rates, rates, -1.0, None, ALU.mult)
            with dve.Fori(0, T // n // 2) as i:
                for j in range(2):
                    g = 2 * i + j
                    dve.wait_ge(S["high"], g + 1)
                    nc.vector.tensor_tensor(s[f"rest{j}"], m.psum[0:32, 3 * j + 2, 0:n], s[f"high{j}"],
                                            ALU.subtract).then_inc(S["rest"], 1)
                    dve.wait_ge(S["mag"], g + 1)
                    for c in range(2):
                        last = nc.vector.tensor_scalar(delta[:, c, span(g, n)], m.psum[:, 3 * j + c, 0:n],
                                                       w["bd"][:, c:c + 1], 0.0, ALU.add, ALU.max)
                    last.then_inc(S["max"], 1)
                for j in range(2):
                    g = 2 * i + j
                    dve.wait_ge(S["log"], g + 1)
                    dve.wait_ge(S["max"], g + 1)
                    d = delta[:, :, span(g, n)]
                    nc.vector.tensor_tensor(d, d, s[f"mag{j}"], ALU.add).then_inc(S["out"], 1)
                    dve.wait_ge(S["mid"], g + 1)
                    nc.vector.tensor_tensor(coef[64:96, span(g, n)], s[f"rest{j}"], s[f"mid{j}"],
                                            ALU.subtract).then_inc(S["low"], 1)
    finish(nc, sems)


def scan_block(nc, m, w, load, delta, coef, rates):
    CH = 24
    s = carve(m.scratch[:], {f"{k}{j}": (128, (N,), F32) for j in range(2) for k in ("a", "b", "h", "y")}
              | {"pick": (96, (32,), BF16), "picks": (96, (16, 128), BF16), "delta": (128, (2, N), F32)})
    names = ("copied", "pick", "zero", "spread", "a", "b", "scan", "y", "out", "sum")
    sems = signals(nc, "scan", *names)
    S = dict(zip(names, sems))
    bl = lambda t: t.rearrange("p (b l) -> p b l", l=L)
    part = lambda q: 0 if q < STATES else 1
    with nc.Block() as block:
        @block.sync
        def _(sp):
            load(sp)

        @block.gpsimd
        def _(pool):
            with pool.Fori(0, GROUPS) as i:
                pool.wait_ge(S["a"], CH * i + 2)
                nc.gpsimd.tensor_copy(s["delta"], delta[:, :, span(i, N)]).then_inc(S["copied"], 1)

        @block.tensor
        def _(pe):
            pe.wait_ge(m.loaded, m.due)
            pe.wait_ge(S["pick"], 2)
            with pe.Fori(0, GROUPS) as i:
                def out(q):
                    pe.wait_ge(S["y"], CH * i + q + 4)
                    if q == 0:
                        pe.wait_ge(S["sum"], 2 * i + 2)
                    for c in range(2):
                        last = nc.tensor.matmul(m.psum[0:P, 6 + c, 0:N], w["Wout"][:, q, c * P:c * P + P],
                                                s[f"y{q % 2}"], start=q == 0, stop=q == CH - 1)
                    last.then_inc(S["out"], 1)

                def spread(q):
                    pe.wait_ge(S["y"], CH * i + q + 1)
                    for k in range(2):
                        if part(q) == 0:
                            pick = s["pick"][:, 16 * k + q:16 * k + q + 1].broadcast_to([96, 128])
                        else:
                            pick = s["picks"][:, 8 * k + q - STATES, :]
                        last = nc.tensor.matmul(m.psum[:, 2 * (q % 3) + k, 0:N], pick, coef[:, span(i, N)],
                                                start=True, stop=True)
                    last.then_inc(S["spread"], 1)

                spread(0)
                spread(1)
                for q in range(CH):
                    if q + 2 < CH:
                        spread(q + 2)
                    out(q)

        @block.scalar
        def _(act):
            act.sem_inc(S["a"], 2)
            act.wait_ge(S["zero"], 2)
            with act.Fori(0, GROUPS) as i:
                for q in range(CH):
                    act.wait_ge(S["scan"], CH * i + q + 1)
                    if q == 0:
                        act.wait_ge(S["copied"], i + 1)
                    nc.scalar.activation(bl(s[f"a{q % 2}"])[:, :, 1:L], bl(s["delta"][:, part(q), :])[:, :, 1:L],
                                         ACT.Exp, scale=rates[:, q:q + 1]).then_inc(S["a"], 1)

        @block.vector
        def _(dve):
            dve.sem_inc(S["y"], 3)
            dve.sem_inc(S["scan"], 2)
            dve.sem_inc(S["out"], 2)
            dve.sem_inc(S["sum"], 2)
            dve.wait_ge(m.loaded, m.due)
            nc.vector.tensor_copy(s["pick"], w["pick"]).then_inc(S["pick"], 1)
            nc.vector.tensor_copy(s["picks"].rearrange("p m (h r) -> p (m h) r", h=2),
                                  w["pick"].rearrange("p (n a) -> p n a", a=1).broadcast_to([96, 32, 64])
                                  ).then_inc(S["pick"], 1)
            for j in range(2):
                nc.vector.memset(bl(s[f"a{j}"])[:, :, 0:1], 0.0).then_inc(S["zero"], 1)
            with dve.Fori(0, GROUPS) as i:
                def inputs(q):
                    dve.wait_ge(S["spread"], CH * i + q + 1)
                    dve.wait_ge(S["scan"], CH * i + q + 1)
                    nc.vector.tensor_tensor(s[f"b{q % 2}"], delta[:, part(q), span(i, N)],
                                            m.psum[:, 2 * (q % 3), 0:N], ALU.mult).then_inc(S["b"], 1)

                inputs(0)
                for q in range(CH):
                    dve.wait_ge(S["a"], CH * i + q + 3)
                    dve.wait_ge(S["b"], CH * i + q + 1)
                    dve.wait_ge(S["y"], CH * i + q + 2)
                    nc.vector.tensor_tensor_scan(s[f"h{q % 2}"], s[f"a{q % 2}"], s[f"b{q % 2}"], 0.0, ALU.mult,
                                                 ALU.add).then_inc(S["scan"], 1)
                    if q + 1 < CH:
                        inputs(q + 1)
                    dve.wait_ge(S["scan"], CH * i + q + 3)
                    dve.wait_ge(S["out"], CH * i + q + 1)
                    nc.vector.tensor_tensor(s[f"y{q % 2}"], s[f"h{q % 2}"], m.psum[:, 2 * (q % 3) + 1, 0:N],
                                            ALU.mult).then_inc(S["y"], 1)
                dve.wait_ge(S["out"], CH * i + CH + 2)
                for c in range(2):
                    h = m.h[:, c, span(i, N)]
                    nc.vector.scalar_tensor_tensor(out=h, in0=m.psum[0:P, 6 + c, 0:N], scalar=w["bout"][:, c:c + 1],
                                                   in1=h, op0=ALU.add, op1=ALU.add).then_inc(S["sum"], 1)
    finish(nc, sems)


def image_gate_block(nc, m, w, load, x, gates, dram_gates):
    E = 3
    s = carve(m.scratch[:], {"mean": (P, (2, B), F32), "logit": (B, (E,), F32), "top": (B, (1,), F32),
                             "first": (B, (E,), F32), "rest": (B, (1,), F32)})
    names = ("mean", "logits", "step", "exp", "gates", "stored", "done")
    sems = signals(nc, "gate", *names)
    S = dict(zip(names, sems))
    with nc.Block() as block:
        @block.sync
        def _(sp):
            load(sp)
            sp.wait_ge(S["gates"], 1)
            for e in range(E):
                sp.dma_start(dram_gates[e].rearrange("(b a) -> b a", a=1), s["logit"][:, e:e + 1]
                             ).then_inc(S["stored"], 16)
            sp.wait_ge(S["stored"], 16 * E)
            sp.dma_start(gates, dram_gates.rearrange("(a e) b -> a (e b)", a=1).broadcast_to([P, E * B])
                         ).then_inc(S["done"], 16)
            sp.wait_ge(S["done"], 16)

        @block.tensor
        def _(pe):
            pe.wait_ge(m.loaded, m.due)
            pe.wait_ge(S["mean"], 1)
            for c in range(2):
                last = nc.tensor.matmul(m.psum[0:B, 0, 0:E], s["mean"][:, c, :], w["Wg"][:, c, :],
                                        start=c == 0, stop=c == 1)
            last.then_inc(S["logits"], 1)

        @block.scalar
        def _(act):
            act.wait_ge(S["step"], 3)
            nc.scalar.activation(s["logit"], s["logit"], ACT.Exp).then_inc(S["exp"], 1)

        @block.vector
        def _(dve):
            done = [0]

            def step(ins):
                done[0] += 1
                ins.then_inc(S["step"], 1)
                dve.wait_ge(S["step"], done[0])

            step(nc.vector.tensor_reduce(s["mean"], x.rearrange("p c (b l) -> p c b l", l=L), AXX, ALU.add))
            nc.vector.tensor_scalar(s["mean"], s["mean"], 1.0 / L, None, ALU.mult).then_inc(S["mean"], 1)
            dve.wait_ge(S["logits"], 1)
            step(nc.vector.tensor_reduce(s["top"], m.psum[0:B, 0, 0:E], AXX, ALU.max))
            step(nc.vector.tensor_scalar(s["logit"], m.psum[0:B, 0, 0:E], s["top"], None, ALU.subtract))
            dve.wait_ge(S["exp"], 1)
            step(nc.vector.tensor_reduce(s["rest"], s["logit"], AXX, ALU.add))
            step(nc.vector.reciprocal(s["rest"], s["rest"]))
            step(nc.vector.tensor_scalar(s["logit"], s["logit"], s["rest"], None, ALU.mult))
            step(nc.vector.tensor_reduce(s["top"], s["logit"], AXX, ALU.max))
            step(nc.vector.tensor_scalar(s["first"], s["logit"], s["top"], None, ALU.is_equal))
            step(nc.vector.tensor_scalar(s["rest"], s["first"][:, 0:1], -1.0, 1.0, ALU.mult, ALU.add))
            step(nc.vector.tensor_tensor(s["first"][:, 1:2], s["first"][:, 1:2], s["rest"], ALU.mult))
            step(nc.vector.tensor_tensor(s["first"][:, 2:3], s["rest"], s["first"][:, 1:2], ALU.subtract))
            nc.vector.tensor_tensor(s["logit"], s["logit"], s["first"], ALU.mult).then_inc(S["gates"], 1)
    finish(nc, sems)


def retention_block(nc, m, w, load, x):
    s = carve(m.scratch[:], {f"{k}{j}": v for j in range(2) for k, v in (
        ("x", (P, (2, N), F32)), ("q", (P, (2, N), F32)), ("k", (P, (2, N), F32)),
        ("v", (PAIR, (4, D), F32)), ("score", (PAIR, (4, PAIR), F32)))})
    ps = lambda j, q: m.psum[:, 4 * j + q, :]
    names = ("copied", "queries", "keys", "q_out", "k_out", "values", "v_out", "scores", "masked", "sums", "out")
    sems = signals(nc, "retention", *names)
    S = dict(zip(names, sems))
    with nc.Block() as block:
        @block.sync
        def _(sp):
            load(sp)

        @block.gpsimd
        def _(pool):
            with pool.Fori(0, GROUPS // 2) as i:
                for j in range(2):
                    g = 2 * i + j
                    pool.wait_ge(S["values"], g + 1)
                    nc.gpsimd.tensor_copy(s[f"x{j}"], x[:, :, span(g, N)]).then_inc(S["copied"], 1)

        @block.tensor
        def _(pe):
            pe.sem_inc(S["values"], 2)
            pe.wait_ge(m.loaded, m.due)
            with pe.Fori(0, GROUPS // 2) as i:
                for j in range(2):
                    g = 2 * i + j
                    pe.wait_ge(S["out"], g + 1)
                    for q in range(2):
                        for c in range(2):
                            for k in range(2):
                                last = nc.tensor.matmul(ps(j, 2 * q + c)[0:P, 0:N],
                                                        w["Wqkv"][:, k, q * D + c * P:q * D + c * P + P],
                                                        x[:, k, span(g, N)], start=k == 0, stop=k == 1)
                        last.then_inc(S["queries"] if q == 0 else S["keys"], 1)
                for j in range(2):
                    g = 2 * i + j
                    pe.wait_ge(S["copied"], g + 1)
                    pe.wait_ge(S["q_out"], g + 1)
                    for p in range(4):
                        for c in range(2):
                            last = nc.tensor.matmul(ps(j, p // 2)[0:PAIR, (p % 2) * D:(p % 2) * D + D],
                                                    s[f"x{j}"][:, c, p * PAIR:p * PAIR + PAIR],
                                                    w["Wqkv"][:, c, 2 * D:3 * D], start=c == 0, stop=c == 1)
                    last.then_inc(S["values"], 1)
                    pe.wait_ge(S["k_out"], g + 1)
                    for p in range(4):
                        for c in range(2):
                            last = nc.tensor.matmul(ps(j, 2)[0:PAIR, p * PAIR:p * PAIR + PAIR],
                                                    s[f"k{j}"][:, c, p * PAIR:p * PAIR + PAIR],
                                                    s[f"q{j}"][:, c, p * PAIR:p * PAIR + PAIR],
                                                    start=c == 0, stop=c == 1)
                    last.then_inc(S["scores"], 1)
                for j in range(2):
                    g = 2 * i + j
                    pe.wait_ge(S["v_out"], g + 1)
                    pe.wait_ge(S["masked"], g + 1)
                    for c in range(2):
                        for p in range(4):
                            last = nc.tensor.matmul(ps(j, 3 * (1 - c))[0:P, p * PAIR:p * PAIR + PAIR],
                                                    s[f"v{j}"][:, p, c * P:c * P + P], s[f"score{j}"][:, p, :],
                                                    start=True, stop=True)
                    last.then_inc(S["sums"], 1)

        @block.scalar
        def _(act):
            act.wait_ge(m.loaded, m.due)
            with act.Fori(0, GROUPS // 2) as i:
                for q, (done, out, t) in enumerate((("queries", "q_out", "q"), ("keys", "k_out", "k"))):
                    for j in range(2):
                        g = 2 * i + j
                        act.wait_ge(S[done], g + 1)
                        for c in range(2):
                            last = nc.scalar.activation(s[f"{t}{j}"][:, c, :], ps(j, 2 * q + c)[0:P, 0:N],
                                                        ACT.Identity, bias=w["bqk"][:, 2 * q + c:2 * q + c + 1])
                        last.then_inc(S[out], 1)

        @block.vector
        def _(dve):
            dve.sem_inc(S["out"], 2)
            dve.wait_ge(m.loaded, m.due)
            with dve.Fori(0, GROUPS // 2) as i:
                for j in range(2):
                    g = 2 * i + j
                    dve.wait_ge(S["values"], g + 3)
                    for q in range(2):
                        last = nc.vector.tensor_tensor(
                            s[f"v{j}"][:, 2 * q:2 * q + 2, :],
                            ps(j, q)[0:PAIR, 0:2 * D].rearrange("p (a b) -> p a b", a=2),
                            w["bv"].rearrange("p (a b) -> p a b", a=1).broadcast_to([PAIR, 2, D]), ALU.add)
                    last.then_inc(S["v_out"], 1)
                    dve.wait_ge(S["scores"], g + 1)
                    nc.vector.tensor_tensor(s[f"score{j}"], ps(j, 2)[0:PAIR, 0:N].rearrange("p (a b) -> p a b", a=4),
                                            w["decay"].rearrange("p (a b) -> p a b", a=1)
                                            .broadcast_to([PAIR, 4, PAIR]), ALU.mult).then_inc(S["masked"], 1)
                for j in range(2):
                    g = 2 * i + j
                    dve.wait_ge(S["sums"], g + 1)
                    for c in range(2):
                        h = m.h[:, c, span(g, N)]
                        last = nc.vector.tensor_tensor(h, ps(j, 3 * (1 - c))[0:P, 0:N], h, ALU.add)
                    last.then_inc(S["out"], 1)
    finish(nc, sems)


def adapter_block(nc, m, w, load, x, logits, hidden, gates, dram_logits, dram_gates):
    n, E, R = WIDE, 3, 8
    TT = T // 128
    s = carve(m.scratch[:], {"logit": (128, (E, TT), F32), "top": (128, (TT,), F32), "sum": (128, (TT,), F32),
                             "drop": (128, (E, TT), F32), "keep": (128, (E, TT), F32)})
    names = ("product", "acted", "stored", "loaded", "step", "exp", "gates", "gates_stored", "gates_loaded")
    sems = signals(nc, "adapter", *names)
    S = dict(zip(names, sems))
    one = lambda a: a.rearrange("p (a t) -> p a t", a=1).broadcast_to([128, E, TT])
    with nc.Block() as block:
        @block.sync
        def _(sp):
            load(sp)
            sp.wait_ge(S["acted"], T // n + 2)
            sp.dma_start(dram_logits, logits).then_inc(S["stored"], 16)
            sp.wait_ge(S["stored"], 16)
            for e in range(E):
                sp.dma_start(s["logit"][:, e, :], dram_logits[e].rearrange("(p t) -> p t", p=128)
                             ).then_inc(S["loaded"], 16)
            sp.wait_ge(S["gates"], 1)
            for e in range(E):
                sp.dma_start(dram_gates[e].rearrange("(p t) -> p t", p=128), s["keep"][:, e, :]
                             ).then_inc(S["gates_stored"], 16)
            sp.wait_ge(S["gates_stored"], 16 * E)
            for e in range(E):
                sp.dma_start(gates[R * e:R * e + R, :], dram_gates[e:e + 1, :].broadcast_to([R, T])
                             ).then_inc(S["gates_loaded"], 16)

        @block.tensor
        def _(pe):
            pe.wait_ge(m.loaded, m.due)
            with pe.Fori(0, T // n // 2) as i:
                for j in range(2):
                    g = 2 * i + j
                    pe.wait_ge(S["acted"], g + 1)
                    for out, wt in ((m.psum[0:E, 2 * j, 0:n], w["router"]), (m.psum[0:E * R, 2 * j + 1, 0:n], w["down"])):
                        for c in range(2):
                            last = nc.tensor.matmul(out, wt[:, c, :], x[:, c, span(g, n)], start=c == 0, stop=c == 1)
                    last.then_inc(S["product"], 1)

        @block.scalar
        def _(act):
            act.sem_inc(S["acted"], 2)
            act.wait_ge(m.loaded, m.due)
            with act.Fori(0, T // n // 2) as i:
                for j in range(2):
                    g = 2 * i + j
                    act.wait_ge(S["product"], g + 1)
                    nc.scalar.activation(logits[:, span(g, n)], m.psum[0:E, 2 * j, 0:n], ACT.Identity,
                                         bias=w["router_b"])
                    nc.scalar.activation(hidden[:, span(g, n)], m.psum[0:E * R, 2 * j + 1, 0:n],
                                         ACT.Gelu).then_inc(S["acted"], 1)
            act.wait_ge(S["step"], 2)
            nc.scalar.activation(s["logit"], s["logit"], ACT.Exp).then_inc(S["exp"], 1)

        @block.vector
        def _(dve):
            done = [0]

            def step(ins):
                done[0] += 1
                ins.then_inc(S["step"], 1)
                dve.wait_ge(S["step"], done[0])

            dve.wait_ge(S["loaded"], 16 * E)
            te = lambda a: a.rearrange("p e t -> p t e")
            step(nc.vector.tensor_reduce(s["top"], te(s["logit"]), AXX, ALU.max))
            step(nc.vector.tensor_tensor(s["logit"], s["logit"], one(s["top"]), ALU.subtract))
            dve.wait_ge(S["exp"], 1)
            step(nc.vector.tensor_reduce(s["sum"], te(s["logit"]), AXX, ALU.add))
            step(nc.vector.reciprocal(s["sum"], s["sum"]))
            step(nc.vector.tensor_tensor(s["logit"], s["logit"], one(s["sum"]), ALU.mult))
            p = [s["logit"][:, e, :] for e in range(E)]
            d = [s["drop"][:, e, :] for e in range(E)]
            step(nc.vector.tensor_tensor(d[0], p[2], p[0], ALU.is_le))
            step(nc.vector.tensor_tensor(d[2], p[2], p[1], ALU.is_le))
            step(nc.vector.tensor_tensor(d[2], d[2], d[0], ALU.mult))
            step(nc.vector.tensor_scalar(s["sum"], d[2], -1.0, 1.0, ALU.mult, ALU.add))
            step(nc.vector.tensor_tensor(d[1], p[1], p[0], ALU.is_le))
            step(nc.vector.tensor_tensor(d[1], d[1], s["sum"], ALU.mult))
            step(nc.vector.tensor_tensor(d[0], s["sum"], d[1], ALU.subtract))
            step(nc.vector.tensor_scalar(s["drop"], s["drop"], -1.0, 1.0, ALU.mult, ALU.add))
            step(nc.vector.tensor_tensor(s["keep"], s["logit"], s["drop"], ALU.mult))
            step(nc.vector.tensor_reduce(s["sum"], te(s["keep"]), AXX, ALU.add))
            step(nc.vector.tensor_scalar(s["sum"], s["sum"], 1e-6, None, ALU.add))
            step(nc.vector.reciprocal(s["sum"], s["sum"]))
            nc.vector.tensor_tensor(s["keep"], s["keep"], one(s["sum"]), ALU.mult).then_inc(S["gates"], 1)
            dve.wait_ge(S["gates_loaded"], 16 * E)
            dve.wait_ge(S["acted"], T // n + 2)
            nc.vector.tensor_tensor(hidden, hidden, gates, ALU.mult)
    finish(nc, sems)


def mamba_input_block(nc, m, w, load, x, xc, gate):
    C, TAPS = DI // 128, 4
    LP = L + TAPS - 1
    s = carve(m.scratch[:], {f"{k}{j}": v for j in range(2) for k, v in (
        ("pad", (128, (C, GB, LP), F32)), ("conv", (128, (C, GB, L), F32)))})
    names = ("zero", "product", "padded", "tap", "conv", "silu")
    sems = signals(nc, "input", *names)
    S = dict(zip(names, sems))
    bl = lambda t: t.rearrange("p (b l) -> p b l", l=L)
    per = 2 * C
    with nc.Block() as block:
        @block.sync
        def _(sp):
            load(sp)

        @block.tensor
        def _(pe):
            pe.wait_ge(m.loaded, m.due)
            with pe.Fori(0, GROUPS // 2) as i:
                for j in range(2):
                    g = 2 * i + j
                    for k in range(per):
                        pe.wait_ge(S["padded"], per * g + k + 1)
                        for c in range(2):
                            last = nc.tensor.matmul(m.psum[:, k, 0:N], w["Win"][:, c, k * 128:k * 128 + 128],
                                                    x[:, c, span(g, N)], start=c == 0, stop=c == 1)
                        last.then_inc(S["product"], 1)

        @block.scalar
        def _(act):
            nc.scalar.preload_act_table_set(SILU)
            act.sem_inc(S["padded"], per)
            act.wait_ge(m.loaded, m.due)
            act.wait_ge(S["zero"], 2)
            with act.Fori(0, GROUPS // 2) as i:
                for j in range(2):
                    g = 2 * i + j
                    act.wait_ge(S["conv"], C * g + C)
                    for k in range(per):
                        act.wait_ge(S["product"], per * g + k + 1)
                        if k < C:
                            nc.scalar.activation(s[f"pad{j}"][:, k, :, TAPS - 1:LP], bl(m.psum[:, k, 0:N]),
                                                 ACT.Copy).then_inc(S["padded"], 1)
                        else:
                            nc.scalar.activation(gate[:, k - C, span(g, N)], m.psum[:, k, 0:N],
                                                 ACT.Silu).then_inc(S["padded"], 1)
                for j in range(2):
                    g = 2 * i + j
                    for k in range(C):
                        act.wait_ge(S["conv"], C * g + k + 7)
                        nc.scalar.activation(bl(xc[:, k, span(g, N)]), s[f"conv{j}"][:, k, :, :], ACT.Silu,
                                             bias=w["conv_b"][:, k:k + 1]).then_inc(S["silu"], 1)

        @block.vector
        def _(dve):
            dve.sem_inc(S["conv"], 6)
            for j in range(2):
                nc.vector.memset(s[f"pad{j}"][:, :, :, 0:TAPS - 1], 0.0).then_inc(S["zero"], 1)
            dve.wait_ge(m.loaded, m.due)
            dve.sem_inc(S["silu"], 6)
            with dve.Fori(0, GROUPS // 2) as i:
                for j in range(2):
                    g = 2 * i + j
                    dve.wait_ge(S["silu"], C * g + C)
                    for k in range(C):
                        dve.wait_ge(S["padded"], per * g + k + 7)
                        out = s[f"conv{j}"][:, k, :, :]
                        for tap in range(TAPS):
                            src = s[f"pad{j}"][:, k, :, tap:tap + L]
                            wt = w["conv_w"][:, k, tap:tap + 1]
                            if tap:
                                dve.wait_ge(S["tap"], (TAPS - 1) * (C * g + k) + tap)
                                ins = nc.vector.scalar_tensor_tensor(out=out, in0=src, scalar=wt, in1=out,
                                                                     op0=ALU.mult, op1=ALU.add)
                            else:
                                ins = nc.vector.tensor_scalar(out, src, wt, None, ALU.mult)
                            ins.then_inc(S["conv" if tap == TAPS - 1 else "tap"], 1)
    finish(nc, sems)


def mamba_rates_block(nc, m, w, load, xc, dt, coef, rates):
    n, C = N, DI // 128
    s = carve(m.scratch[:], {f"{k}{j}": v for j in range(2) for k, v in (
        ("mag", (128, (C, n), F32)), ("rest", (32, (n,), F32)), ("high", (32, (n,), BF16)),
        ("mid", (32, (n,), BF16)), ("raw", (1, (n,), F32)))})
    names = ("coefs", "raw", "product", "mag", "exp", "log", "max", "out", "high", "rest", "mid", "low", "rates",
             "negated")
    sems = signals(nc, "mrates", *names)
    S = dict(zip(names, sems))
    small = lambda j: m.psum[:, 3 + 4 * j, :]
    with nc.Block() as block:
        @block.sync
        def _(sp):
            load(sp)

        @block.tensor
        def _(pe):
            pe.wait_ge(m.loaded, m.due)
            with pe.Fori(0, T // n // 2) as i:
                for j in range(2):
                    g = 2 * i + j
                    pe.wait_ge(S["low"], g + 1)
                    pe.wait_ge(S["product"], g + 1)
                    pe.wait_ge(S["out"], g + 1)
                    for k in range(C):
                        nc.tensor.matmul(small(j)[0:32, 0:n], w["xproj"][:, k, 0:32], xc[:, k, span(g, n)],
                                         start=k == 0, stop=k == C - 1)
                    for k in range(C):
                        last = nc.tensor.matmul(m.psum[0:1, 4 * j, 0:n], w["xproj"][:, k, 32:33],
                                                xc[:, k, span(g, n)], start=k == 0, stop=k == C - 1)
                    last.then_inc(S["coefs"], 1)
                for j in range(2):
                    g = 2 * i + j
                    pe.wait_ge(S["raw"], g + 1)
                    for k in range(C):
                        last = nc.tensor.matmul(m.psum[:, 4 * j + k, 0:n], w["w_dt"][:, k * 128:k * 128 + 128],
                                                s[f"raw{j}"], start=True, stop=True)
                    last.then_inc(S["product"], 1)

        @block.scalar
        def _(act):
            nc.scalar.preload_act_table_set(LOG_EXP)
            act.wait_ge(m.loaded, m.due)
            nc.scalar.activation(rates, w["A_log"], ACT.Exp).then_inc(S["rates"], 1)
            with act.Fori(0, T // n // 2) as i:
                for j in range(2):
                    g = 2 * i + j
                    act.wait_ge(S["coefs"], g + 1)
                    act.wait_ge(S["product"], g + 1)
                    act.wait_ge(S["low"], g + 1)
                    nc.scalar.activation(s[f"raw{j}"], m.psum[0:1, 4 * j, 0:n], ACT.Copy).then_inc(S["raw"], 1)
                    nc.scalar.activation(s[f"high{j}"], small(j)[0:32, 0:n], ACT.Copy)
                    nc.scalar.activation(coef[0:32, span(g, n)], small(j)[0:32, 0:n], ACT.Copy
                                         ).then_inc(S["high"], 1)
                for j in range(2):
                    g = 2 * i + j
                    act.wait_ge(S["product"], g + 3)
                    act.wait_ge(S["out"], g + 1)
                    for k in range(C):
                        last = nc.scalar.activation(s[f"mag{j}"][:, k, :], m.psum[:, 4 * j + k, 0:n], ACT.Abs,
                                                    bias=w["b_dt"][:, k:k + 1])
                    last.then_inc(S["mag"], 1)
                    act.wait_ge(S["mag"], g + 1)
                    nc.scalar.activation(s[f"mag{j}"], s[f"mag{j}"], ACT.Exp, scale=-1.0).then_inc(S["exp"], 1)
                    act.wait_ge(S["exp"], g + 1)
                    nc.scalar.activation(s[f"mag{j}"], s[f"mag{j}"], ACT.Ln, bias=m.ones[:, 0:1]
                                         ).then_inc(S["log"], 1)
                    act.wait_ge(S["rest"], g + 1)
                    nc.scalar.activation(s[f"mid{j}"], s[f"rest{j}"], ACT.Copy)
                    nc.scalar.activation(coef[32:64, span(g, n)], s[f"rest{j}"], ACT.Copy).then_inc(S["mid"], 1)

        @block.vector
        def _(dve):
            dve.sem_inc(S["out"], 2)
            dve.sem_inc(S["low"], 2)
            dve.sem_inc(S["product"], 2)
            dve.wait_ge(m.loaded, m.due)
            dve.wait_ge(S["rates"], 1)
            nc.vector.tensor_scalar(rates, rates, -1.0, None, ALU.mult).then_inc(S["negated"], 1)
            with dve.Fori(0, T // n // 2) as i:
                for j in range(2):
                    g = 2 * i + j
                    dve.wait_ge(S["high"], g + 1)
                    nc.vector.tensor_tensor(s[f"rest{j}"], small(j)[0:32, 0:n], s[f"high{j}"],
                                            ALU.subtract).then_inc(S["rest"], 1)
                for j in range(2):
                    g = 2 * i + j
                    dve.wait_ge(S["mag"], g + 1)
                    for k in range(C):
                        last = nc.vector.tensor_scalar(dt[:, k, span(g, n)], m.psum[:, 4 * j + k, 0:n],
                                                       w["b_dt"][:, k:k + 1], 0.0, ALU.add, ALU.max)
                    last.then_inc(S["max"], 1)
                    dve.wait_ge(S["log"], g + 1)
                    dve.wait_ge(S["max"], g + 1)
                    d = dt[:, :, span(g, n)]
                    nc.vector.tensor_tensor(d, d, s[f"mag{j}"], ALU.add).then_inc(S["out"], 1)
                    dve.wait_ge(S["mid"], g + 1)
                    nc.vector.tensor_tensor(coef[64:96, span(g, n)], s[f"rest{j}"], s[f"mid{j}"],
                                            ALU.subtract).then_inc(S["low"], 1)
    finish(nc, sems)


def mamba_scan_block(nc, m, w, load, xc, gate, dt, coef, rates, dst):
    C = DI // 128
    s = carve(m.scratch[:], {f"{k}{j}": (128, (C, N), F32) for j in range(2) for k in ("a", "b", "h", "y")}
              | {"pick": (96, (32,), BF16), "dt": (128, (C, N), F32), "dtx": (128, (C, N), F32),
                 "gated": (128, (C, N), F32)})
    names = ("copied", "pick", "zero", "spread", "a", "b", "scan", "y", "sum", "dtx", "skip", "gated", "out", "added")
    sems = signals(nc, "mscan", *names)
    S = dict(zip(names, sems))
    bl = lambda t: t.rearrange("p (b l) -> p b l", l=L)
    flat = lambda t: t.rearrange("p c t -> p (c t)")
    with nc.Block() as block:
        @block.sync
        def _(sp):
            load(sp)

        @block.gpsimd
        def _(pool):
            with pool.Fori(0, GROUPS) as i:
                pool.wait_ge(S["a"], STATES * i + 2)
                nc.gpsimd.tensor_copy(s["dt"], dt[:, :, span(i, N)]).then_inc(S["copied"], 1)

        @block.tensor
        def _(pe):
            pe.wait_ge(m.loaded, m.due)
            pe.wait_ge(S["pick"], 1)
            with pe.Fori(0, GROUPS) as i:
                def spread(q):
                    pe.wait_ge(S["y"], STATES * i + q + 1)
                    for k in range(2):
                        last = nc.tensor.matmul(m.psum[:, 2 * (q % 2) + k, 0:N],
                                                s["pick"][:, 16 * k + q:16 * k + q + 1].broadcast_to([96, 128]),
                                                coef[:, span(i, N)], start=True, stop=True)
                    last.then_inc(S["spread"], 1)

                def add(q):
                    pe.wait_ge(S["y"], STATES * i + q + 3)
                    if q == 0:
                        pe.wait_ge(S["added"], 2 * i + 2)
                    for c in range(C):
                        last = nc.tensor.matmul(m.psum[:, 4 + c, 0:N], m.identity[:], s[f"y{q % 2}"][:, c, :],
                                                start=q == 0, stop=q == STATES - 1)
                    last.then_inc(S["sum"], 1)

                spread(0)
                spread(1)
                for q in range(STATES):
                    if q + 2 < STATES:
                        spread(q + 2)
                    add(q)
                pe.wait_ge(S["gated"], i + 1)
                for c in range(2):
                    for k in range(C):
                        last = nc.tensor.matmul(m.psum[0:P, 7 if c == 0 else 4, 0:N],
                                                w["Wout"][:, k, c * P:c * P + P], s["gated"][:, k, :],
                                                start=k == 0, stop=k == C - 1)
                    last.then_inc(S["out"], 1)

        @block.scalar
        def _(act):
            act.sem_inc(S["a"], 2)
            act.wait_ge(S["zero"], 2)
            with act.Fori(0, GROUPS) as i:
                act.wait_ge(S["copied"], i + 1)
                for q in range(STATES):
                    act.wait_ge(S["scan"], STATES * i + q + 1)
                    for c in range(C):
                        last = nc.scalar.activation(bl(s[f"a{q % 2}"][:, c, :])[:, :, 1:L],
                                                    bl(s["dt"][:, c, :])[:, :, 1:L],
                                                    ACT.Exp, scale=rates[:, c, q:q + 1])
                    last.then_inc(S["a"], 1)

        @block.vector
        def _(dve):
            for k, v in (("y", 2), ("scan", 2), ("sum", 2), ("added", 2), ("out", 2)):
                dve.sem_inc(S[k], v)
            dve.wait_ge(m.loaded, m.due)
            nc.vector.tensor_copy(s["pick"], w["pick"]).then_inc(S["pick"], 1)
            for j in range(2):
                nc.vector.memset(s[f"a{j}"].rearrange("p c (b l) -> p c b l", l=L)[:, :, :, 0:1], 0.0
                                 ).then_inc(S["zero"], 1)
            with dve.Fori(0, GROUPS) as i:
                nc.vector.tensor_tensor(s["dtx"], dt[:, :, span(i, N)], xc[:, :, span(i, N)],
                                        ALU.mult).then_inc(S["dtx"], 1)
                dve.wait_ge(S["dtx"], i + 1)

                def spread_of(q, k):
                    return m.psum[:, 2 * (q % 2) + k:2 * (q % 2) + k + 1, 0:N].broadcast_to([128, C, N])

                def inputs(q):
                    dve.wait_ge(S["spread"], STATES * i + q + 1)
                    dve.wait_ge(S["scan"], STATES * i + q + 1)
                    nc.vector.tensor_tensor(s[f"b{q % 2}"], s["dtx"], spread_of(q, 0), ALU.mult).then_inc(S["b"], 1)

                inputs(0)
                for q in range(STATES):
                    dve.wait_ge(S["a"], STATES * i + q + 3)
                    dve.wait_ge(S["b"], STATES * i + q + 1)
                    dve.wait_ge(S["y"], STATES * i + q + 1)
                    nc.vector.tensor_tensor_scan(flat(s[f"h{q % 2}"]), flat(s[f"a{q % 2}"]), flat(s[f"b{q % 2}"]),
                                                 0.0, ALU.mult, ALU.add).then_inc(S["scan"], 1)
                    if q + 1 < STATES:
                        inputs(q + 1)
                    dve.wait_ge(S["scan"], STATES * i + q + 3)
                    dve.wait_ge(S["sum"], STATES * i + q + 1)
                    nc.vector.tensor_tensor(s[f"y{q % 2}"], s[f"h{q % 2}"], spread_of(q, 1),
                                            ALU.mult).then_inc(S["y"], 1)
                dve.wait_ge(S["sum"], STATES * i + STATES + 2)
                dve.wait_ge(S["out"], 2 * i + 2)
                for c in range(C):
                    nc.vector.scalar_tensor_tensor(out=s["gated"][:, c, :], in0=xc[:, c, span(i, N)],
                                                   scalar=w["D"][:, c:c + 1], in1=m.psum[:, 4 + c, 0:N],
                                                   op0=ALU.mult, op1=ALU.add).then_inc(S["skip"], 1)
                dve.wait_ge(S["skip"], C * i + C)
                nc.vector.tensor_tensor(s["gated"], s["gated"], gate[:, :, span(i, N)],
                                        ALU.mult).then_inc(S["gated"], 1)
                for c in range(2):
                    dve.wait_ge(S["out"], 2 * i + c + 3)
                    d = dst[:, c, span(i, N)]
                    nc.vector.tensor_tensor(d, m.psum[0:P, 7 if c == 0 else 4, 0:N], d,
                                            ALU.add).then_inc(S["added"], 1)
    finish(nc, sems)


def route_block(nc, m, w, load, name, x, r, rows, tokens, y_rows):
    E, K, STRIDE = r.experts, r.picks, r.stride
    R, TM, NT = STRIDE // TILE, r.steps, RT * K
    s = carve(m.scratch[:], {f"{k}{j}": v for j in range(2) for k, v in (
        ("x", (P, (2, ROWS), F32)), ("row", (128, (D,), F32)), ("score", (128, (E,), F32)),
        ("choice", (128, (E,), F32)), ("best", (128, (8,), F32)), ("index", (128, (8,), U32)),
        ("indexf", (128, (8,), F32)), ("hot", (128, (K, E), F32)), ("picked", (128, (K, E), F32)), ("ranked", (128, (K, E), F32)),
        ("mask", (128, (E,), BF16)), ("total", (128, (E,), BF16)))} | {
        "before": (128, (128,), BF16), "ones": (128, (128,), BF16), "router": (P, (2, E), F32),
        "expert": (128, (RT, K), F32), "rank": (128, (RT, K), F32), "keep": (128, (RT, K), F32),
        "slotf": (128, (RT, K), F32), "value": (128, (RT, K), F32),
        "sum": (128, (RT, 1), F32),
        "count": (128, (1,), F32), "steps": (128, (1,), F32), "over": (128, (R,), F32),
        "end": (128, (1,), F32), "passed": (128, (TM,), F32), "passed_steps": (128, (TM,), F32),
        "tabf": (1, (2 * TM + 8,), F32)})
    names = ("ids", "dve_turn", "copied", "products", "rows_out", "stored0", "stored1", "scores", "choice", "best",
             "index", "indexf", "hot", "mask", "total", "ranks", "picked", "done", "step", "exp", "slots",
             "count", "counted", "ends", "ended", "row_ready", "weighed")
    sems = signals(nc, name, *names)
    S = dict(zip(names, sems))
    stored = S["stored0"], S["stored1"]
    per_k = lambda a: a.rearrange("p (a e) -> p a e", a=1).broadcast_to([128, K, E])
    with nc.Block() as block:
        @block.sync
        def _(sp):
            load(sp)
            with sp.Fori(0, RT // 2) as i:
                for j in range(2):
                    sp.wait_ge(S["rows_out"], 2 * i + j + 3)
                    sp.dma_start(rows[bass.ds((2 * i + j) * ROWS, ROWS), :], s[f"row{j}"]).then_inc(stored[j], 16)
            for j in range(2):
                sp.wait_ge(stored[j], 16 * (RT // 2) + 16)

        @block.gpsimd
        def _(pool):
            pool.wait_ge(m.loaded, m.due)
            nc.gpsimd.iota(r.ids, pattern=[[ROWS, RT], [0, 1]], base=0, channel_multiplier=1
                           ).then_inc(S["ids"], 1)
            with pool.Fori(0, RT // 2) as i:
                for j in range(2):
                    t = 2 * i + j
                    pool.wait_ge(S["products"], t + 1)
                    nc.gpsimd.tensor_copy(s[f"x{j}"], x[:, :, span(t, ROWS)]).then_inc(S["copied"], 1)
            pool.wait_ge(S["ids"], 1)

        @block.tensor
        def _(pe):
            pe.sem_inc(S["products"], 2)
            pe.sem_inc(S["ranks"], 1)
            pe.wait_ge(m.loaded, m.due)
            pe.wait_ge(S["row_ready"], 4)

            def products(i):
                for j in range(2):
                    t = 2 * i + j
                    pe.wait_ge(S["copied"], t + 1)
                    pe.wait_ge(S["rows_out"], t + 1)
                    pe.wait_ge(S["scores"], t + 1)
                    for c in range(2):
                        nc.tensor.transpose(m.psum[:, 4 * j, c * P:c * P + P], s[f"x{j}"][:, c, :],
                                            m.identity[0:P, 0:P])
                    for c in range(2):
                        last = nc.tensor.matmul(m.psum[:, 4 * j + 1, 0:E], s[f"x{j}"][:, c, :], s["router"][:, c, :],
                                                start=c == 0, stop=c == 1)
                    last.then_inc(S["products"], 1)

            def ranks(i):
                for j in range(2):
                    t = 2 * i + j
                    pe.wait_ge(S["mask"], t + 1)
                    pe.wait_ge(S["total"], t + 1)
                    nc.tensor.matmul(m.psum[:, 4 * j + 2, 0:E], s["before"], s[f"mask{j}"], start=True, stop=False)
                    nc.tensor.matmul(m.psum[:, 4 * j + 2, 0:E], s["ones"], s[f"total{j}"], start=False, stop=True
                                     ).then_inc(S["ranks"], 1)

            products(0)
            with pe.Fori(0, RT // 2 - 1) as i:
                products(i + 1)
                ranks(i)
            ranks(RT // 2 - 1)
            pe.wait_ge(S["total"], RT + 1)
            nc.tensor.matmul(m.psum[0:E, 3, 0:1], s["total0"], s["ones"][:, 0:1], start=True, stop=True
                             ).then_inc(S["count"], 1)
            pe.wait_ge(S["counted"], 3)
            nc.tensor.matmul(m.psum[0:E, 3, 1:2], w["upto"][0:E, 0:E], s["steps"][0:E, :], start=True, stop=True
                             ).then_inc(S["count"], 1)
            pe.wait_ge(S["ended"], 3)
            one = m.ones[0:E, 0:1]
            nc.tensor.matmul(m.psum[0:1, 7, 0:TM], one, s["passed"][0:E, :], start=True, stop=True)
            nc.tensor.matmul(m.psum[0:1, 7, TM:2 * TM], one, s["passed_steps"][0:E, :], start=True, stop=True)
            nc.tensor.matmul(m.psum[0:1, 7, 2 * TM:2 * TM + 1], one, s["steps"][0:E, :], start=True, stop=True
                             ).then_inc(S["count"], 1)

        @block.scalar
        def _(act):
            nc.scalar.preload_act_table_set(SIGMOID)
            act.sem_inc(stored[0], 16)
            act.sem_inc(stored[1], 16)
            act.sem_inc(S["rows_out"], 2)
            act.sem_inc(S["scores"], 2)
            with act.Fori(0, RT // 2) as i:
                for j in range(2):
                    t = 2 * i + j
                    act.wait_ge(S["products"], t + 3)
                    act.wait_ge(stored[j], 16 * i + 16)
                    nc.scalar.activation(s[f"row{j}"], m.psum[:, 4 * j, 0:D], ACT.Copy).then_inc(S["rows_out"], 1)
                    act.wait_ge(S["done"], t + 1)
                    nc.scalar.activation(s[f"score{j}"], m.psum[:, 4 * j + 1, 0:E],
                                         ACT.Sigmoid if r.sigmoid else ACT.Copy).then_inc(S["scores"], 1)
            if not r.sigmoid:
                act.wait_ge(S["step"], 4)
                nc.scalar.activation(s["value"], s["value"], ACT.Exp).then_inc(S["exp"], 1)

        @block.vector
        def _(dve):
            done = [0]

            def step(ins):
                done[0] += 1
                ins.then_inc(S["step"], 1)
                dve.wait_ge(S["step"], done[0])

            dve.sem_inc(S["done"], 2)
            dve.sem_inc(S["picked"], 4)
            dve.wait_ge(m.loaded, m.due)
            nc.vector.tensor_copy(s["before"], w["before"]).then_inc(S["row_ready"], 1)
            nc.vector.tensor_copy(s["ones"], m.ones[:]).then_inc(S["row_ready"], 1)
            for c in range(2):
                if r.scaled:
                    ins = nc.vector.tensor_scalar(s["router"][:, c, :], w["router"][:, c, :], w["gamma"][:, c:c + 1],
                                                  None, ALU.mult)
                else:
                    ins = nc.vector.tensor_copy(s["router"][:, c, :], w["router"][:, c, :])
                ins.then_inc(S["row_ready"], 1)
            nc.vector.memset(s["total0"], 0.0).then_inc(S["total"], 1)
            with dve.Fori(0, RT // 2) as i:
                for j in range(2):
                    t = 2 * i + j
                    dve.wait_ge(S["scores"], t + 3)
                    dve.wait_ge(S["done"], t + 1)
                    if r.bias:
                        choice = s[f"choice{j}"]
                        nc.vector.tensor_tensor(choice, s[f"score{j}"], w["bias"], ALU.add).then_inc(S["choice"], 1)
                        dve.wait_ge(S["choice"], t + 1)
                    else:
                        choice = s[f"score{j}"]
                    own_wait(dve, S["dve_turn"])
                    nc.vector.max(s[f"best{j}"], choice).then_inc(S["best"], 1)
                    dve.wait_ge(S["best"], t + 1)
                    own_wait(dve, S["dve_turn"])
                    nc.vector.max_index(s[f"index{j}"], s[f"best{j}"], choice).then_inc(S["index"], 1)
                    dve.wait_ge(S["index"], t + 1)
                    nc.vector.tensor_copy(s[f"indexf{j}"], s[f"index{j}"]).then_inc(S["indexf"], 1)
                    dve.wait_ge(S["indexf"], t + 1)
                    dve.wait_ge(S["picked"], 2 * t + 2)
                    nc.vector.tensor_copy(s["expert"][:, bass.ds(t, 1), :].rearrange("p a k -> p (a k)"),
                                          s[f"indexf{j}"][:, 0:K])
                    nc.vector.tensor_tensor(s[f"hot{j}"], per_k(w["iota"]),
                                            s[f"indexf{j}"][:, 0:K].rearrange("p (k a) -> p k a", a=1)
                                            .broadcast_to([128, K, E]), ALU.is_equal).then_inc(S["hot"], 1)
                    dve.wait_ge(S["hot"], t + 1)
                    with nc.allow_low_precision("sums of zeros and ones"):
                        nc.vector.tensor_reduce(s[f"mask{j}"], s[f"hot{j}"].rearrange("p k e -> p e k"), AXX,
                                                ALU.add).then_inc(S["mask"], 1)
                    dve.wait_ge(S["mask"], t + 1)
                    dve.wait_ge(S["total"], t + 1)
                    dve.wait_ge(S["ranks"], t + 1)
                    nc.vector.tensor_tensor(s[f"total{1 - j}"], s[f"total{j}"], s[f"mask{j}"], ALU.add
                                            ).then_inc(S["total"], 1)
                    at = lambda a: s[a][:, bass.ds(t, 1), :].rearrange("p a k -> p (a k)")
                    if r.sigmoid:
                        nc.vector.tensor_tensor(s[f"picked{j}"], s[f"hot{j}"], per_k(s[f"score{j}"]),
                                                ALU.mult).then_inc(S["weighed"], 1)
                        dve.wait_ge(S["weighed"], t + 1)
                        nc.vector.tensor_reduce(at("value"), s[f"picked{j}"], AXX, ALU.add).then_inc(S["done"], 1)
                    else:
                        nc.vector.tensor_copy(at("value"), s[f"best{j}"][:, 0:K]).then_inc(S["done"], 1)
                for j in range(2):
                    t = 2 * i + j
                    at = lambda a: s[a][:, bass.ds(t, 1), :].rearrange("p a k -> p (a k)")
                    dve.wait_ge(S["ranks"], t + 2)
                    nc.vector.tensor_tensor(s[f"ranked{j}"], s[f"hot{j}"], per_k(m.psum[:, 4 * j + 2, 0:E]),
                                            ALU.mult).then_inc(S["picked"], 1)
                    dve.wait_ge(S["picked"], 2 * t + 5)
                    nc.vector.tensor_reduce(at("rank"), s[f"ranked{j}"], AXX, ALU.add).then_inc(S["picked"], 1)
            dve.wait_ge(S["done"], RT + 2)
            dve.wait_ge(S["picked"], 2 * RT + 4)
            weight, slot = r.weight, r.slot
            step(nc.vector.tensor_scalar(s["keep"], s["rank"], r.capacity - 0.5, None, ALU.is_lt))
            step(nc.vector.scalar_tensor_tensor(out=s["slotf"], in0=s["expert"], scalar=float(STRIDE), in1=s["rank"],
                                                op0=ALU.mult, op1=ALU.add))
            if r.sigmoid:
                step(nc.vector.tensor_reduce(s["sum"], s["value"], AXX, ALU.add))
                step(nc.vector.tensor_scalar(s["sum"], s["sum"], 1e-20, None, ALU.add))
            else:
                step(nc.vector.tensor_copy(s["sum"], s["value"][:, :, 0:1]))
                step(nc.vector.tensor_tensor(s["value"], s["value"], s["sum"].broadcast_to([128, RT, K]),
                                             ALU.subtract))
                dve.wait_ge(S["exp"], 1)
                step(nc.vector.tensor_reduce(s["sum"], s["value"], AXX, ALU.add))
            step(nc.vector.reciprocal(s["sum"], s["sum"]))
            step(nc.vector.tensor_tensor(s["value"], s["value"], s["sum"].broadcast_to([128, RT, K]), ALU.mult))
            step(nc.vector.scalar_tensor_tensor(out=weight, in0=s["value"], scalar=r.factor, in1=s["keep"],
                                                op0=ALU.mult, op1=ALU.mult))
            step(nc.vector.tensor_tensor(s["slotf"], s["slotf"], s["keep"], ALU.mult))
            step(nc.vector.tensor_scalar(s["keep"], s["keep"], -1.0, 1.0, ALU.mult, ALU.add))
            step(nc.vector.scalar_tensor_tensor(out=slot, in0=s["keep"], scalar=float(r.slots - 1), in1=s["slotf"],
                                                op0=ALU.mult, op1=ALU.add))
            step(nc.vector.tensor_tensor(s["keep"], s["keep"], w["spill"], ALU.mult))
            nc.vector.tensor_tensor(r.scatter, s["keep"], s["slotf"], ALU.add).then_inc(S["slots"], 1)
            dve.wait_ge(S["count"], 1)
            nc.vector.tensor_scalar(s["count"][0:E, :], m.psum[0:E, 3, 0:1], float(r.capacity), None, ALU.min
                                    ).then_inc(S["counted"], 1)
            dve.wait_ge(S["counted"], 1)
            nc.vector.tensor_scalar(s["over"][0:E, :], w["starts"][0:E, :], s["count"][0:E, :], None, ALU.is_lt
                                    ).then_inc(S["counted"], 1)
            dve.wait_ge(S["counted"], 2)
            nc.vector.tensor_reduce(s["steps"][0:E, :], s["over"][0:E, :], AXX, ALU.add).then_inc(S["counted"], 1)
            dve.wait_ge(S["count"], 2)
            nc.vector.tensor_copy(s["end"][0:E, :], m.psum[0:E, 3, 1:2]).then_inc(S["ended"], 1)
            dve.wait_ge(S["ended"], 1)
            nc.vector.tensor_scalar(s["passed"][0:E, :], w["numbers"][0:E, :], s["end"][0:E, :], None, ALU.is_ge
                                    ).then_inc(S["ended"], 1)
            dve.wait_ge(S["ended"], 2)
            nc.vector.tensor_scalar(s["passed_steps"][0:E, :], s["passed"][0:E, :], s["steps"][0:E, :], None,
                                    ALU.mult).then_inc(S["ended"], 1)
            dve.wait_ge(S["count"], 3)
            ps = m.psum[0:1, 7, :]
            tf = s["tabf"]
            step(nc.vector.tensor_tensor(tf[:, 0:TM], w["numbers"][0:1, :], ps[:, TM:2 * TM], ALU.subtract))
            step(nc.vector.tensor_scalar(tf[:, TM:2 * TM], tf[:, 0:TM], float(TILE), None, ALU.mult))
            step(nc.vector.scalar_tensor_tensor(out=tf[:, TM:2 * TM], in0=ps[:, 0:TM], scalar=float(STRIDE),
                                                in1=tf[:, TM:2 * TM], op0=ALU.mult, op1=ALU.add))
            step(nc.vector.tensor_scalar(tf[:, TM:2 * TM], tf[:, TM:2 * TM], float(E * STRIDE), None, ALU.min))
            step(nc.vector.tensor_scalar(tf[:, 0:TM], ps[:, 0:TM], float(E - 1), None, ALU.min))
            step(nc.vector.tensor_scalar(tf[:, 2 * TM:2 * TM + 1], ps[:, 2 * TM:2 * TM + 1], 0.5, 0.25, ALU.mult,
                                         ALU.add))
            nc.vector.tensor_copy(r.table[:, 0:2 * TM + 1], tf[:, 0:2 * TM + 1])
    finish(nc, sems)


class Scatter:

    def __init__(self, nc, m, name, r, tokens, scratch):
        self.nc, self.m, self.r, self.tokens = nc, m, r, tokens
        self.s = carve(scratch, {f"{k}{j}": v for j in range(2) for k, v in (
            ("slots", (128, (r.picks,), U32)), ("token", (128, (1,), U32)))})
        self.sems = signals(nc, name, "staged", "slots_free", "scattered0", "scattered1", "pool_turn")
        self.staged, self.slots_free, *scattered, self.pool_turn = self.sems
        self.scattered = scattered

    def sync(self, sp):
        K = self.r.picks
        sp.sem_inc(self.slots_free, 2)
        with sp.Fori(0, RT // 2) as i:
            for j in range(2):
                sp.wait_ge(self.scattered[j], 16 * K * i + 16 * K)
                sp.sem_inc(self.slots_free, 1)

    def gpsimd(self, pool):
        nc, m, r, s, K = self.nc, self.m, self.r, self.s, self.r.picks
        row = lambda a, t: a[:, bass.ds(t, 1), :].rearrange("p a k -> p (a k)")
        pool.wait_ge(m.filled, m.all_filled)
        with pool.Fori(0, RT // 2) as i:
            for j in range(2):
                t = 2 * i + j
                pool.wait_ge(self.slots_free, t + 1)
                nc.gpsimd.tensor_copy(s[f"slots{j}"], row(r.scatter, t))
                nc.gpsimd.tensor_copy(s[f"token{j}"], row(r.ids, t)).then_inc(self.staged, 1)
                pool.wait_ge(self.staged, t + 1)
                own_wait(pool, self.pool_turn)
                for k in range(K):
                    nc.gpsimd.indirect_dma_start(
                        out=self.tokens, in_=s[f"token{j}"], in_offset=None,
                        out_offset=bass.IndirectOffsetOnAxis(ap=s[f"slots{j}"][:, k:k + 1], axis=0)
                    ).then_inc(self.scattered[j], 16)
        for j in range(2):
            pool.wait_ge(self.scattered[j], 16 * K * (RT // 2))

    def vector(self, dve, i, j):
        pass


class Gather:

    def __init__(self, nc, name, r, y_rows, sums, gathered, scratch):
        self.nc, self.r, self.y_rows, self.sums, self.gathered = nc, r, y_rows, sums, gathered
        self.s = carve(scratch, {f"{k}{j}": (128, (r.picks,), t) for j in range(2) for k, t in (
            ("slots", U32), ("weights", F32))} | {f"sum{j}": (128, (D,), F32) for j in range(2)})
        self.sems = signals(nc, name, "staged", "gathered0", "gathered1", "weights", "sum", "pool_turn")
        self.staged, *arrived, self.weights, self.sum, self.pool_turn = self.sems
        self.arrived = arrived

    def row(self, a, t):
        return a[:, bass.ds(t, 1), :].rearrange("p a k -> p (a k)")

    def sync(self, sp):
        pass

    def gpsimd(self, pool):
        nc, r, s, K = self.nc, self.r, self.s, self.r.picks
        pool.sem_inc(self.sum, 2 * K)
        with pool.Fori(0, RT // 2) as i:
            for j in range(2):
                t = 2 * i + j
                pool.wait_ge(self.sum, K * t + K)
                nc.gpsimd.tensor_copy(s[f"slots{j}"], self.row(r.slot, t)).then_inc(self.staged, 1)
                pool.wait_ge(self.staged, t + 1)
                own_wait(pool, self.pool_turn)
                for k in range(K):
                    nc.gpsimd.indirect_dma_start(
                        out=self.gathered[j][:, k, :], out_offset=None, in_=self.y_rows,
                        in_offset=bass.IndirectOffsetOnAxis(ap=s[f"slots{j}"][:, k:k + 1], axis=0)
                    ).then_inc(self.arrived[j], 16)

    def vector(self, dve, i, j):
        nc, r, s, K = self.nc, self.r, self.s, self.r.picks
        for n in range(3 * j, 3 * j + 3):
            t, b = 6 * i + n, n % 2
            dve.wait_ge(self.sum, K * t + K)
            nc.vector.tensor_copy(s[f"weights{b}"], self.row(r.weight, t)).then_inc(self.weights, 1)
            dve.wait_ge(self.weights, t + 1)
            dve.wait_ge(self.arrived[b], 16 * K * (3 * i + n // 2) + 16 * K)
            for k in range(K):
                g, wt, acc = self.gathered[b][:, k, :], s[f"weights{b}"][:, k:k + 1], s[f"sum{b}"]
                if k == 0:
                    ins = nc.vector.tensor_scalar(acc, g, wt, None, ALU.mult)
                else:
                    dve.wait_ge(self.sum, K * t + 2 * K + k)
                    dst = self.row(self.sums, t) if k == K - 1 else acc
                    ins = nc.vector.scalar_tensor_tensor(out=dst, in0=g, scalar=wt, in1=acc, op0=ALU.mult,
                                                         op1=ALU.add)
                ins.then_inc(self.sum, 1)


def scatter_block(nc, m, name, load, r, tokens):
    side = Scatter(nc, m, name, r, tokens, m.scratch[:])
    with nc.Block() as block:
        @block.sync
        def _(sp):
            load(sp)
            side.sync(sp)

        @block.gpsimd
        def _(pool):
            side.gpsimd(pool)
    finish(nc, side.sems)


def output_block(nc, m, name, load, sums, h, out):
    s = carve(m.scratch[:], {f"{k}{j}": v for j in range(2) for k, v in (
        ("h", (P, (2, ROWS), F32)), ("row", (128, (D,), F32)))})
    sems = signals(nc, name, "copied", "turned", "added", "stored0", "stored1")
    s_copied, s_turned, s_added, *s_stored = sems
    with nc.Block() as block:
        @block.sync
        def _(sp):
            load(sp)
            with sp.Fori(0, RT // 2) as i:
                for j in range(2):
                    t = 2 * i + j
                    sp.wait_ge(s_added, t + 3)
                    sp.dma_start(out[bass.ds(t * ROWS, ROWS), :], s[f"row{j}"]).then_inc(s_stored[j], 16)
            for j in range(2):
                sp.wait_ge(s_stored[j], 16 * (RT // 2) + 16)

        @block.scalar
        def _(act):
            with act.Fori(0, RT // 2) as i:
                for j in range(2):
                    t = 2 * i + j
                    act.wait_ge(s_turned, t + 1)
                    nc.scalar.activation(s[f"h{j}"], h[:, :, span(t, ROWS)], ACT.Copy).then_inc(s_copied, 1)

        @block.tensor
        def _(pe):
            pe.sem_inc(s_turned, 2)
            with pe.Fori(0, RT // 2) as i:
                for j in range(2):
                    t = 2 * i + j
                    pe.wait_ge(s_added, t + 1)
                    pe.wait_ge(s_copied, t + 1)
                    for c in range(2):
                        last = nc.tensor.transpose(m.psum[:, j, c * P:c * P + P], s[f"h{j}"][:, c, :],
                                                   m.identity[0:P, 0:P])
                    last.then_inc(s_turned, 1)

        @block.vector
        def _(dve):
            dve.sem_inc(s_added, 2)
            for j in range(2):
                dve.sem_inc(s_stored[j], 16)
            with dve.Fori(0, RT // 2) as i:
                for j in range(2):
                    t = 2 * i + j
                    dve.wait_ge(s_turned, t + 3)
                    dve.wait_ge(s_stored[j], 16 * i + 16)
                    nc.vector.tensor_tensor(s[f"row{j}"], sums[:, bass.ds(t, 1), :].rearrange("p a d -> p (a d)"),
                                            m.psum[:, j, 0:D], ALU.add).then_inc(s_added, 1)
    finish(nc, sems)


def expert_block(nc, m, load, name, r, rows, tokens, y_rows, wg, wu, wd, chunk, chunks, scale=None):
    E, TM = r.experts, r.steps
    F = chunk * chunks
    s = carve(m.scratch[:], {f"{k}{j}": v for j in range(2) for k, v in (
        ("index", (P, (2,), U32)), ("gathered", (P, (2, D), F32)), ("x", (P, (2, TILE), F32)),
        ("silu", (chunk, (TILE,), F32)), ("hidden", (chunk, (chunks, TILE), F32)), ("y", (P, (2, D), F32)),
        ("scale", (P, (2,), F32)))})
    wb = carve(m.full[:, 4:10, :].rearrange("p a t -> p (a t)"), {f"{k}{j}": v for j in range(2) for k, v in (
        ("wg", (P, (2, F), F32)), ("wu", (P, (2, F), F32)), ("wd", (chunk, (chunks, D), F32)))})
    names = ("index0", "index1", "weights0", "weights1", "gathered0", "gathered1", "turned", "x", "up", "silu",
             "hidden", "down", "y", "stored0", "stored1", "down_weights0", "down_weights1", "pool_turn", "act_turn", "sp_turn")
    sems = signals(nc, name, *names)
    S = dict(zip(names, sems))
    pair = lambda k: (S[k + "0"], S[k + "1"])
    s_index, s_weights, s_down_weights, s_gathered, s_stored = map(
        pair, ("index", "weights", "down_weights", "gathered", "stored"))
    loads = 16 * (2 if scale is None else 3)
    trips = lambda eng: eng.value_load(r.table[0:1, 2 * TM:2 * TM + 1], min_val=1, max_val=TM // 2)
    first_slot = lambda eng, t: eng.value_load(r.table[0:1, bass.ds(t + TM, 1)], min_val=0, max_val=E * r.stride)
    with nc.Block() as block:
        @block.sync
        def _(sp):
            load(sp)
            with sp.Fori(0, trips(sp)) as i:
                for j in range(2):
                    t = 2 * i + j
                    at = first_slot(sp, t)
                    sp.wait_ge(S["turned"], t + 1)
                    own_wait(sp, S["sp_turn"])
                    sp.dma_start(s[f"index{j}"], tokens[bass.ds(at, TILE), :].rearrange("(p h) a -> p (h a)", h=2)
                                 ).then_inc(s_index[j], 16)
                for j in range(2):
                    t = 2 * i + j
                    e = sp.value_load(r.table[0:1, bass.ds(t, 1)], min_val=0, max_val=E - 1)
                    sp.wait_ge(S["up"], chunks * t + chunks)
                    own_wait(sp, S["sp_turn"])
                    for k, src in ((wb[f"wg{j}"], wg), (wb[f"wu{j}"], wu)):
                        sp.dma_start(k, src[bass.ds(e, 1)].rearrange("e p c f -> p (e c) f")
                                     ).then_inc(s_weights[j], 16)
                    if scale is not None:
                        sp.dma_start(s[f"scale{j}"], scale[bass.ds(e, 1)].rearrange("e p c -> p (e c)")
                                     ).then_inc(s_weights[j], 16)
                for j in range(2):
                    t = 2 * i + j
                    e = sp.value_load(r.table[0:1, bass.ds(t, 1)], min_val=0, max_val=E - 1)
                    sp.wait_ge(S["down"], t + 1)
                    own_wait(sp, S["sp_turn"])
                    sp.dma_start(wb[f"wd{j}"], wd[bass.ds(e, 1)].rearrange("e p c f -> p (e c) f")
                                 ).then_inc(s_down_weights[j], 16)

        @block.gpsimd
        def _(pool):
            with pool.Fori(0, trips(pool)) as i:
                for j in range(2):
                    t = 2 * i + j
                    pool.wait_ge(s_index[j], 16 * i + 16)
                    pool.wait_ge(S["turned"], t + 1)
                    own_wait(pool, S["pool_turn"])
                    for h in range(2):
                        nc.gpsimd.indirect_dma_start(
                            out=s[f"gathered{j}"][:, h, :], out_offset=None, in_=rows,
                            in_offset=bass.IndirectOffsetOnAxis(ap=s[f"index{j}"][:, h:h + 1], axis=0)
                        ).then_inc(s_gathered[j], 16)

        @block.tensor
        def _(pe):
            pe.sem_inc(S["down"], 2)
            pe.sem_inc(S["up"], 2 * chunks)
            pe.sem_inc(S["turned"], 2)
            with pe.Fori(0, trips(pe)) as i:
                for j in range(2):
                    t = 2 * i + j
                    pe.wait_ge(s_gathered[j], 32 * i + 32)
                    pe.wait_ge(S["x"], t + 1)
                    for c in range(2):
                        for h in range(2):
                            last = nc.tensor.transpose(m.psum[0:P, 4 + j, c * TILE + h * HALF:c * TILE + h * HALF + HALF],
                                                       s[f"gathered{j}"][:, h, c * P:c * P + P],
                                                       m.identity[0:P, 0:P])
                    last.then_inc(S["turned"], 1)
                for j in range(2):
                    t = 2 * i + j
                    pe.wait_ge(S["x"], t + 3)
                    pe.wait_ge(s_weights[j], loads * i + loads)
                    for k in range(chunks):
                        pe.wait_ge(S["hidden"], chunks * t + k + 1)
                        for q, wt in enumerate((wb[f"wg{j}"], wb[f"wu{j}"])):
                            for c in range(2):
                                last = nc.tensor.matmul(m.psum[0:chunk, (j * chunks + k) % 4, q * TILE:q * TILE + TILE],
                                                        wt[:, c, k * chunk:k * chunk + chunk], s[f"x{j}"][:, c, :],
                                                        start=c == 0, stop=c == 1)
                        last.then_inc(S["up"], 1)
                for j in range(2):
                    t = 2 * i + j
                    pe.wait_ge(S["hidden"], chunks * t + chunks + 4)
                    pe.wait_ge(S["y"], t + 1)
                    pe.wait_ge(s_down_weights[j], 16 * i + 16)
                    for h in range(2):
                        for k in range(chunks):
                            last = nc.tensor.matmul(m.psum[0:P, 6 + j, h * D:h * D + D],
                                                    s[f"hidden{j}"][:, k, h * HALF:h * HALF + HALF],
                                                    wb[f"wd{j}"][:, k, :], start=k == 0, stop=k == chunks - 1)
                    last.then_inc(S["down"], 1)

        @block.scalar
        def _(act):
            nc.scalar.preload_act_table_set(SILU)
            act.sem_inc(S["x"], 2)
            act.sem_inc(S["y"], 2)
            for j in range(2):
                act.sem_inc(s_stored[j], 16)
            n = trips(act)
            with act.Fori(0, n) as i:
                for j in range(2):
                    t = 2 * i + j
                    act.wait_ge(S["turned"], t + 3)
                    act.wait_ge(S["down"], t + 1)
                    act.wait_ge(s_weights[j], loads * i + loads)
                    for c in range(2):
                        last = nc.scalar.activation(s[f"x{j}"][:, c, :], m.psum[0:P, 4 + j, c * TILE:c * TILE + TILE],
                                                    ACT.Copy if scale is None else ACT.Identity,
                                                    **({} if scale is None else {"scale": s[f"scale{j}"][:, c:c + 1]}))
                    last.then_inc(S["x"], 1)
                for j in range(2):
                    t = 2 * i + j
                    for k in range(chunks):
                        nth = j * chunks + k
                        act.wait_ge(S["up"], chunks * t + k + 1 + 2 * chunks)
                        act.wait_ge(S["hidden"], chunks * t + k + 3)
                        nc.scalar.activation(s[f"silu{nth % 2}"], m.psum[0:chunk, nth % 4, 0:TILE], ACT.Silu
                                             ).then_inc(S["silu"], 1)
                for j in range(2):
                    t = 2 * i + j
                    at = first_slot(act, t)
                    act.wait_ge(S["down"], t + 3)
                    act.wait_ge(s_stored[j], 16 * i + 16)
                    nc.scalar.activation(s[f"y{j}"], m.psum[0:P, 6 + j, 0:2 * D].rearrange("p (h d) -> p h d", h=2),
                                         ACT.Copy).then_inc(S["y"], 1)
                    act.wait_ge(S["y"], t + 3)
                    act.dma_start(y_rows[bass.ds(at, TILE), :].rearrange("(p h) d -> p h d", h=2), s[f"y{j}"]
                                  ).then_inc(s_stored[j], 16)
            for j in range(2):
                act.wait_ge(s_stored[j], 16 * n + 16)
            own_wait(act, S["act_turn"])

        @block.vector
        def _(dve):
            dve.sem_inc(S["hidden"], 4)
            with dve.Fori(0, trips(dve)) as i:
                for j in range(2):
                    t = 2 * i + j
                    dve.wait_ge(S["down"], t + 1)
                    for k in range(chunks):
                        nth = j * chunks + k
                        dve.wait_ge(S["silu"], chunks * t + k + 1)
                        nc.vector.tensor_tensor(s[f"hidden{j}"][:, k, :], s[f"silu{nth % 2}"],
                                                m.psum[0:chunk, nth % 4, TILE:2 * TILE], ALU.mult
                                                ).then_inc(S["hidden"], 1)
    finish(nc, sems)


def combine_block(nc, m, load, name, r, y_rows, h, out=None):
    K = r.picks
    s = carve(m.scratch[:], {f"{k}{j}": v for j in range(2) for k, v in (
        ("slots", (128, (K,), U32)), ("weights", (128, (K,), F32)), ("gathered", (128, (K, D), F32)),
        ("sum", (128, (D,), F32)), ("h", (P, (2, ROWS), F32)))})
    names = ("pool_turn", "staged", "gathered0", "gathered1", "weights", "sum", "copied", "turned", "added", "stored0", "stored1")
    sems = signals(nc, name, *names)
    S = dict(zip(names, sems))
    s_gathered, s_stored = (S["gathered0"], S["gathered1"]), (S["stored0"], S["stored1"])
    row = lambda a, t: a[:, bass.ds(t, 1), :].rearrange("p a k -> p (a k)")
    with nc.Block() as block:
        @block.sync
        def _(sp):
            load(sp)
            if out is not None:
                with sp.Fori(0, RT // 2) as i:
                    for j in range(2):
                        sp.wait_ge(S["added"], 2 * i + j + 3)
                        sp.dma_start(out[bass.ds((2 * i + j) * ROWS, ROWS), :], s[f"sum{j}"]).then_inc(s_stored[j], 16)
                for j in range(2):
                    sp.wait_ge(s_stored[j], 16 * (RT // 2) + 16)

        @block.gpsimd
        def _(pool):
            with pool.Fori(0, RT // 2) as i:
                for j in range(2):
                    t = 2 * i + j
                    pool.wait_ge(S["sum"], K * t + K)
                    nc.gpsimd.tensor_copy(s[f"slots{j}"], row(r.slot, t)).then_inc(S["staged"], 1)
                    pool.wait_ge(S["staged"], t + 1)
                    own_wait(pool, S["pool_turn"])
                    for k in range(K):
                        nc.gpsimd.indirect_dma_start(
                            out=s[f"gathered{j}"][:, k, :], out_offset=None, in_=y_rows,
                            in_offset=bass.IndirectOffsetOnAxis(ap=s[f"slots{j}"][:, k:k + 1], axis=0)
                        ).then_inc(s_gathered[j], 16)
                    if out is not None:
                        pool.wait_ge(S["turned"], t + 1)
                        nc.gpsimd.tensor_copy(s[f"h{j}"], h[:, :, span(t, ROWS)]).then_inc(S["copied"], 1)

        @block.tensor
        def _(pe):
            pe.sem_inc(S["turned"], 2)
            with pe.Fori(0, RT // 2) as i:
                for j in range(2):
                    t = 2 * i + j
                    pe.wait_ge(S["added"], t + 1)
                    if out is None:
                        pe.wait_ge(S["sum"], K * t + 3 * K)
                        for c in range(2):
                            last = nc.tensor.transpose(m.psum[0:P, j, c * ROWS:c * ROWS + ROWS],
                                                       s[f"sum{j}"][:, c * P:c * P + P], m.identity[:])
                    else:
                        pe.wait_ge(S["copied"], t + 1)
                        for c in range(2):
                            last = nc.tensor.transpose(m.psum[:, j, c * P:c * P + P], s[f"h{j}"][:, c, :],
                                                       m.identity[0:P, 0:P])
                    last.then_inc(S["turned"], 1)

        @block.vector
        def _(dve):
            dve.sem_inc(S["sum"], 2 * K)
            dve.sem_inc(S["added"], 2)
            for j in range(2):
                dve.sem_inc(s_stored[j], 16)
            with dve.Fori(0, RT // 2) as i:
                for j in range(2):
                    t = 2 * i + j
                    dve.wait_ge(S["sum"], K * t + K)
                    nc.vector.tensor_copy(s[f"weights{j}"], row(r.weight, t)).then_inc(S["weights"], 1)
                    dve.wait_ge(S["weights"], t + 1)
                    dve.wait_ge(s_gathered[j], 16 * K * i + 16 * K)
                    if out is None:
                        dve.wait_ge(S["turned"], t + 1)
                    else:
                        dve.wait_ge(s_stored[j], 16 * i + 16)
                    for k in range(K):
                        g, wt = s[f"gathered{j}"][:, k, :], s[f"weights{j}"][:, k:k + 1]
                        if k == 0:
                            ins = nc.vector.tensor_scalar(s[f"sum{j}"], g, wt, None, ALU.mult)
                        else:
                            dve.wait_ge(S["sum"], K * t + 2 * K + k)
                            ins = nc.vector.scalar_tensor_tensor(out=s[f"sum{j}"], in0=g, scalar=wt, in1=s[f"sum{j}"],
                                                                 op0=ALU.mult, op1=ALU.add)
                        ins.then_inc(S["sum"], 1)
                for j in range(2):
                    t = 2 * i + j
                    dve.wait_ge(S["turned"], t + 3)
                    if out is None:
                        d = h[:, :, span(t, ROWS)]
                        nc.vector.tensor_tensor(d, m.psum[0:P, j, 0:2 * ROWS].rearrange("p (c t) -> p c t", c=2), d,
                                                ALU.add).then_inc(S["added"], 1)
                    else:
                        dve.wait_ge(S["sum"], K * t + 3 * K)
                        nc.vector.tensor_tensor(s[f"sum{j}"], s[f"sum{j}"], m.psum[:, j, 0:D], ALU.add
                                                ).then_inc(S["added"], 1)
    finish(nc, sems)



def program(nc, a, out):
    with ExitStack() as ctx:
        m = Memory(nc, ctx)
        blocks = []

        def stage(weights, block):
            blocks.append((weights, block))

        ln = lambda name, src, dst, **k: stage({}, lambda w, load: norm_block(nc, m, name, load, src, dst, 1e-5, **k))
        x0, x = m.act(0), m.act(2)

        def dram(name, shape, dt=F32):
            return nc.dram_tensor(name, shape, dt).ap()

        def matrix(name, parts, *shape, dt=F32):
            return {name.split("_", 2)[-1]: (parts, shape, dt, a[name])}

        def add_bias_and(dst, bias, n):
            return lambda dve, c, g, product: nc.vector.scalar_tensor_tensor(
                out=dst[:, c, span(g, n)], in0=product, scalar=bias[:, c:c + 1], in1=dst[:, c, span(g, n)],
                op0=ALU.add, op1=ALU.add)

        stage({"W": (128, (6, D), F32, a["tok_W"]), "b": (P, (2,), F32, a["tok_b"]),
               "pos": (P, (2, L), F32, a["tok_pos"])},
              lambda w, load: patch_block(nc, m, w, load, a["patches"]))

        ln("ln0a", m.h, x)
        stage({"Wqk": (P, (2, 128), F32, a["a0_Wqk"]), "Wff": (P, (2, 128), F32, a["a0_Wff"]),
               "Wv": (P, (2, D), F32, a["a0_Wv"]), "bf": (128, (1,), F32, a["a0_bf"]),
               "sign": (128, (1,), F32, a["c_sign"]), "carry": (128, (N,), F32, a["c_carry"]),
               "causal": (PAIR, (PAIR,), F32, a["c_causal"])},
              lambda w, load: decay_attention_block(nc, m, w, load, x, m.act(4)))
        stage({"gamma": (P, (2,), F32, a["a0_gamma"]), "beta": (P, (2,), F32, a["a0_beta"])},
              lambda w, load: norm_block(nc, m, "ln0h", load, m.act(4), m.act(4), 1e-5,
                                         gamma=w["gamma"], beta=w["beta"]))
        stage({"Wo": (P, (2, D), F32, a["a0_Wo"])},
              lambda w, load: project_block(nc, m, "out0", load, m.act(4), w["Wo"], m.h))

        f = "f0_"
        mask_rows = m.full[0:2, 10, :]
        ln("ln0b", m.h, x0)
        stage({"gamma": (P, (2,), F32, a[f + "g1"]), "beta": (P, (2,), F32, a[f + "b1"])},
              lambda w, load: norm_block(nc, m, "ln0f", load, x0, x, 1e-5, gamma=w["gamma"], beta=w["beta"]))
        stage({"Wr": (P, (2,), F32, a[f + "Wr"]), "br": (P, (1,), F32, a[f + "br"].broadcast_to([P, 1])),
               "before": (B, (L, L), F32, a["c_before"].broadcast_to([B, L * L])
                          .rearrange("p (a b) -> p a b", a=L))},
              lambda w, load: mix_block(nc, m, w, load, x, m.act(4), m.act(6), m.full[0:P, 8, :],
                                        m.full[0:P, 9, :], mask_rows, dram("score_rows", (1, T)),
                                        dram("mask_dram", (2, T))))
        stage({**{k: (P, (2, D), F32, a[f + k]) for k in ("Wq", "Wk", "Wv", "Wo", "Wm")},
               **{k: (P, (2,), F32, a[f + k]) for k in ("bq", "bk", "bv")},
               "bom": (2, (D,), F32, a[f + "bom"]), "head": (P, (6,), F32, a["c_head"]),
               "rows": (3 * L, (2, P), F32, a["c_rows"])},
              lambda w, load: softmax_attention_block(nc, m, w, load, x, x0, m.act(4), m.full[0:P, 9, :],
                                                      mask_rows, m.act(6)))
        stage({"gamma": (P, (2,), F32, a[f + "g2"]), "beta": (P, (2,), F32, a[f + "b2"])},
              lambda w, load: norm_block(nc, m, "ln0g", load, m.act(6), x, 1e-5, gamma=w["gamma"],
                                         beta=w["beta"]))

        def layer0_mlp(w, load):
            def evacuate(dve, c, g, product):
                y = m.act(6)[:, c, span(g, WIDE)]
                return nc.vector.scalar_tensor_tensor(out=y, in0=product, scalar=w["bf2"][:, c:c + 1],
                                                      in1=y, op0=ALU.add, op1=ALU.add)
            mlp_block(nc, m, "mlp0", load, x, w["W1"], w["bf1"], w["W2"], evacuate, ACT.Gelu)

        stage({"W1": (P, (2, HID), F32, a[f + "W1"]), "bf1": (128, (6,), F32, a[f + "bf1"]),
               "W2": (128, (6, D), F32, a[f + "W2"]), "bf2": (P, (2,), F32, a[f + "bf2"])}, layer0_mlp)
        stage({}, lambda w, load: add_block(nc, m, "add0", load, m.act(6), m.h))

        coef, rates = m.coef[:], m.rates[:, 0:24]
        ln("ln1a", m.h, x)
        stage({"Wd": (P, (2, 256), F32, a["a1_Wd"]), "WBC": (P, (2, 32), F32, a["a1_WBC"]),
               "bd": (128, (2,), F32, a["a1_bd"]), "loglam": (128, (24,), F32, a["a1_loglam"])},
              lambda w, load: rates_block(nc, m, w, load, x, m.act(4, 2, 128), coef, rates))
        stage({"Wout": (128, (24, D), F32, a["a1_Wout"]), "bout": (P, (2,), F32, a["a1_bout"]),
               "pick": (96, (32,), F32, a["c_pick"])},
              lambda w, load: scan_block(nc, m, w, load, m.act(4, 2, 128), coef, rates))

        gates = m.full[0:P, 9, 0:3 * B]
        ln("ln1b", m.h, x)
        stage({"Wg": (P, (2, 3), F32, a["f1_Wg"])},
              lambda w, load: image_gate_block(nc, m, w, load, x, gates, dram("image_gates", (3, B))))
        for e in range(3):
            def expert(w, load, e=e):
                def evacuate(dve, c, g, product):
                    h = m.h[:, c, span(g, N)]
                    return nc.vector.tensor_tensor(h, product, h, ALU.add)
                mlp_block(nc, m, f"expert{e}", load, x, w["W1"], w["b1"], w["W2"], evacuate, ACT.Gelu, n=N,
                          scale=(w["b2"], gates[:, e * B:e * B + B]))
            stage({"W1": (P, (2, HID), F32, a["f1_W1"][e]), "b1": (128, (6,), F32, a["f1_b1"][e]),
                   "W2": (128, (6, D), F32, a["f1_W2"][e]), "b2": (P, (2,), F32, a["f1_b2"][e])}, expert)

        ln("ln2a", m.h, x)
        stage({"Wqkv": (P, (2, 3 * D), F32, a["a2_Wqkv"]), "bqk": (P, (4,), F32, a["a2_bqk"]),
               "bv": (PAIR, (D,), F32, a["a2_bv"].broadcast_to([PAIR, D])),
               "decay": (PAIR, (PAIR,), F32, a["c_decay"])},
              lambda w, load: retention_block(nc, m, w, load, x))

        hidden = m.full[0:24, 9, :]
        ln("ln2b", m.h, x)
        stage({"router": (P, (2, 3), F32, a["f2_router_w"]), "router_b": (3, (1,), F32, a["f2_router_b"]),
               "down": (P, (2, 24), F32, a["f2_down"])},
              lambda w, load: adapter_block(nc, m, w, load, x, m.full[0:3, 8, :], hidden, m.full[0:24, 10, :],
                                            dram("adapter_logits", (3, T)), dram("adapter_gates", (3, T))))

        def layer2_mlp(w, load):
            mlp_block(nc, m, "mlp2", load, x, w["w1"], w["b1"], w["w2"], add_bias_and(m.h, w["b2"], WIDE),
                      ACT.Gelu, extra=(w["up"], hidden))

        stage({"w1": (P, (2, HID), F32, a["f2_w1"]), "b1": (128, (6,), F32, a["f2_b1"]),
               "w2": (128, (6, D), F32, a["f2_w2"]), "b2": (P, (2,), F32, a["f2_b2"]),
               "up": (24, (D,), F32, a["f2_up"])}, layer2_mlp)

        xc, gate, dt = m.full[:, 5:8, :], m.full[:, 8:11, :], m.full[:, 2:5, :]
        coef3 = m.coef[0:96, :]
        rates3 = m.rates[:].rearrange("p (c n) -> p c n", n=STATES)
        ln("ln3a", m.h, x0)
        stage({"gamma": (P, (2,), F32, a["a3_g_mamba"])},
              lambda w, load: norm_block(nc, m, "rms3a", load, x0, x, 1e-6, centre=False, gamma=w["gamma"]))
        stage({"Win": (P, (2, 2 * DI), F32, a["a3_w_in"]), "conv_w": (128, (3, 4), F32, a["a3_conv_w"]),
               "conv_b": (128, (3,), F32, a["a3_conv_b"])},
              lambda w, load: mamba_input_block(nc, m, w, load, x, xc, gate))
        stage({"xproj": (128, (3, 33), F32, a["a3_w_xproj"]), "w_dt": (1, (DI,), F32, a["a3_w_dt"]),
               "b_dt": (128, (3,), F32, a["a3_b_dt"]), "A_log": (128, (3, STATES), F32, a["a3_A_log"])},
              lambda w, load: mamba_rates_block(nc, m, w, load, xc, dt, coef3, rates3))
        stage({"Wout": (128, (3, D), F32, a["a3_w_out"]), "D": (128, (3,), F32, a["a3_D_skip"]),
               "pick": (96, (32,), F32, a["c_pick"])},
              lambda w, load: mamba_scan_block(nc, m, w, load, xc, gate, dt, coef3, rates3, x0))
        stage({}, lambda w, load: add_block(nc, m, "addm", load, x0, m.h))
        r3 = Routing(m, E1, K1, STRIDE1, T, 32, False, 1.0)
        rows3, tokens3 = dram("rows3", (T, D)), dram("tokens3", (r3.slots, 1), U32)
        y3 = dram("y3", (r3.slots, D))
        m.zeroing(tokens3, 1)
        m.zeroing(y3, D)
        stage({}, lambda w, load: norm_block(nc, m, "rms3b", load, x0, x, 1e-6, centre=False))
        stage({"router": (P, (2, E1), F32, a["a3_w_router"]), "gamma": (P, (2,), F32, a["a3_g_moe"]),
               **route_constants(a, r3)},
              lambda w, load: route_block(nc, m, w, load, "route3", x, r3, rows3, tokens3, y3))
        stage({}, lambda w, load: scatter_block(nc, m, "scatter3", load, r3, tokens3))
        stage({}, lambda w, load: expert_block(nc, m, load, "experts3", r3, rows3, tokens3, y3, a["a3_w1"],
                                               a["a3_w3"], a["a3_w2"], 128, HID // 128, a["a3_g_exp"]))
        stage({}, lambda w, load: combine_block(nc, m, load, "combine3", r3, y3, m.h))

        r4 = Routing(m, E2, K2, STRIDE2, STRIDE2, E2 + 2, True, 2.5)
        rows4, tokens4 = dram("rows4", (T, D)), dram("tokens4", (r4.slots, 1), U32)
        y4 = dram("y4", (r4.slots, D))
        m.zeroing(tokens4, 1)
        m.zeroing(y4, D)
        ln("ln3b", m.h, x)
        stage({"router": (P, (2, E2), F32, a["f3_Wg"]), "bias": (128, (E2,), F32, a["f3_e_bias"].broadcast_to([128, E2])),
               **route_constants(a, r4)},
              lambda w, load: route_block(nc, m, w, load, "route4", x, r4, rows4, tokens4, y4))
        flat = lambda t: t.rearrange("p a t -> p (a t)")
        sums = flat(m.full[:, 4:6, :])[:, 0:RT * D].rearrange("p (t d) -> p t d", d=D)
        gathered = [flat(m.full[:, 6 + j:7 + j, :])[:, 0:K2 * D].rearrange("p (k d) -> p k d", d=D)
                    for j in range(2)]
        sides = (lambda: Scatter(nc, m, "scatter4", r4, tokens4, m.scratch[:, 8192:8256]),
                 lambda: Gather(nc, "gather4", r4, y4, sums, gathered, m.scratch[:, 8192:9216]))

        def shared(part):
            n, chunks = SHARED // 2, 4
            return ({"Wsg": (P, (2, n), F32, a["f3_Wsg"][:, :, part * n:part * n + n]),
                     "Wsu": (P, (2, n), F32, a["f3_Wsu"][:, :, part * n:part * n + n]),
                     "Wsd": (n // chunks, (chunks, D), F32, a["f3_Wsd"][:, chunks * part:chunks * part + chunks, :])},
                    lambda w, load: gated_block(nc, m, f"shared{part}", load, x, w["Wsg"], w["Wsu"], w["Wsd"],
                                                n // chunks, chunks, sides[part]()))

        stage(*shared(0))
        stage({}, lambda w, load: expert_block(nc, m, load, "experts4", r4, rows4, tokens4, y4, a["f3_Wgate"],
                                               a["f3_Wup"], a["f3_Wdown"], 116, F2 // 116))
        stage(*shared(1))
        stage({}, lambda w, load: output_block(nc, m, "output", load, sums, m.h, out))

        share = -(-len(m.fills) // 14)
        m.all_filled = 16 * len(m.fills)
        placed = [carve(m.half[k % 2][:], {n: s[:3] for n, s in weights.items()})
                  for k, (weights, _) in enumerate(blocks)]

        def loader(k):
            def load(sp):
                for table, words in m.fills[(k - 1) * share:k * share] if k else []:
                    sp.dma_start(table, words).then_inc(m.filled, 16)
                if k < len(blocks):
                    for name, (_, _, _, source) in blocks[k][0].items():
                        sp.dma_start(placed[k][name], source).then_inc(m.arrived[k % 2], 16)
            return load

        def first_load(sp):
            loader(0)(sp)
            sp.dma_start(m.identity[:], a["c_identity"]).then_inc(m.setup, 16)
            sp.wait_ge(m.setup, 16)
        start_block(nc, m, first_load)
        dues = [0, 0]
        for k, (weights, block) in enumerate(blocks):
            dues[k % 2] += 16 * len(weights)
            m.loaded, m.due = m.arrived[k % 2], dues[k % 2]
            block(placed[k], loader(k + 1))


def route_constants(a, r):
    R = r.stride // TILE
    return {"before": (128, (128,), F32, a["c_tokens_before"]), "upto": (128, (128,), F32, a["c_upto"]),
            "iota": (128, (r.experts,), F32, a["c_numbers"][:, 0:r.experts].broadcast_to([128, r.experts])),
            "numbers": (128, (r.steps,), F32, a["c_numbers"][:, 0:r.steps].broadcast_to([128, r.steps])),
            "starts": (128, (R,), F32, a["c_starts"][:, 0:R].broadcast_to([128, R])),
            "spill": (128, (RT, r.picks), F32, a[f"c_spill{r.experts}"])}


def add_block(nc, m, name, load, x, dst):
    with nc.Block() as block:
        @block.sync
        def _(sp):
            load(sp)

        @block.vector
        def _(dve):
            nc.vector.tensor_tensor(dst[:, 0, :], x[:, 0, :], dst[:, 0, :], ALU.add)

        @block.gpsimd
        def _(pool):
            nc.gpsimd.tensor_tensor(dst[:, 1, :], x[:, 1, :], dst[:, 1, :], ALU.add)



def layout(v):
    f32 = lambda x: np.ascontiguousarray(x, dtype=np.float32)
    rows = lambda x, k=2: f32(x.reshape(k, x.shape[0] // k, -1).transpose(1, 0, 2))
    col = lambda x, k=2: f32(x.reshape(k, -1).T)
    o = {}
    x = v["x"].reshape(B, 3, 6, 16, 6, 16).transpose(0, 2, 4, 1, 3, 5).reshape(GROUPS, N, PD // 128, 128)
    o["patches"] = f32(x.transpose(0, 3, 2, 1))
    o["tok_W"] = rows(v["L0_tok_W"].reshape(D, PD).T, PD // 128)
    o["tok_b"] = col(v["L0_tok_b"])
    i = np.arange(L, dtype=np.float32)[:, None]
    j = np.arange(D)
    angle = i / np.power(np.float32(10000.0), (2 * (j // 2)).astype(np.float32) / np.float32(D))
    angle = angle + np.where(j % 2 == 1, np.float32(np.pi / 2), np.float32(0))
    o["tok_pos"] = f32(np.sin(angle).astype(np.float32).T.reshape(2, P, L).transpose(1, 0, 2))
    t, u = np.arange(PAIR)[:, None], np.arange(PAIR)[None, :]
    o["c_causal"] = f32((t // L == u // L) & (t <= u))
    o["c_sign"] = f32(np.where(np.arange(128) < 64, -1, 1)[:, None])
    o["c_carry"] = f32(np.broadcast_to(np.arange(N) % L != 0, (128, N)))
    a, b = np.arange(L)[:, None], np.arange(L)[None, :]
    o["c_before"] = f32(b < a).reshape(1, L * L)
    o["c_head"] = f32(np.arange(P)[:, None] // DH == np.arange(6)[None, :])
    r, q, f = np.arange(3 * L)[:, None, None] // L, np.arange(2)[None, :, None], np.arange(P)[None, None, :]
    o["c_rows"] = f32(f // DH == 3 * q + r)
    o["c_identity"] = f32(np.eye(128))
    A = "L0_attn_"
    o["a0_Wqk"] = rows(np.concatenate([v[A + "Wq"], v[A + "Wk"]], 1))
    o["a0_Wff"] = rows(np.concatenate([v[A + "Wf"], v[A + "Wf"]], 1))
    o["a0_Wv"], o["a0_Wo"] = rows(v[A + "Wv"]), rows(v[A + "Wo"])
    o["a0_bf"] = f32(np.concatenate([v[A + "bf"], v[A + "bf"]])[:, None])
    o["a0_gamma"], o["a0_beta"] = col(v[A + "gamma"]), col(v[A + "beta"])
    A = "L0_ffn_"
    for k in ("Wq", "Wk", "Wv", "Wo", "Wm", "W1"):
        o["f0_" + k] = rows(v[A + k])
    for k in ("g1", "b1", "g2", "b2", "Wr", "bq", "bk", "bv", "bf2"):
        o["f0_" + k] = col(v[A + k])
    o["f0_br"] = f32(v[A + "br"].reshape(1, 1))
    o["f0_bom"] = f32(np.stack([v[A + "bo"], v[A + "bm"]]))
    o["f0_bf1"], o["f0_W2"] = col(v[A + "bf1"], 6), rows(v[A + "W2"], 6)
    A = "L1_attn_"
    twice = lambda x: np.concatenate([x[0:128], x[128:D], x[128:D]])
    o["a1_Wd"], o["a1_bd"] = rows(twice(v[A + "Wd"]).T), col(twice(v[A + "bd"]))
    o["a1_WBC"] = rows(np.concatenate([v[A + "WB"], v[A + "WC"]]).T)

    def by_chunk(x):
        tail = x[128:D].reshape(64, 8, 2, *x.shape[2:]).swapaxes(1, 2).swapaxes(0, 1)
        return f32(np.concatenate([x[0:128], tail.reshape(128, 8, *x.shape[2:])], 1))

    o["a1_loglam"] = by_chunk(v[A + "log_lambda"])
    o["a1_Wout"] = by_chunk(v[A + "Wout"].T.reshape(D, STATES, D))
    o["a1_bout"] = col(v[A + "bout"])
    k, n = np.arange(96)[:, None] % 32, np.arange(32)[None, :]
    o["c_pick"] = f32(k == n)
    A = "L1_ffn_"
    o["f1_Wg"] = rows(v[A + "Wg"].T)
    for key, cut, k in (("W1", rows, 2), ("W2", rows, 6), ("b1", col, 6), ("b2", col, 2)):
        o["f1_" + key] = f32(np.stack([cut(v[A + key][e], k) for e in range(3)]))
    A = "L2_attn_"
    o["a2_Wqkv"] = rows(v[A + "W_qkv"].T)
    o["a2_bqk"] = col(v[A + "b_qkv"][0:2 * D], 4)
    o["a2_bv"] = f32(v[A + "b_qkv"][None, 2 * D:])
    o["c_decay"] = f32(np.where((t // L == u // L) & (t <= u), 0.99 ** np.maximum(u - t, 0), 0) / np.sqrt(D))
    A = "L2_ffn_"
    o["f2_w1"], o["f2_b1"] = rows(v[A + "w1"]), col(v[A + "b1"], 6)
    o["f2_w2"], o["f2_b2"] = rows(v[A + "w2"], 6), col(v[A + "b2"])
    o["f2_router_w"], o["f2_router_b"] = rows(v[A + "router_w"]), f32(v[A + "router_b"][:, None])
    o["f2_down"] = rows(v[A + "w_down"].transpose(1, 0, 2).reshape(D, 24))
    o["f2_up"] = f32(v[A + "w_up"].reshape(24, D))
    A = "L3_attn_"
    for k in ("g_mamba", "g_moe"):
        o["a3_" + k] = col(v[A + k])
    for k in ("conv_b", "b_dt", "D_skip"):
        o["a3_" + k] = col(v[A + k], 3)
    for k in ("conv_w", "w_xproj", "A_log", "w_out"):
        o["a3_" + k] = rows(v[A + k], 3)
    o["a3_w_router"] = rows(v[A + "w_router"])
    per_expert = lambda x, k: f32(np.stack([rows(e, k) for e in x]))
    o["a3_w1"], o["a3_w3"], o["a3_w2"] = per_expert(v[A + "w1"], 2), per_expert(v[A + "w3"], 2), per_expert(v[A + "w2"], 6)
    o["a3_g_exp"] = f32(v[A + "g_exp"].reshape(E1, 2, P).transpose(0, 2, 1))
    A2 = "L3_ffn_"
    o["f3_Wg"], o["f3_e_bias"] = rows(v[A2 + "Wg"].T), f32(v[A2 + "e_bias"][None])
    o["f3_Wgate"], o["f3_Wup"] = (per_expert(v[A2 + "W_gate_up"][:, :, k * F2:k * F2 + F2], 2) for k in range(2))
    o["f3_Wdown"] = per_expert(v[A2 + "W_down"], 4)
    o["f3_Wsg"], o["f3_Wsu"], o["f3_Wsd"] = rows(v[A2 + "Wsg"]), rows(v[A2 + "Wsu"]), rows(v[A2 + "Wsd"], 8)
    q = np.arange(128)
    o["c_tokens_before"], o["c_upto"] = f32(q[:, None] < q[None, :]), f32(q[:, None] <= q[None, :])
    o["c_numbers"] = f32(np.arange(E2 + 2))[None]
    o["c_starts"] = f32(np.arange(STRIDE1 // TILE) * TILE)[None]
    for e, k, stride in ((E1, K1, STRIDE1), (E2, K2, STRIDE2)):
        tile, choice = np.arange(RT)[:, None], np.arange(k)[None, :]
        o[f"c_spill{e}"] = f32(e * stride + (12 * q[:, None, None] + tile % 2 * k + choice))
    o["a3_w_in"], o["a3_w_dt"] = rows(v[A + "w_in"]), f32(v[A + "w_dt"])
    return o

def kernel(**inputs):
    import concourse.bacc as bacc
    from concourse.bass_utils import run_bass_kernel_spmd

    arrays = layout({name: np.asarray(x) for name, x in inputs.items()})
    nc = bacc.Bacc("TRN2", target_bir_lowering=False, num_devices=1)
    dram = {name: nc.dram_tensor(name, x.shape, mybir.dt.from_np(x.dtype), kind="ExternalInput").ap()
            for name, x in arrays.items()}
    out = nc.dram_tensor("out", (T, D), F32, kind="ExternalOutput").ap()
    program(nc, dram, out)
    result = run_bass_kernel_spmd(nc, [arrays], core_ids=[0])
    return result.results[0]["out"].reshape(B, L, D)
```

```python
from contextlib import ExitStack

import numpy as np

import concourse.bass as bass
from concourse import mybir

F32 = mybir.dt.float32
BF16 = mybir.dt.bfloat16
I32 = mybir.dt.int32
U32 = mybir.dt.uint32
ALU = mybir.AluOpType
ACT = mybir.ActivationFunctionType
AXX = mybir.AxisListType.X
SILU, SIGMOID, GELU = "silu_and_others", "sigmoid_and_others", "gelu_and_others"
EXP = "exp_and_others"
LOG_EXP = "natural_log_exp_and_others"

B, L, D = 64, 36, 192
T = B * L
P = 96
GB = 8
N = GB * L
GROUPS = T // N
IMAGE_GROUPS = 10
WIDE = 384
PAIR = 2 * L
ROWS = 128
RT = T // ROWS
HEADS, DH = 12, 16
HID = 768
PD = 768
STATES = 16
DI = 384
TILE = 192
HALF = TILE // 2

E1, K1, STRIDE1 = 8, 2, T
E2, K2, STRIDE2 = 128, 6, 192
F2 = 464
SHARED = 928


def signals(nc, block, *names):
    return [nc.alloc_semaphore(f"{block}_{n}") for n in names]


def finish(nc, sems):
    nc.clear_and_free_semaphores(sems)
    nc.all_engine_barrier()


def own_wait(engine, turn):
    engine.sem_inc(turn, 1)


def span(g, n):
    return bass.ds(g * n, n)


class Memory:

    WEIGHTS = 4800

    def __init__(self, nc, ctx):
        self.nc, self.ctx = nc, ctx
        sb = lambda name, shape, dt=F32: ctx.enter_context(nc.sbuf_tensor(name, shape, dt))
        self.sb = sb
        self.h = sb("residual", [P, 2, T])
        self.full = sb("full", [128, 11, T])
        self.half = [sb(f"weights{n}", [128, self.WEIGHTS]) for n in range(2)]
        self.scratch = sb("scratch", [128, self.SCRATCH])
        self.psum = ctx.enter_context(nc.psum_tensor("psum", [128, 8, 512], F32))
        self.ones = sb("ones", [128, 128])
        self.mean = sb("mean_weights", [P, P])
        self.eps = sb("eps", [128, 2])
        self.identity = sb("identity", [128, 128])
        self.coef = sb("coef", [96, T], BF16)
        self.rates = sb("rates", [128, 3 * STATES])
        self.arrived = [nc.alloc_semaphore(f"weights_loaded{n}") for n in range(2)]
        self.setup = nc.alloc_semaphore("constants_set")
        self.zeros = sb("zeros", [128, self.FILL // 2])
        self.fills = []
        self.filled = nc.alloc_semaphore("tables_zeroed")

    FILL = 2304
    SCRATCH = 10496

    def zeroing(self, rows, words):
        parts = rows.rearrange("(n p b a) d -> n p b (a d)", p=128, b=2, a=self.FILL // words // 2)
        zeros = self.zeros[:].rearrange("p (b f) -> p b f", b=1).broadcast_to([128, 2, self.FILL // 2])
        if words == 1:
            zeros = zeros.bitcast(U32)
        self.fills += [(parts[n], zeros) for n in range(rows.shape[0] * words // (128 * self.FILL))]

    def act(self, first, n=2, parts=P):
        return self.full[0:parts, first:first + n, :]


def carve(base, specs):
    at, tiles = 0, {}
    for name, (parts, shape, dt) in specs.items():
        count = int(np.prod(shape))
        words = count if dt in (F32, I32, U32) else (count + 1) // 2
        flat = base[0:parts, at:at + words]
        if dt is not F32:
            flat = flat.bitcast(dt)
        names = " ".join(f"a{k}" for k in range(len(shape)))
        sizes = {f"a{k}": s for k, s in enumerate(shape)}
        tiles[name] = flat.rearrange(f"p ({names}) -> p {names}", **sizes) if len(shape) > 1 else flat
        at += words + (-words) % 8
    assert at <= base.shape[1], (at, base.shape)
    return tiles



class Routing:

    def __init__(self, m, experts, picks, stride, capacity, steps, sigmoid, factor):
        self.experts, self.picks, self.stride, self.capacity = experts, picks, stride, capacity
        self.steps, self.sigmoid, self.factor = steps, sigmoid, factor
        self.bias, self.scaled = sigmoid, not sigmoid
        self.slots = experts * stride + m.FILL * 128 // D
        self.token_slots = -(-(experts * T + TILE) // (m.FILL * 128)) * m.FILL * 128
        data = m.full[:, 10, :]
        self.weight = data[:, 0:RT * picks].rearrange("p (t k) -> p t k", k=picks)
        self.slot = data[:, 128:128 + RT * picks].bitcast(U32).rearrange("p (t k) -> p t k", k=picks)
        self.scatter = data[:, 640:640 + RT * picks].bitcast(U32).rearrange("p (t k) -> p t k", k=picks)
        self.ids = data[:, 768:768 + RT].bitcast(U32).rearrange("p (t a) -> p t a", a=1)
        self.table = data[0:1, 256:256 + 2 * steps + 1].bitcast(I32)


def start_block(nc, m, load):
    with nc.Block() as block:
        @block.vector
        def _(dve):
            nc.vector.memset(m.ones[:], 1.0)
            nc.vector.memset(m.mean[:], 1.0 / D)
            nc.vector.memset(m.eps[:, 0:1], 1e-5)
            nc.vector.memset(m.eps[:, 1:2], 1e-6)
            nc.vector.memset(m.psum[:], 0.0)
            nc.vector.memset(m.zeros[:], 0.0)

        @block.sync
        def _(sp):
            load(sp)


def norm_block(nc, m, name, load, src, dst, eps, centre=True, gamma=None, beta=None,
               twice=None, add_to=None):
    final = twice[0] if twice else dst
    n, steps, J = N, T // N, 4
    s = carve(m.scratch[:], {f"{k}{j}": v for j in range(J) for k, v in (
        ("centred", (P, (2, n), F32)), ("square", (P, (2, n), F32)), ("rstd", (P, (n,), F32)),
        ("var", (P, (n,), F32)), ("rstd2", (P, (n,), F32)))})
    mean = [m.psum[0:P, j, 0:n] for j in range(J)]
    var = [m.psum[0:P, J + j, 0:n] for j in range(J)]
    sems = signals(nc, name, "mean", "centred", "squared", "var", "log", "rstd", "scaled", "shifted", "ratio",
                   "log2", "rstd2", "first")
    s_mean, s_centred, s_squared, s_var, s_log, s_rstd, s_scaled, s_shifted, s_ratio, s_log2, s_rstd2, s_first = sems
    e = m.eps[0:P, 0:1] if eps == 1e-5 else m.eps[0:P, 1:2]
    with nc.Block() as block:
        @block.sync
        def _(sp):
            load(sp)

        @block.gpsimd
        def _(pool):
            if add_to is not None:
                nc.gpsimd.tensor_tensor(add_to, src, add_to, ALU.add)

        @block.tensor
        def _(pe):
            with pe.Fori(0, steps // J) as i:
                if centre:
                    for j in range(J):
                        g = J * i + j
                        for c in range(2):
                            last = nc.tensor.matmul(mean[j], m.mean[:], src[:, c, span(g, n)],
                                                    start=c == 0, stop=c == 1)
                        last.then_inc(s_mean, 1)
                for j in range(J):
                    pe.wait_ge(s_squared, J * i + j + 1)
                    for c in range(2):
                        last = nc.tensor.matmul(var[j], m.mean[:], s[f"square{j}"][:, c, :],
                                                start=c == 0, stop=c == 1)
                    last.then_inc(s_var, 1)

        @block.scalar
        def _(act):
            nc.scalar.preload_act_table_set(LOG_EXP)
            if gamma is not None:
                act.wait_ge(m.loaded, m.due)
            with act.Fori(0, steps // J) as i:
                for j in range(J):
                    g = J * i + j
                    if centre:
                        act.wait_ge(s_centred, g + 1)
                        x = s[f"centred{j}"]
                    else:
                        x = src[:, :, span(g, n)]
                    nc.scalar.activation(s[f"square{j}"], x, ACT.Square).then_inc(s_squared, 1)
                for j in range(J):
                    g = J * i + j
                    act.wait_ge(s_var, g + 1)
                    act.wait_ge(s_scaled, g + 1)
                    nc.scalar.activation(s[f"rstd{j}"], var[j], ACT.Ln, bias=e).then_inc(s_log, 1)
                    act.wait_ge(s_log, g + 1)
                    nc.scalar.activation(s[f"rstd{j}"], s[f"rstd{j}"], ACT.Exp, scale=-0.5).then_inc(s_rstd, 1)
                if twice:
                    e2 = m.eps[0:P, 0:1] if twice[1] == 1e-5 else m.eps[0:P, 1:2]
                    for j in range(J):
                        g = J * i + j
                        act.wait_ge(s_ratio, 2 * g + 2)
                        nc.scalar.activation(s[f"rstd2{j}"], s[f"var{j}"], ACT.Ln, bias=e2).then_inc(s_log2, 1)
                        act.wait_ge(s_log2, g + 1)
                        nc.scalar.activation(s[f"rstd2{j}"], s[f"rstd2{j}"], ACT.Exp, scale=-0.5).then_inc(s_rstd2, 1)
                if beta is not None:
                    for j in range(J):
                        g = J * i + j
                        act.wait_ge(s_scaled, g + J + 1)
                        for c in range(2):
                            nc.scalar.activation(final[:, c, span(g, n)], final[:, c, span(g, n)], ACT.Identity,
                                                 bias=beta[:, c:c + 1]).then_inc(s_shifted, 1)

        @block.vector
        def _(dve):
            if gamma is not None:
                dve.wait_ge(m.loaded, m.due)
            dve.sem_inc(s_scaled, J)
            with dve.Fori(0, steps // J) as i:
                if centre:
                    for j in range(J):
                        g = J * i + j
                        dve.wait_ge(s_mean, g + 1)
                        dve.wait_ge(s_scaled, g + 1)
                        nc.vector.tensor_tensor(s[f"centred{j}"], src[:, :, span(g, n)],
                                                m.psum[0:P, j:j + 1, 0:n].broadcast_to([P, 2, n]),
                                                ALU.subtract).then_inc(s_centred, 1)
                for j in range(J):
                    g = J * i + j
                    dve.wait_ge(s_rstd, g + 1)
                    if centre:
                        dve.wait_ge(s_centred, g + 1)
                    for c in range(2):
                        x = s[f"centred{j}"][:, c, :] if centre else src[:, c, span(g, n)]
                        if gamma is None or twice:
                            last = nc.vector.tensor_tensor(dst[:, c, span(g, n)], x, s[f"rstd{j}"], ALU.mult)
                        else:
                            last = nc.vector.scalar_tensor_tensor(
                                out=dst[:, c, span(g, n)], in0=x, scalar=gamma[:, c:c + 1],
                                in1=s[f"rstd{j}"], op0=ALU.mult, op1=ALU.mult)
                    if not twice:
                        last.then_inc(s_scaled, 1)
                    else:
                        last.then_inc(s_first, 1)
                        nc.vector.tensor_tensor(s[f"var{j}"], var[j], s[f"rstd{j}"], ALU.mult).then_inc(s_ratio, 1)
                        dve.wait_ge(s_ratio, 2 * g + 1)
                        nc.vector.tensor_tensor(s[f"var{j}"], s[f"var{j}"], s[f"rstd{j}"], ALU.mult
                                                ).then_inc(s_ratio, 1)
                if twice:
                    for j in range(J):
                        g = J * i + j
                        dve.wait_ge(s_rstd2, g + 1)
                        dve.wait_ge(s_first, g + 1)
                        for c in range(2):
                            last = nc.vector.scalar_tensor_tensor(
                                out=final[:, c, span(g, n)], in0=dst[:, c, span(g, n)], scalar=gamma[:, c:c + 1],
                                in1=s[f"rstd2{j}"], op0=ALU.mult, op1=ALU.mult)
                        last.then_inc(s_scaled, 1)
    finish(nc, sems)


def patch_block(nc, m, w, load, patches):
    s = carve(m.scratch[:], {f"patch{j}": (128, (PD // 128, N), F32) for j in range(2)})
    sems = signals(nc, "patch", "loaded0", "loaded1", "product", "evacuated")
    s_in, (s_prod, s_out) = sems[:2], sems[2:]
    with nc.Block() as block:
        @block.sync
        def _(sp):
            load(sp)
            with sp.Fori(0, GROUPS // 2) as i:
                for j in range(2):
                    g = 2 * i + j
                    sp.wait_ge(s_prod, 2 * g + 2)
                    sp.dma_start(s[f"patch{j}"], patches[g]).then_inc(s_in[j], 16)

        @block.tensor
        def _(pe):
            pe.sem_inc(s_prod, 4)
            pe.wait_ge(m.loaded, m.due)
            with pe.Fori(0, GROUPS // 2) as i:
                for j in range(2):
                    g = 2 * i + j
                    pe.wait_ge(s_in[j], 16 * i + 16)
                    pe.wait_ge(s_out, g + 1)
                    for c in range(2):
                        for k in range(PD // 128):
                            last = nc.tensor.matmul(m.psum[0:P, 2 * j + c, 0:N], w["W"][:, k, c * P:c * P + P],
                                                    s[f"patch{j}"][:, k, :], start=k == 0, stop=k == PD // 128 - 1)
                        last.then_inc(s_prod, 1)

        @block.vector
        def _(dve):
            dve.sem_inc(s_out, 2)
            dve.wait_ge(m.loaded, m.due)
            with dve.Fori(0, GROUPS // 2) as i:
                for j in range(2):
                    g = 2 * i + j
                    for c in range(2):
                        dve.wait_ge(s_prod, 2 * g + c + 5)
                        last = nc.vector.scalar_tensor_tensor(
                            out=m.h[:, c, span(g, N)].rearrange("p (b l) -> p b l", l=L),
                            in0=m.psum[0:P, 2 * j + c, 0:N].rearrange("p (b l) -> p b l", l=L),
                            scalar=w["b"][:, c:c + 1], in1=w["pos"][:, c:c + 1, :].broadcast_to([P, GB, L]),
                            op0=ALU.add, op1=ALU.add)
                    last.then_inc(s_out, 1)
    finish(nc, sems)


def mlp_block(nc, m, name, load, x, w1, b1, w2, evacuate, func, extra=None):
    n, chunks = WIDE, HID // 128
    s = carve(m.scratch[:], {f"hidden{j}": (128, (chunks, n), F32) for j in range(2)})
    sems = signals(nc, name, "up", "hidden", "down", "evacuated")
    s_up, s_hidden, s_down, s_out = sems
    up = lambda k: m.psum[:, k % 4, 0:n]
    with nc.Block() as block:
        @block.sync
        def _(sp):
            load(sp)

        @block.tensor
        def _(pe):
            pe.sem_inc(s_down, 4)
            pe.wait_ge(m.loaded, m.due)
            with pe.Fori(0, T // n // 2) as i:
                for j in range(2):
                    g = 2 * i + j
                    for k in range(chunks):
                        pe.wait_ge(s_hidden, chunks * g + k + 1)
                        for c in range(2):
                            last = nc.tensor.matmul(up(j * chunks + k), w1[:, c, k * 128:k * 128 + 128],
                                                    x[:, c, span(g, n)], start=c == 0, stop=c == 1)
                        last.then_inc(s_up, 1)
                for j in range(2):
                    g = 2 * i + j
                    pe.wait_ge(s_hidden, chunks * g + chunks + 4)
                    pe.wait_ge(s_out, 2 * g + 2)
                    for c in range(2):
                        out = m.psum[0:P, 4 + 2 * j + c, 0:n]
                        for k in range(chunks):
                            last = nc.tensor.matmul(out, w2[:, k, c * P:c * P + P], s[f"hidden{j}"][:, k, :],
                                                    start=k == 0, stop=k == chunks - 1 and extra is None)
                        if extra is not None:
                            last = nc.tensor.matmul(out, extra[0][:, c * P:c * P + P],
                                                    extra[1][:, span(g, n)], start=False, stop=True)
                        last.then_inc(s_down, 1)

        @block.scalar
        def _(act):
            nc.scalar.preload_act_table_set(GELU)
            act.sem_inc(s_hidden, 4)
            act.wait_ge(m.loaded, m.due)
            with act.Fori(0, T // n // 2) as i:
                for j in range(2):
                    g = 2 * i + j
                    act.wait_ge(s_down, 2 * g + 2)
                    for k in range(chunks):
                        act.wait_ge(s_up, chunks * g + k + 1)
                        nc.scalar.activation(s[f"hidden{j}"][:, k, :], up(j * chunks + k), func,
                                             bias=b1[:, k:k + 1]).then_inc(s_hidden, 1)

        @block.vector
        def _(dve):
            dve.sem_inc(s_out, 4)
            dve.wait_ge(m.loaded, m.due)
            with dve.Fori(0, T // n // 2) as i:
                for j in range(2):
                    g = 2 * i + j
                    for c in range(2):
                        dve.wait_ge(s_down, 2 * g + c + 5)
                        product = m.psum[0:P, 4 + 2 * j + c, 0:n]
                        evacuate(dve, c, g, product).then_inc(s_out, 1)
    finish(nc, sems)


def gated_block(nc, m, name, load, x, wg, wu, wd, chunk, chunks, side):
    n = WIDE
    s = carve(m.scratch[:], {f"hidden{j}": (chunk, (chunks, n), F32) for j in range(2)}
              | {f"silu{j}": (chunk, (n,), F32) for j in range(2)})
    sems = signals(nc, name, "up", "silu", "hidden", "down", "evacuated")
    s_up, s_silu, s_hidden, s_down, s_out = sems
    up = lambda k, q: m.psum[0:chunk, 2 * (k % 2) + q, 0:n]
    with nc.Block() as block:
        @block.sync
        def _(sp):
            load(sp)

        @block.gpsimd
        def _(pool):
            if side:
                side.gpsimd(pool)

        @block.tensor
        def _(pe):
            pe.sem_inc(s_down, 4)
            pe.wait_ge(m.loaded, m.due)
            with pe.Fori(0, T // n // 2) as i:
                for j in range(2):
                    g = 2 * i + j
                    for k in range(chunks):
                        pe.wait_ge(s_hidden, chunks * g + k + 1)
                        for q, w in enumerate((wg, wu)):
                            for c in range(2):
                                last = nc.tensor.matmul(up(j * chunks + k, q), w[:, c, k * chunk:k * chunk + chunk],
                                                        x[:, c, span(g, n)], start=c == 0, stop=c == 1)
                        last.then_inc(s_up, 1)
                for j in range(2):
                    g = 2 * i + j
                    pe.wait_ge(s_hidden, chunks * g + chunks + 2)
                    pe.wait_ge(s_out, 2 * g + 2)
                    for c in range(2):
                        for k in range(chunks):
                            last = nc.tensor.matmul(m.psum[0:P, 4 + 2 * j + c, 0:n], wd[:, k, c * P:c * P + P],
                                                    s[f"hidden{j}"][:, k, :], start=k == 0, stop=k == chunks - 1)
                        last.then_inc(s_down, 1)

        @block.scalar
        def _(act):
            nc.scalar.preload_act_table_set(SILU)
            with act.Fori(0, T // n // 2) as i:
                for j in range(2):
                    g = 2 * i + j
                    for k in range(chunks):
                        act.wait_ge(s_up, chunks * g + k + 1)
                        act.wait_ge(s_hidden, chunks * g + k + 1)
                        nc.scalar.activation(s[f"silu{(j * chunks + k) % 2}"], up(j * chunks + k, 0),
                                             ACT.Silu).then_inc(s_silu, 1)

        @block.vector
        def _(dve):
            dve.sem_inc(s_out, 4)
            dve.sem_inc(s_hidden, 2)
            with dve.Fori(0, T // n // 2) as i:
                for j in range(2):
                    g = 2 * i + j
                    dve.wait_ge(s_down, 2 * g + 2)
                    for k in range(chunks):
                        dve.wait_ge(s_silu, chunks * g + k + 1)
                        nc.vector.tensor_tensor(s[f"hidden{j}"][:, k, :], s[f"silu{(j * chunks + k) % 2}"],
                                                up(j * chunks + k, 1), ALU.mult).then_inc(s_hidden, 1)
                for j in range(2):
                    g = 2 * i + j
                    for c in range(2):
                        dve.wait_ge(s_down, 2 * g + c + 5)
                        h = m.h[:, c, span(g, n)]
                        nc.vector.tensor_tensor(h, m.psum[0:P, 4 + 2 * j + c, 0:n], h, ALU.add).then_inc(s_out, 1)
                    if side:
                        side.vector(dve, i, j)
    finish(nc, sems + (side.sems if side else []))


def project_block(nc, m, name, load, x, w, dst):
    n = WIDE
    sems = signals(nc, name, "product", "evacuated")
    s_prod, s_out = sems
    with nc.Block() as block:
        @block.sync
        def _(sp):
            load(sp)

        @block.tensor
        def _(pe):
            pe.wait_ge(m.loaded, m.due)
            with pe.Fori(0, T // n // 2) as i:
                for j in range(2):
                    g = 2 * i + j
                    pe.wait_ge(s_out, 2 * g + 2)
                    for c in range(2):
                        for k in range(2):
                            last = nc.tensor.matmul(m.psum[0:P, 2 * j + c, 0:n], w[:, k, c * P:c * P + P],
                                                    x[:, k, span(g, n)], start=k == 0, stop=k == 1)
                        last.then_inc(s_prod, 1)

        @block.vector
        def _(dve):
            dve.sem_inc(s_out, 4)
            with dve.Fori(0, T // n // 2) as i:
                for j in range(2):
                    g = 2 * i + j
                    for c in range(2):
                        dve.wait_ge(s_prod, 2 * g + c + 1)
                        d = dst[:, c, span(g, n)]
                        nc.vector.tensor_tensor(d, m.psum[0:P, 2 * j + c, 0:n], d, ALU.add).then_inc(s_out, 1)
    finish(nc, sems)


def decay_attention_block(nc, m, w, load, x, dst):
    F = (N,)
    s = carve(m.scratch[:], {f"{k}{j}": v for j in range(2) for k, v in (
        ("x", (P, (2, N), F32)), ("forget", (128, F, F32)), ("cum", (128, F, F32)),
        ("neg", (128, F, F32)), ("elu", (128, F, F32)), ("q", (64, F, F32)), ("k", (64, F, F32)),
        ("v", (PAIR, (4, D), F32)), ("score", (PAIR, (4, PAIR), F32)), ("den", (P, F, F32)))}
        | {"negb": (128, (1,), F32)})
    ps = lambda j, q: m.psum[:, 4 * j + q, :]
    names = ("copied", "products", "values", "v_copied", "e", "u", "log", "scan", "clip", "decay", "min", "exp",
             "elu", "qk", "scores", "masked", "sums", "den", "recip", "out", "negb")
    sems = signals(nc, "decay", *names)
    S = dict(zip(names, sems))
    r4 = lambda a, k: a.rearrange("p (a b) -> p a b", a=k)
    with nc.Block() as block:
        @block.sync
        def _(sp):
            load(sp)

        @block.gpsimd
        def _(pool):
            with pool.Fori(0, GROUPS // 2) as i:
                for j in range(2):
                    g = 2 * i + j
                    pool.wait_ge(S["values"], g + 1)
                    nc.gpsimd.tensor_copy(s[f"x{j}"], x[:, :, span(g, N)]).then_inc(S["copied"], 1)

        @block.tensor
        def _(pe):
            pe.sem_inc(S["values"], 2)
            pe.wait_ge(m.loaded, m.due)
            with pe.Fori(0, GROUPS // 2) as i:
                for j in range(2):
                    g = 2 * i + j
                    pe.wait_ge(S["out"], g + 1)
                    for q, wt in enumerate((w["Wqk"], w["Wff"])):
                        for c in range(2):
                            last = nc.tensor.matmul(ps(j, q)[:, 0:N], wt[:, c, :], x[:, c, span(g, N)],
                                                    start=c == 0, stop=c == 1)
                    last.then_inc(S["products"], 1)
                    pe.wait_ge(S["copied"], g + 1)
                    for p in range(4):
                        for c in range(2):
                            last = nc.tensor.matmul(ps(j, 2 + p // 2)[0:PAIR, (p % 2) * D:(p % 2) * D + D],
                                                    s[f"x{j}"][:, c, p * PAIR:p * PAIR + PAIR], w["Wv"][:, c, :],
                                                    start=c == 0, stop=c == 1)
                    last.then_inc(S["values"], 1)
                for j in range(2):
                    g = 2 * i + j
                    pe.wait_ge(S["qk"], g + 1)
                    for p in range(4):
                        last = nc.tensor.matmul(ps(j, 0)[0:PAIR, p * PAIR:p * PAIR + PAIR],
                                                s[f"k{j}"][:, p * PAIR:p * PAIR + PAIR],
                                                s[f"q{j}"][:, p * PAIR:p * PAIR + PAIR], start=True, stop=True)
                    last.then_inc(S["scores"], 1)
                for j in range(2):
                    g = 2 * i + j
                    pe.wait_ge(S["masked"], g + 1)
                    pe.wait_ge(S["v_copied"], g + 1)
                    nc.tensor.matmul(ps(j, 3)[0:P, 0:N], m.ones[0:PAIR, 0:P],
                                     s[f"score{j}"].rearrange("p a b -> p (a b)"), start=True, stop=True)
                    for c in range(2):
                        for p in range(4):
                            last = nc.tensor.matmul(ps(j, 1 + c)[0:P, p * PAIR:p * PAIR + PAIR],
                                                    s[f"v{j}"][:, p, c * P:c * P + P], s[f"score{j}"][:, p, :],
                                                    start=True, stop=True)
                    last.then_inc(S["sums"], 1)

        @block.scalar
        def _(act):
            nc.scalar.preload_act_table_set(LOG_EXP)
            act.wait_ge(S["negb"], 1)
            with act.Fori(0, GROUPS // 2) as i:
                for j in range(2):
                    g = 2 * i + j
                    act.wait_ge(S["products"], g + 1)
                    nc.scalar.activation(s[f"forget{j}"], ps(j, 1)[:, 0:N], ACT.Exp, bias=s["negb"],
                                         scale=-1.0).then_inc(S["e"], 1)
                    act.wait_ge(S["min"], g + 1)
                    nc.scalar.activation(s[f"neg{j}"], s[f"neg{j}"], ACT.Exp).then_inc(S["exp"], 1)
                    act.wait_ge(S["values"], g + 3)
                    for q in range(2):
                        last = nc.scalar.activation(s[f"v{j}"][:, 2 * q:2 * q + 2, :],
                                                    r4(ps(j, 2 + q)[0:PAIR, 0:2 * D], 2), ACT.Copy)
                    last.then_inc(S["v_copied"], 1)
                for j in range(2):
                    g = 2 * i + j
                    act.wait_ge(S["u"], g + 1)
                    nc.scalar.activation(s[f"forget{j}"], s[f"forget{j}"], ACT.Ln).then_inc(S["log"], 1)
                for j in range(2):
                    g = 2 * i + j
                    act.wait_ge(S["clip"], g + 1)
                    nc.scalar.activation(s[f"cum{j}"], s[f"cum{j}"], ACT.Exp,
                                         scale=w["sign"]).then_inc(S["decay"], 1)

        @block.vector
        def _(dve):
            dve.sem_inc(S["out"], 2)
            dve.wait_ge(m.loaded, m.due)
            nc.vector.tensor_scalar(s["negb"], w["bf"], -1.0, None, ALU.mult).then_inc(S["negb"], 1)
            with dve.Fori(0, GROUPS // 2) as i:
                for j in range(2):
                    g = 2 * i + j
                    dve.wait_ge(S["products"], g + 1)
                    nc.vector.tensor_scalar(s[f"neg{j}"], ps(j, 0)[:, 0:N], 0.0, None,
                                            ALU.min).then_inc(S["min"], 1)
                    dve.wait_ge(S["e"], g + 1)
                    nc.vector.tensor_scalar(s[f"forget{j}"], s[f"forget{j}"], 1.0, 1e6, ALU.add,
                                            ALU.min).then_inc(S["u"], 1)
                    dve.wait_ge(S["exp"], g + 1)
                    nc.vector.scalar_tensor_tensor(out=s[f"elu{j}"], in0=ps(j, 0)[:, 0:N], scalar=0.0,
                                                   in1=s[f"neg{j}"], op0=ALU.max, op1=ALU.add).then_inc(S["elu"], 1)
                for j in range(2):
                    g = 2 * i + j
                    dve.wait_ge(S["log"], g + 1)
                    nc.vector.tensor_tensor_scan(s[f"cum{j}"], w["carry"], s[f"forget{j}"], 0.0, ALU.mult,
                                                 ALU.add).then_inc(S["scan"], 1)
                    dve.wait_ge(S["scan"], g + 1)
                    nc.vector.tensor_scalar(s[f"cum{j}"], s[f"cum{j}"], 20.0, -20.0, ALU.min,
                                            ALU.max).then_inc(S["clip"], 1)
                for j in range(2):
                    g = 2 * i + j
                    dve.wait_ge(S["decay"], g + 1)
                    dve.wait_ge(S["elu"], g + 1)
                    nc.vector.scalar_tensor_tensor(out=s[f"q{j}"], in0=s[f"elu{j}"][0:64, :], scalar=64 ** -0.5,
                                                   in1=s[f"cum{j}"][0:64, :], op0=ALU.mult, op1=ALU.mult)
                    nc.vector.tensor_tensor(s[f"k{j}"], s[f"elu{j}"][64:128, :], s[f"cum{j}"][64:128, :],
                                            ALU.mult).then_inc(S["qk"], 1)
                for j in range(2):
                    g = 2 * i + j
                    dve.wait_ge(S["scores"], g + 1)
                    nc.vector.tensor_tensor(s[f"score{j}"], r4(ps(j, 0)[0:PAIR, 0:N], 4),
                                            w["causal"].rearrange("p (a b) -> p a b", a=1)
                                            .broadcast_to([PAIR, 4, PAIR]), ALU.mult).then_inc(S["masked"], 1)
                for j in range(2):
                    g = 2 * i + j
                    dve.wait_ge(S["sums"], g + 1)
                    nc.vector.tensor_scalar(s[f"den{j}"], ps(j, 3)[0:P, 0:N], 1e-6, None,
                                            ALU.add).then_inc(S["den"], 1)
                    dve.wait_ge(S["den"], g + 1)
                    nc.vector.reciprocal(s[f"den{j}"], s[f"den{j}"]).then_inc(S["recip"], 1)
                    dve.wait_ge(S["recip"], g + 1)
                    for c in range(2):
                        last = nc.vector.tensor_tensor(dst[:, c, span(g, N)], ps(j, 1 + c)[0:P, 0:N],
                                                       s[f"den{j}"], ALU.mult)
                    last.then_inc(S["out"], 1)
    finish(nc, sems)


def mix_block(nc, m, w, load, x, mix, work, score, mask, mask_rows, dram_score, dram_mask):
    few = max(1, int(round(0.15 * L)))
    n = WIDE
    s = carve(m.scratch[:], {"row": (B, (L,), F32), "less": (B, (L, L), F32), "equal": (B, (L, L), F32),
                             "rank": (B, (L,), F32), "low": (B, (2, L), F32), "sum": (P, (B,), F32),
                             "pooled": (P, (2, B), F32)})
    names = ("product", "score", "stored", "rows", "step", "mask", "mask_stored", "mask_loaded", "pooled",
             "compared", "ranked", "kept_loaded", "equal")
    sems = signals(nc, "mix", *names)
    S = dict(zip(names, sems))
    bl = lambda a: a.rearrange("p (b l) -> p b l", l=L)
    kept = work[:, 0, :]
    with nc.Block() as block:
        @block.sync
        def _(sp):
            load(sp)
            sp.wait_ge(S["score"], T // n + 4)
            sp.dma_start(dram_score, score[0:1, :]).then_inc(S["stored"], 16)
            sp.wait_ge(S["stored"], 16)
            sp.dma_start(s["row"], dram_score.rearrange("a (b l) -> (a b) l", l=L)).then_inc(S["rows"], 16)
            sp.wait_ge(S["mask"], 1)
            for k in range(2):
                sp.dma_start(dram_mask[k].rearrange("(b l) -> b l", l=L), s["low"][:, k, :]
                             ).then_inc(S["mask_stored"], 16)
            sp.wait_ge(S["mask_stored"], 32)
            sp.wait_ge(S["pooled"], 1)
            sp.dma_start(kept, dram_mask[1:2, :].broadcast_to([P, T])).then_inc(S["kept_loaded"], 16)
            sp.dma_start(mask, dram_mask[0:1, :].broadcast_to([P, T])).then_inc(S["mask_loaded"], 16)
            sp.dma_start(mask_rows, dram_mask).then_inc(S["mask_loaded"], 16)
            sp.wait_ge(S["mask_loaded"], 32)

        @block.tensor
        def _(pe):
            pe.wait_ge(m.loaded, m.due)
            with pe.Fori(0, T // n // 2) as i:
                for j in range(2):
                    g = 2 * i + j
                    pe.wait_ge(S["score"], g + 3)
                    for c in range(2):
                        last = nc.tensor.matmul(m.psum[0:P, j, 0:n], w["Wr"][:, c:c + 1].broadcast_to([P, P]),
                                                x[:, c, span(g, n)], start=c == 0, stop=c == 1)
                    last.then_inc(S["product"], 1)

        @block.scalar
        def _(act):
            act.sem_inc(S["score"], 4)
            act.wait_ge(m.loaded, m.due)
            with act.Fori(0, T // n // 2) as i:
                for j in range(2):
                    g = 2 * i + j
                    act.wait_ge(S["product"], g + 1)
                    nc.scalar.activation(score[:, span(g, n)], m.psum[0:P, j, 0:n], ACT.Sigmoid,
                                         bias=w["br"]).then_inc(S["score"], 1)

        @block.vector
        def _(dve):
            done = [0]

            def step(ins):
                done[0] += 1
                ins.then_inc(S["step"], 1)
                dve.wait_ge(S["step"], done[0])

            dve.wait_ge(S["score"], T // n + 4)
            step(nc.vector.tensor_reduce(s["sum"], bl(score), AXX, ALU.add))
            step(nc.vector.tensor_scalar(s["sum"], s["sum"], 1e-6, None, ALU.add))
            step(nc.vector.reciprocal(s["sum"], s["sum"]))
            step(nc.vector.tensor_tensor(bl(mix[:, 0, :]), bl(score),
                                         s["sum"].rearrange("p (b a) -> p b a", a=1).broadcast_to([P, B, L]),
                                         ALU.mult))
            dve.wait_ge(S["rows"], 16)
            si = s["row"].rearrange("p (a l) -> p l a", a=1).broadcast_to([B, L, L])
            sj = s["row"].rearrange("p (a l) -> p a l", a=1).broadcast_to([B, L, L])
            nc.vector.tensor_tensor(s["less"], sj, si, ALU.is_lt)
            nc.vector.tensor_tensor(s["equal"], sj, si, ALU.is_equal).then_inc(S["ranked"], 1)
            step(nc.vector.tensor_tensor(work, x, mix[:, 0:1, :].broadcast_to([P, 2, T]), ALU.mult))
            nc.vector.tensor_reduce(s["pooled"], work.rearrange("p c (b l) -> p c b l", l=L), AXX, ALU.add
                                    ).then_inc(S["pooled"], 1)
            dve.wait_ge(S["compared"], 1)
            step(nc.vector.tensor_reduce(s["rank"], s["less"], AXX, ALU.add))
            nc.vector.tensor_scalar(s["low"][:, 0, :], s["rank"], few - 0.5, None, ALU.is_lt)
            nc.vector.tensor_scalar(s["low"][:, 1, :], s["rank"], few - 0.5, None, ALU.is_gt).then_inc(S["mask"], 1)
            dve.wait_ge(S["pooled"], 1)
            for c in range(2):
                step(nc.vector.tensor_tensor(bl(mix[:, c, :]), bl(score),
                                             s["pooled"][:, c, :].rearrange("p (b a) -> p b a", a=1)
                                             .broadcast_to([P, B, L]), ALU.mult))
            step(nc.vector.tensor_tensor(mix, mix, x, ALU.add))
            dve.wait_ge(S["kept_loaded"], 16)
            nc.vector.tensor_tensor(mix, mix, kept.rearrange("p (a t) -> p a t", a=1).broadcast_to([P, 2, T]),
                                    ALU.mult)

        @block.gpsimd
        def _(pool):
            pool.wait_ge(m.loaded, m.due)
            pool.wait_ge(S["ranked"], 1)
            nc.gpsimd.tensor_tensor(s["equal"], s["equal"], w["before"], ALU.mult).then_inc(S["equal"], 1)
            pool.wait_ge(S["equal"], 1)
            nc.gpsimd.tensor_tensor(s["less"], s["less"], s["equal"], ALU.add).then_inc(S["compared"], 1)
    finish(nc, sems)


def softmax_attention_block(nc, m, w, load, x, x0, mix, mask, mask_rows, dst):
    H3 = 3 * L
    s = carve(m.scratch[:], {"x3": (P, (2, GB, 3, L), F32), "q": (P, (2, N), F32), "k": (P, (2, N), F32),
                             "context": (P, (2, N), F32)}
              | {f"{k}{j}": v for j in range(2) for k, v in (
                  ("max", (100, (HEADS,), F32)), ("sum", (100, (HEADS,), F32)),
                  ("prob", (100, (HEADS, L), F32)), ("turned", (H3, (4, 100), F32)),
                  ("v", (H3, (2, 4, P), F32)))} | {"bq": (P, (2,), F32), "apart": (P, (2, GB, 6, L), F32)})
    names = ("copied", "q", "k", "qk_out", "apart", "logits", "values", "v_apart", "max", "sub", "exp", "sum",
             "recip", "prob", "turned", "turned_out", "ctx", "ctx_out", "product", "out", "bq")
    sems = signals(nc, "attention", *names)
    S = dict(zip(names, sems))
    kx = s["apart"]
    PAIRS = GB // 2
    with nc.Block() as block:
        @block.sync
        def _(sp):
            load(sp)

        @block.gpsimd
        def _(pool):
            with pool.Fori(0, GROUPS) as i:
                pool.wait_ge(S["values"], PAIRS * i + 4)
                for c in range(2):
                    nc.gpsimd.tensor_copy(s["x3"][:, c, :, :, :],
                                          x[:, c, span(i, N)].rearrange("p (b a l) -> p b a l", a=1, l=L)
                                          .broadcast_to([P, GB, 3, L])).then_inc(S["copied"], 1)

        @block.tensor
        def _(pe):
            pe.sem_inc(S["values"], 4)
            pe.wait_ge(m.loaded, m.due)

            def projections(i):
                pe.wait_ge(S["turned_out"], PAIRS * i + 2)
                for q, wt in enumerate((w["Wq"], w["Wk"])):
                    if q == 1:
                        pe.wait_ge(S["qk_out"], 4 * i + 2)
                    for c in range(2):
                        for k in range(2):
                            last = nc.tensor.matmul(m.psum[0:P, 4 + c, 0:N], wt[:, k, c * P:c * P + P],
                                                    x[:, k, span(i, N)], start=k == 0, stop=k == 1)
                        last.then_inc(S["q"], 1)

            def group(i, final):

                def front(p):
                    r = p % 2
                    if p == 0:
                        pe.wait_ge(S["copied"], 2 * i + 2)
                    pe.wait_ge(S["v_apart"], PAIRS * i + p + 1)
                    for b in range(2):
                        for c in range(2):
                            rep = s["x3"][:, c, 2 * p + b, :, :].rearrange("p a l -> p (a l)")
                            last = nc.tensor.matmul(m.psum[0:H3, 2 + r, b * D:b * D + D], rep, w["Wv"][:, c, :],
                                                    start=c == 0, stop=c == 1)
                    last.then_inc(S["values"], 1)
                    if p == 0:
                        pe.wait_ge(S["apart"], 2 * i + 2)
                    pe.wait_ge(S["sub"], PAIRS * i + p + 1)
                    for b in range(2):
                        at = (2 * p + b) * L
                        for c in range(2):
                            last = nc.tensor.matmul(m.psum[64 * b:64 * b + L, r, c * 216:c * 216 + 216],
                                                    s["q"][:, c, at:at + L],
                                                    kx[:, c, 2 * p + b, :, :].rearrange("p h l -> p (h l)"),
                                                    start=True, stop=True)
                    last.then_inc(S["logits"], 1)

                def turn(p):
                    r = p % 2
                    pe.wait_ge(S["prob"], PAIRS * i + p + 1)
                    pe.wait_ge(S["turned_out"], PAIRS * i + p + 1)
                    for q in range(4):
                        last = nc.tensor.transpose(m.psum[0:H3, 4 + r, q * 100:q * 100 + 100],
                                                   s[f"prob{r}"][:, 3 * q:3 * q + 3, :].rearrange("p h l -> p (h l)"),
                                                   m.identity[0:100, 0:100])
                    last.then_inc(S["turned"], 1)

                def context(p):
                    r = p % 2
                    pe.wait_ge(S["turned_out"], PAIRS * i + p + 3)
                    pe.wait_ge(S["v_apart"], PAIRS * i + p + 3)
                    for b in range(2):
                        at = (2 * p + b) * L
                        for c in range(2):
                            for q in range(2):
                                last = nc.tensor.matmul(m.psum[0:P, 6 + c, at:at + L],
                                                        s[f"v{r}"][:, b, 2 * c + q, :],
                                                        s[f"turned{r}"][:, 2 * c + q, 64 * b:64 * b + L],
                                                        start=q == 0, stop=q == 1)
                    last.then_inc(S["ctx"], 1)

                front(0)
                front(1)
                pe.wait_ge(S["qk_out"], 4 * i + 4)
                for p in range(PAIRS):
                    turn(p)
                    if p + 2 < PAIRS:
                        front(p + 2)
                    if p == 0:
                        pe.wait_ge(S["out"], 2 * i + 2)
                    context(p)
                if not final:
                    projections(i + 1)
                pe.wait_ge(S["ctx_out"], 2 * i + 2)
                for c in range(2):
                    out = m.psum[0:P, 6 + c, 0:N]
                    for k in range(2):
                        nc.tensor.matmul(out, w["Wo"][:, k, c * P:c * P + P], s["context"][:, k, :],
                                         start=k == 0, stop=False)
                        nc.tensor.matmul(out, w["Wm"][:, k, c * P:c * P + P], mix[:, k, span(i, N)],
                                         start=False, stop=False)
                    nc.tensor.matmul(out, w["bom"][:, c * P:c * P + P], mask_rows[:, span(i, N)],
                                     start=False, stop=True).then_inc(S["product"], 1)

            projections(0)
            with pe.Fori(0, GROUPS - 1) as i:
                group(i, False)
            group(GROUPS - 1, True)

        @block.scalar
        def _(act):
            nc.scalar.preload_act_table_set(EXP)
            act.sem_inc(S["turned_out"], 2)
            act.wait_ge(m.loaded, m.due)
            act.wait_ge(S["bq"], 1)

            def projections(i):
                for q in range(2):
                    for c in range(2):
                        act.wait_ge(S["q"], 4 * i + 2 * q + c + 1)
                        if q == 0:
                            nc.scalar.activation(s["q"][:, c, :], m.psum[0:P, 4 + c, 0:N], ACT.Identity,
                                                 bias=s["bq"][:, c:c + 1], scale=DH ** -0.5).then_inc(S["qk_out"], 1)
                        else:
                            nc.scalar.activation(s["k"][:, c, :], m.psum[0:P, 4 + c, 0:N], ACT.Identity,
                                                 bias=w["bk"][:, c:c + 1]).then_inc(S["qk_out"], 1)

            def group(i, final):
                def turned(p):
                    r = p % 2
                    act.wait_ge(S["turned"], PAIRS * i + p + 1)
                    nc.scalar.activation(s[f"turned{r}"],
                                         m.psum[0:H3, 4 + r, 0:400].rearrange("p (a b) -> p a b", a=4),
                                         ACT.Copy).then_inc(S["turned_out"], 1)

                def exponential(p):
                    r = p % 2
                    act.wait_ge(S["sub"], PAIRS * i + p + 3)
                    nc.scalar.activation(s[f"prob{r}"], s[f"prob{r}"], ACT.Exp).then_inc(S["exp"], 1)

                exponential(0)
                exponential(1)
                for p in range(PAIRS):
                    turned(p)
                    if p + 2 < PAIRS:
                        exponential(p + 2)
                if not final:
                    projections(i + 1)

            projections(0)
            with act.Fori(0, GROUPS - 1) as i:
                group(i, False)
            group(GROUPS - 1, True)

        @block.vector
        def _(dve):
            dve.sem_inc(S["out"], 2)
            dve.sem_inc(S["v_apart"], 2)
            dve.sem_inc(S["sub"], 2)
            dve.wait_ge(m.loaded, m.due)
            nc.vector.tensor_scalar(s["bq"], w["bq"], DH ** -0.5, None, ALU.mult).then_inc(S["bq"], 1)

            def keys_apart(i):
                for c in range(2):
                    dve.wait_ge(S["qk_out"], 4 * i + 3 + c)
                    for h in range(6):
                        last = nc.vector.tensor_scalar(kx[:, c, :, h, :],
                                                       s["k"][:, c, :].rearrange("p (b l) -> p b l", l=L),
                                                       w["head"][:, h:h + 1], None, ALU.mult)
                    last.then_inc(S["apart"], 1)

            def group(i, final):
                def top(p):
                    r = p % 2
                    dve.wait_ge(S["logits"], PAIRS * i + p + 1)
                    lg = m.psum[0:100, r, 0:432].rearrange("p (h l) -> p h l", l=L)
                    nc.vector.tensor_reduce(s[f"max{r}"], lg, AXX, ALU.max).then_inc(S["max"], 1)
                    dve.wait_ge(S["max"], PAIRS * i + p + 1)
                    if p >= 2:
                        dve.wait_ge(S["turned"], PAIRS * i + p - 1)
                    nc.vector.tensor_tensor(s[f"prob{r}"], lg,
                                            s[f"max{r}"].rearrange("p (h a) -> p h a", a=1)
                                            .broadcast_to([100, HEADS, L]), ALU.subtract).then_inc(S["sub"], 1)
                    dve.wait_ge(S["values"], PAIRS * i + p + 5)
                    if p >= 2:
                        dve.wait_ge(S["ctx"], PAIRS * i + p - 1)
                    for b in range(2):
                        v = m.psum[0:H3, 2 + r, b * D:b * D + D].rearrange("p (c a f) -> p c a f", c=2, a=1)
                        last = nc.vector.tensor_tensor(
                            s[f"v{r}"][:, b, :, :].rearrange("p (c q) f -> p c q f", c=2),
                            v.broadcast_to([H3, 2, 2, P]),
                            w["rows"].rearrange("p (a q) f -> p a q f", a=1).broadcast_to([H3, 2, 2, P]),
                            ALU.mult)
                    last.then_inc(S["v_apart"], 1)

                def norm(p):
                    r = p % 2
                    dve.wait_ge(S["exp"], PAIRS * i + p + 1)
                    nc.vector.tensor_reduce(s[f"sum{r}"], s[f"prob{r}"], AXX, ALU.add).then_inc(S["sum"], 1)
                    dve.wait_ge(S["sum"], PAIRS * i + p + 1)
                    nc.vector.reciprocal(s[f"sum{r}"], s[f"sum{r}"]).then_inc(S["recip"], 1)
                    dve.wait_ge(S["recip"], PAIRS * i + p + 1)
                    nc.vector.tensor_tensor(s[f"prob{r}"], s[f"prob{r}"],
                                            s[f"sum{r}"].rearrange("p (h a) -> p h a", a=1)
                                            .broadcast_to([100, HEADS, L]), ALU.mult).then_inc(S["prob"], 1)

                top(0)
                top(1)
                for p in range(PAIRS):
                    norm(p)
                    if 1 <= p < PAIRS - 1:
                        top(p + 1)
                dve.wait_ge(S["ctx"], PAIRS * i + PAIRS)
                for c in range(2):
                    nc.vector.scalar_tensor_tensor(out=s["context"][:, c, :], in0=m.psum[0:P, 6 + c, 0:N],
                                                   scalar=w["bv"][:, c:c + 1], in1=mask[:, span(i, N)],
                                                   op0=ALU.add, op1=ALU.mult).then_inc(S["ctx_out"], 1)
                if not final:
                    keys_apart(i + 1)
                for c in range(2):
                    dve.wait_ge(S["product"], 2 * i + c + 1)
                    nc.vector.tensor_tensor(dst[:, c, span(i, N)], m.psum[0:P, 6 + c, 0:N],
                                            x0[:, c, span(i, N)], ALU.add).then_inc(S["out"], 1)

            keys_apart(0)
            with dve.Fori(0, GROUPS - 1) as i:
                group(i, False)
            group(GROUPS - 1, True)
    finish(nc, sems)


def rates_block(nc, m, w, load, x, delta, coef, rates):
    n = WIDE
    s = carve(m.scratch[:], {f"{k}{j}": v for j in range(2) for k, v in (
        ("mag", (128, (2, n), F32)), ("rest", (32, (n,), F32)), ("high", (32, (n,), BF16)),
        ("mid", (32, (n,), BF16)))} | {"lmag": (128, (24,), F32)})
    names = ("product", "mag", "exp", "log", "max", "out", "high", "rest", "mid", "low", "rates",
             "negated")
    sems = signals(nc, "rates", *names)
    S = dict(zip(names, sems))
    with nc.Block() as block:
        @block.sync
        def _(sp):
            load(sp)

        @block.tensor
        def _(pe):
            pe.wait_ge(m.loaded, m.due)
            with pe.Fori(0, T // n // 2) as i:
                for j in range(2):
                    g = 2 * i + j
                    pe.wait_ge(S["out"], g + 1)
                    pe.wait_ge(S["low"], g + 1)
                    for c in range(2):
                        for k in range(2):
                            nc.tensor.matmul(m.psum[:, 3 * j + c, 0:n], w["Wd"][:, k, c * 128:c * 128 + 128],
                                             x[:, k, span(g, n)], start=k == 0, stop=k == 1)
                    for k in range(2):
                        last = nc.tensor.matmul(m.psum[0:32, 3 * j + 2, 0:n], w["WBC"][:, k, :],
                                                x[:, k, span(g, n)], start=k == 0, stop=k == 1)
                    last.then_inc(S["product"], 1)

        @block.scalar
        def _(act):
            nc.scalar.preload_act_table_set(LOG_EXP)
            act.wait_ge(m.loaded, m.due)
            nc.scalar.activation(s["lmag"], w["loglam"], ACT.Abs).then_inc(S["rates"], 1)
            act.wait_ge(S["rates"], 1)
            nc.scalar.activation(s["lmag"], s["lmag"], ACT.Exp, scale=-1.0).then_inc(S["rates"], 1)
            act.wait_ge(S["rates"], 2)
            nc.scalar.activation(s["lmag"], s["lmag"], ACT.Ln, bias=m.ones[:, 0:1]).then_inc(S["rates"], 1)
            with act.Fori(0, T // n // 2) as i:
                for j in range(2):
                    g = 2 * i + j
                    act.wait_ge(S["product"], g + 1)
                    act.wait_ge(S["out"], g + 1)
                    act.wait_ge(S["low"], g + 1)
                    nc.scalar.activation(s[f"high{j}"], m.psum[0:32, 3 * j + 2, 0:n], ACT.Copy)
                    nc.scalar.activation(coef[0:32, span(g, n)], m.psum[0:32, 3 * j + 2, 0:n],
                                         ACT.Copy).then_inc(S["high"], 1)
                    for c in range(2):
                        last = nc.scalar.activation(s[f"mag{j}"][:, c, :], m.psum[:, 3 * j + c, 0:n], ACT.Abs,
                                                    bias=w["bd"][:, c:c + 1])
                    last.then_inc(S["mag"], 1)
                for j in range(2):
                    g = 2 * i + j
                    act.wait_ge(S["mag"], g + 1)
                    nc.scalar.activation(s[f"mag{j}"], s[f"mag{j}"], ACT.Exp, scale=-1.0).then_inc(S["exp"], 1)
                    act.wait_ge(S["exp"], g + 1)
                    nc.scalar.activation(s[f"mag{j}"], s[f"mag{j}"], ACT.Ln, bias=m.ones[:, 0:1]
                                         ).then_inc(S["log"], 1)
                    act.wait_ge(S["rest"], g + 1)
                    nc.scalar.activation(s[f"mid{j}"], s[f"rest{j}"], ACT.Copy)
                    nc.scalar.activation(coef[32:64, span(g, n)], s[f"rest{j}"], ACT.Copy).then_inc(S["mid"], 1)

        @block.vector
        def _(dve):
            dve.sem_inc(S["out"], 2)
            dve.sem_inc(S["low"], 2)
            dve.wait_ge(m.loaded, m.due)
            nc.vector.tensor_scalar(rates, w["loglam"], 0.0, None, ALU.max).then_inc(S["negated"], 1)
            dve.wait_ge(S["rates"], 3)
            dve.wait_ge(S["negated"], 1)
            nc.vector.tensor_tensor(rates, rates, s["lmag"], ALU.add).then_inc(S["negated"], 1)
            dve.wait_ge(S["negated"], 2)
            nc.vector.tensor_scalar(rates, rates, -1.0, None, ALU.mult)
            with dve.Fori(0, T // n // 2) as i:
                for j in range(2):
                    g = 2 * i + j
                    dve.wait_ge(S["high"], g + 1)
                    nc.vector.tensor_tensor(s[f"rest{j}"], m.psum[0:32, 3 * j + 2, 0:n], s[f"high{j}"],
                                            ALU.subtract).then_inc(S["rest"], 1)
                    dve.wait_ge(S["mag"], g + 1)
                    for c in range(2):
                        last = nc.vector.tensor_scalar(delta[:, c, span(g, n)], m.psum[:, 3 * j + c, 0:n],
                                                       w["bd"][:, c:c + 1], 0.0, ALU.add, ALU.max)
                    last.then_inc(S["max"], 1)
                for j in range(2):
                    g = 2 * i + j
                    dve.wait_ge(S["log"], g + 1)
                    dve.wait_ge(S["max"], g + 1)
                    d = delta[:, :, span(g, n)]
                    nc.vector.tensor_tensor(d, d, s[f"mag{j}"], ALU.add).then_inc(S["out"], 1)
                    dve.wait_ge(S["mid"], g + 1)
                    nc.vector.tensor_tensor(coef[64:96, span(g, n)], s[f"rest{j}"], s[f"mid{j}"],
                                            ALU.subtract).then_inc(S["low"], 1)
    finish(nc, sems)


def scan_block(nc, m, w, load, delta, coef, rates):
    CH = 24
    s = carve(m.scratch[:], {f"{k}{j}": (128, (N,), F32) for j in range(2) for k in ("a", "b", "h", "y")}
              | {"pick": (96, (32,), BF16), "picks": (96, (16, 128), BF16)})
    names = ("act_turn", "pick", "zero", "spread", "a", "b", "scan", "y", "out", "sum")
    sems = signals(nc, "scan", *names)
    S = dict(zip(names, sems))
    bl = lambda t: t.rearrange("p (b l) -> p b l", l=L)
    part = lambda q: 0 if q < STATES else 1
    with nc.Block() as block:
        @block.sync
        def _(sp):
            load(sp)

        @block.tensor
        def _(pe):
            pe.wait_ge(m.loaded, m.due)
            pe.wait_ge(S["pick"], 2)
            with pe.Fori(0, GROUPS) as i:
                def out(q):
                    pe.wait_ge(S["y"], CH * i + q + 4)
                    if q == 0:
                        pe.wait_ge(S["sum"], 2 * i + 2)
                    for c in range(2):
                        last = nc.tensor.matmul(m.psum[0:P, 6 + c, 0:N], w["Wout"][:, q, c * P:c * P + P],
                                                s[f"y{q % 2}"], start=q == 0, stop=q == CH - 1)
                    last.then_inc(S["out"], 1)

                def spread(q):
                    pe.wait_ge(S["y"], CH * i + q + 1)
                    for k in range(2):
                        if part(q) == 0:
                            pick = s["pick"][:, 16 * k + q:16 * k + q + 1].broadcast_to([96, 128])
                        else:
                            pick = s["picks"][:, 8 * k + q - STATES, :]
                        last = nc.tensor.matmul(m.psum[:, 2 * (q % 3) + k, 0:N], pick, coef[:, span(i, N)],
                                                start=True, stop=True)
                    last.then_inc(S["spread"], 1)

                spread(0)
                spread(1)
                for q in range(CH):
                    if q + 2 < CH:
                        spread(q + 2)
                    out(q)

        @block.scalar
        def _(act):
            act.sem_inc(S["a"], 2)
            act.wait_ge(S["zero"], 2)
            with act.Fori(0, GROUPS) as i:
                for q in range(CH):
                    act.wait_ge(S["scan"], CH * i + q + 1)
                    own_wait(act, S["act_turn"])
                    nc.scalar.activation(bl(s[f"a{q % 2}"])[:, :, 1:L], bl(delta[:, part(q), span(i, N)])[:, :, 1:L],
                                         ACT.Exp, scale=rates[:, q:q + 1]).then_inc(S["a"], 1)

        @block.vector
        def _(dve):
            dve.sem_inc(S["y"], 3)
            dve.sem_inc(S["scan"], 2)
            dve.sem_inc(S["out"], 2)
            dve.sem_inc(S["sum"], 2)
            dve.wait_ge(m.loaded, m.due)
            nc.vector.tensor_copy(s["pick"], w["pick"]).then_inc(S["pick"], 1)
            nc.vector.tensor_copy(s["picks"].rearrange("p m (h r) -> p (m h) r", h=2),
                                  w["pick"].rearrange("p (n a) -> p n a", a=1).broadcast_to([96, 32, 64])
                                  ).then_inc(S["pick"], 1)
            for j in range(2):
                nc.vector.memset(bl(s[f"a{j}"])[:, :, 0:1], 0.0).then_inc(S["zero"], 1)
            with dve.Fori(0, GROUPS) as i:
                def inputs(q):
                    dve.wait_ge(S["spread"], CH * i + q + 1)
                    dve.wait_ge(S["scan"], CH * i + q + 1)
                    nc.vector.tensor_tensor(s[f"b{q % 2}"], delta[:, part(q), span(i, N)],
                                            m.psum[:, 2 * (q % 3), 0:N], ALU.mult).then_inc(S["b"], 1)

                inputs(0)
                for q in range(CH):
                    dve.wait_ge(S["a"], CH * i + q + 3)
                    dve.wait_ge(S["b"], CH * i + q + 1)
                    dve.wait_ge(S["y"], CH * i + q + 2)
                    nc.vector.tensor_tensor_scan(s[f"h{q % 2}"], s[f"a{q % 2}"], s[f"b{q % 2}"], 0.0, ALU.mult,
                                                 ALU.add).then_inc(S["scan"], 1)
                    if q + 1 < CH:
                        inputs(q + 1)
                    dve.wait_ge(S["scan"], CH * i + q + 3)
                    dve.wait_ge(S["out"], CH * i + q + 1)
                    nc.vector.tensor_tensor(s[f"y{q % 2}"], s[f"h{q % 2}"], m.psum[:, 2 * (q % 3) + 1, 0:N],
                                            ALU.mult).then_inc(S["y"], 1)
                dve.wait_ge(S["out"], CH * i + CH + 2)
                for c in range(2):
                    h = m.h[:, c, span(i, N)]
                    nc.vector.scalar_tensor_tensor(out=h, in0=m.psum[0:P, 6 + c, 0:N], scalar=w["bout"][:, c:c + 1],
                                                   in1=h, op0=ALU.add, op1=ALU.add).then_inc(S["sum"], 1)
    finish(nc, sems)


def image_route_block(nc, m, w, load, x, table, factor):
    E, PLACES, TOTAL = 3, IMAGE_GROUPS * GB, IMAGE_GROUPS
    s = carve(m.scratch[:], {"mean": (P, (2, B), F32), "logit": (B, (E,), F32), "top": (B, (1,), F32),
                             "first": (B, (E,), F32), "rest": (B, (1,), F32), "eights": (B, (GB,), F32),
                             "over": (B, (E, GB), F32), "groups": (B, (E,), F32), "end": (B, (E,), F32),
                             "start": (B, (E,), F32), "prob": (B, (1,), F32), "place": (B, (1,), F32),
                             "hot": (B, (PLACES,), F32), "later": (1, (2, TOTAL), F32), "pairs": (1, (1,), F32)})
    names = ("mean", "logits", "step", "exp", "ordered", "placed", "products", "places")
    sems = signals(nc, "images", *names)
    S = dict(zip(names, sems))
    ps = lambda parts, bank, n: m.psum[0:parts, bank, 0:n]
    with nc.Block() as block:
        @block.sync
        def _(sp):
            load(sp)

        @block.tensor
        def _(pe):
            pe.wait_ge(m.loaded, m.due)
            pe.wait_ge(S["mean"], 1)
            for c in range(2):
                last = nc.tensor.matmul(ps(B, 0, E), s["mean"][:, c, :], w["Wg"][:, c, :],
                                        start=c == 0, stop=c == 1)
            last.then_inc(S["logits"], 1)
            pe.wait_ge(S["ordered"], 1)
            nc.tensor.matmul(ps(B, 1, E), w["before"], s["first"], start=True, stop=True)
            nc.tensor.matmul(ps(B, 2, E), m.ones[0:B, 0:B], s["first"], start=True, stop=True
                             ).then_inc(S["products"], 1)
            pe.wait_ge(S["placed"], 1)
            nc.tensor.matmul(ps(1, 3, PLACES), w["token"], s["hot"], start=True, stop=True)
            nc.tensor.matmul(ps(P, 4, PLACES), s["prob"].broadcast_to([B, P]), s["hot"], start=True, stop=True
                             ).then_inc(S["places"], 1)

        @block.scalar
        def _(act):
            act.wait_ge(S["step"], 3)
            nc.scalar.activation(s["logit"], s["logit"], ACT.Exp).then_inc(S["exp"], 1)

        @block.vector
        def _(dve):
            done = [0]

            def step(ins):
                done[0] += 1
                ins.then_inc(S["step"], 1)
                dve.wait_ge(S["step"], done[0])

            step(nc.vector.tensor_reduce(s["mean"], x.rearrange("p c (b l) -> p c b l", l=L), AXX, ALU.add))
            nc.vector.tensor_scalar(s["mean"], s["mean"], 1.0 / L, None, ALU.mult).then_inc(S["mean"], 1)
            dve.wait_ge(S["logits"], 1)
            step(nc.vector.tensor_reduce(s["top"], ps(B, 0, E), AXX, ALU.max))
            step(nc.vector.tensor_scalar(s["logit"], ps(B, 0, E), s["top"], None, ALU.subtract))
            dve.wait_ge(S["exp"], 1)
            step(nc.vector.tensor_reduce(s["rest"], s["logit"], AXX, ALU.add))
            step(nc.vector.reciprocal(s["rest"], s["rest"]))
            step(nc.vector.tensor_scalar(s["logit"], s["logit"], s["rest"], None, ALU.mult))
            step(nc.vector.tensor_reduce(s["prob"], s["logit"], AXX, ALU.max))
            step(nc.vector.tensor_scalar(s["first"], s["logit"], s["prob"], None, ALU.is_equal))
            step(nc.vector.tensor_scalar(s["rest"], s["first"][:, 0:1], -1.0, 1.0, ALU.mult, ALU.add))
            step(nc.vector.tensor_tensor(s["first"][:, 1:2], s["first"][:, 1:2], s["rest"], ALU.mult))
            nc.vector.tensor_tensor(s["first"][:, 2:3], s["rest"], s["first"][:, 1:2], ALU.subtract
                                    ).then_inc(S["ordered"], 1)
            dve.wait_ge(m.loaded, m.due)
            step(nc.vector.tensor_scalar(s["eights"], w["numbers"][:, 0:GB], float(GB), None, ALU.mult))
            dve.wait_ge(S["products"], 1)
            step(nc.vector.tensor_tensor(s["over"], s["eights"].rearrange("p (a n) -> p a n", a=1)
                                         .broadcast_to([B, E, GB]), ps(B, 2, E).rearrange("p (e a) -> p e a", a=1)
                                         .broadcast_to([B, E, GB]), ALU.is_lt))
            step(nc.vector.tensor_reduce(s["groups"], s["over"], AXX, ALU.add))
            step(nc.vector.tensor_copy(s["end"], s["groups"]))
            for e in range(1, E):
                step(nc.vector.tensor_tensor(s["end"][:, e:e + 1], s["end"][:, e - 1:e], s["end"][:, e:e + 1],
                                             ALU.add))
            step(nc.vector.tensor_tensor(s["start"], s["end"], s["groups"], ALU.subtract))
            step(nc.vector.scalar_tensor_tensor(out=s["start"], in0=s["start"], scalar=float(GB),
                                                in1=ps(B, 1, E), op0=ALU.mult, op1=ALU.add))
            step(nc.vector.tensor_tensor(s["start"], s["start"], s["first"], ALU.mult))
            step(nc.vector.tensor_reduce(s["place"], s["start"], AXX, ALU.add))
            nc.vector.tensor_scalar(s["hot"], w["numbers"][:, 0:PLACES], s["place"], None, ALU.is_equal
                                    ).then_inc(S["placed"], 1)
            for e in range(2):
                step(nc.vector.tensor_scalar(s["later"][:, e, :], w["numbers"][0:1, 0:TOTAL], s["end"][0:1, e:e + 1],
                                             None, ALU.is_ge))
            step(nc.vector.tensor_scalar(s["pairs"], s["end"][0:1, 2:3], 0.5, 0.25, ALU.mult, ALU.add))
            nc.vector.tensor_tensor(table[:, PLACES:PLACES + TOTAL], s["later"][:, 0, :], s["later"][:, 1, :],
                                    ALU.add)
            nc.vector.tensor_copy(table[:, PLACES + TOTAL:PLACES + TOTAL + 1], s["pairs"])
            dve.wait_ge(S["places"], 1)
            nc.vector.tensor_copy(table[:, 0:PLACES], ps(1, 3, PLACES))
            nc.vector.tensor_copy(factor, ps(P, 4, PLACES))
    finish(nc, sems)


def image_expert_block(nc, m, load, x, table, factor, w1, b1, w2, b2):
    PLACES, CH = IMAGE_GROUPS * GB, HID // 128
    s = carve(m.scratch[:], {f"{k}{j}": v for j in range(2) for k, v in (
        ("x", (P, (2, N), F32)), ("hidden", (128, (CH, N), F32)), ("scaled", (P, (2, N), F32)))})
    wb = carve(m.full[:, 4:8, :].rearrange("p a t -> p (a t)"), {f"{k}{j}": v for j in range(2) for k, v in (
        ("w1", (P, (2, HID), F32)), ("b1", (128, (CH,), F32)), ("w2", (128, (CH, D), F32)), ("b2", (P, (2,), F32)))})
    names = ("up_weights0", "up_weights1", "down_weights0", "down_weights1", "gathered", "up", "hidden", "down",
             "scaled", "added", "sp_turn", "pool_turn")
    sems = signals(nc, "image_experts", *names)
    S = dict(zip(names, sems))
    s_w1, s_w2 = (S["up_weights0"], S["up_weights1"]), (S["down_weights0"], S["down_weights1"])
    up = lambda k: m.psum[:, k % 4, 0:N]
    trips = lambda eng: eng.value_load(table[0:1, PLACES + IMAGE_GROUPS:PLACES + IMAGE_GROUPS + 1], min_val=1,
                                       max_val=IMAGE_GROUPS // 2)
    token = lambda eng, n: eng.value_load(table[0:1, bass.ds(n, 1)], min_val=0, max_val=T - L)
    with nc.Block() as block:
        @block.sync
        def _(sp):
            load(sp)
            with sp.Fori(0, trips(sp)) as i:
                for j in range(2):
                    t = 2 * i + j
                    e = sp.value_load(table[0:1, bass.ds(t + PLACES, 1)], min_val=0, max_val=2)
                    sp.wait_ge(S["hidden"], CH * t + CH)
                    own_wait(sp, S["sp_turn"])
                    sp.dma_start(wb[f"w1{j}"], w1[bass.ds(e, 1)].rearrange("e p c f -> p (e c) f")
                                 ).then_inc(s_w1[j], 16)
                    sp.dma_start(wb[f"b1{j}"], b1[bass.ds(e, 1)].rearrange("e p c -> p (e c)")
                                 ).then_inc(s_w1[j], 16)
                for j in range(2):
                    t = 2 * i + j
                    e = sp.value_load(table[0:1, bass.ds(t + PLACES, 1)], min_val=0, max_val=2)
                    sp.wait_ge(S["scaled"], 2 * t + 2)
                    own_wait(sp, S["sp_turn"])
                    sp.dma_start(wb[f"w2{j}"], w2[bass.ds(e, 1)].rearrange("e p c f -> p (e c) f")
                                 ).then_inc(s_w2[j], 16)
                    sp.dma_start(wb[f"b2{j}"], b2[bass.ds(e, 1)].rearrange("e p c -> p (e c)")
                                 ).then_inc(s_w2[j], 16)

        @block.gpsimd
        def _(pool):
            with pool.Fori(0, trips(pool)) as i:
                for j in range(2):
                    t = 2 * i + j
                    pool.wait_ge(S["up"], CH * t + CH)
                    own_wait(pool, S["pool_turn"])
                    for n in range(GB):
                        at = token(pool, GB * t + n)
                        last = nc.gpsimd.tensor_copy(s[f"x{j}"][:, :, n * L:n * L + L], x[:, :, bass.ds(at, L)])
                    last.then_inc(S["gathered"], 1)

        @block.tensor
        def _(pe):
            pe.sem_inc(S["up"], 2 * CH)
            pe.sem_inc(S["down"], 4)
            with pe.Fori(0, trips(pe)) as i:
                for j in range(2):
                    t = 2 * i + j
                    pe.wait_ge(s_w1[j], 32 * i + 32)
                    pe.wait_ge(S["gathered"], t + 1)
                    for k in range(CH):
                        pe.wait_ge(S["hidden"], CH * t + k + 1 + 2 * CH - 4)
                        for c in range(2):
                            last = nc.tensor.matmul(up(j * CH + k), wb[f"w1{j}"][:, c, k * 128:k * 128 + 128],
                                                    s[f"x{j}"][:, c, :], start=c == 0, stop=c == 1)
                        last.then_inc(S["up"], 1)
                for j in range(2):
                    t = 2 * i + j
                    pe.wait_ge(s_w2[j], 32 * i + 32)
                    pe.wait_ge(S["hidden"], CH * t + 3 * CH)
                    pe.wait_ge(S["scaled"], 2 * t + 2)
                    for c in range(2):
                        for k in range(CH):
                            last = nc.tensor.matmul(m.psum[0:P, 4 + 2 * j + c, 0:N], wb[f"w2{j}"][:, k, c * P:c * P + P],
                                                    s[f"hidden{j}"][:, k, :], start=k == 0, stop=k == CH - 1)
                        last.then_inc(S["down"], 1)

        @block.scalar
        def _(act):
            nc.scalar.preload_act_table_set(GELU)
            act.sem_inc(S["hidden"], 2 * CH)
            with act.Fori(0, trips(act)) as i:
                for j in range(2):
                    t = 2 * i + j
                    act.wait_ge(S["down"], 2 * t + 2)
                    for k in range(CH):
                        act.wait_ge(S["up"], CH * t + k + 1 + 2 * CH)
                        nc.scalar.activation(s[f"hidden{j}"][:, k, :], up(j * CH + k), ACT.Gelu,
                                             bias=wb[f"b1{j}"][:, k:k + 1]).then_inc(S["hidden"], 1)

        @block.vector
        def _(dve):
            dve.sem_inc(S["scaled"], 4)
            dve.sem_inc(S["added"], 2 * GB)
            with dve.Fori(0, trips(dve)) as i:
                for j in range(2):
                    t = 2 * i + j
                    dve.wait_ge(S["added"], GB * t + GB)
                    for c in range(2):
                        dve.wait_ge(S["down"], 2 * t + c + 5)
                        nc.vector.scalar_tensor_tensor(
                            out=s[f"scaled{j}"][:, c, :].rearrange("p (b l) -> p b l", l=L),
                            in0=m.psum[0:P, 4 + 2 * j + c, 0:N].rearrange("p (b l) -> p b l", l=L),
                            scalar=wb[f"b2{j}"][:, c:c + 1],
                            in1=factor[:, span(t, GB)].rearrange("p (b a) -> p b a", a=1).broadcast_to([P, GB, L]),
                            op0=ALU.add, op1=ALU.mult).then_inc(S["scaled"], 1)
                    dve.wait_ge(S["scaled"], 2 * t + 6)
                    for n in range(GB):
                        at = token(dve, GB * t + n)
                        dve.wait_ge(S["added"], GB * t + n + 2 * GB)
                        h = m.h[:, :, bass.ds(at, L)]
                        nc.vector.tensor_tensor(h, s[f"scaled{j}"][:, :, n * L:n * L + L], h, ALU.add
                                                ).then_inc(S["added"], 1)
    finish(nc, sems)


def retention_block(nc, m, w, load, x):
    s = carve(m.scratch[:], {f"{k}{j}": v for j in range(2) for k, v in (
        ("x", (P, (2, N), F32)), ("q", (P, (2, N), F32)), ("k", (P, (2, N), F32)),
        ("v", (PAIR, (4, D), F32)), ("score", (PAIR, (4, PAIR), F32)))})
    ps = lambda j, q: m.psum[:, 4 * j + q, :]
    names = ("copied", "queries", "keys", "q_out", "k_out", "values", "v_out", "scores", "masked", "sums", "out")
    sems = signals(nc, "retention", *names)
    S = dict(zip(names, sems))
    with nc.Block() as block:
        @block.sync
        def _(sp):
            load(sp)

        @block.gpsimd
        def _(pool):
            with pool.Fori(0, GROUPS // 2) as i:
                for j in range(2):
                    g = 2 * i + j
                    pool.wait_ge(S["values"], g + 1)
                    nc.gpsimd.tensor_copy(s[f"x{j}"], x[:, :, span(g, N)]).then_inc(S["copied"], 1)

        @block.tensor
        def _(pe):
            pe.sem_inc(S["values"], 2)
            pe.wait_ge(m.loaded, m.due)
            with pe.Fori(0, GROUPS // 2) as i:
                for j in range(2):
                    g = 2 * i + j
                    pe.wait_ge(S["out"], g + 1)
                    for q in range(2):
                        for c in range(2):
                            for k in range(2):
                                last = nc.tensor.matmul(ps(j, 2 * q + c)[0:P, 0:N],
                                                        w["Wqkv"][:, k, q * D + c * P:q * D + c * P + P],
                                                        x[:, k, span(g, N)], start=k == 0, stop=k == 1)
                        last.then_inc(S["queries"] if q == 0 else S["keys"], 1)
                for j in range(2):
                    g = 2 * i + j
                    pe.wait_ge(S["copied"], g + 1)
                    pe.wait_ge(S["q_out"], g + 1)
                    for p in range(4):
                        for c in range(2):
                            last = nc.tensor.matmul(ps(j, p // 2)[0:PAIR, (p % 2) * D:(p % 2) * D + D],
                                                    s[f"x{j}"][:, c, p * PAIR:p * PAIR + PAIR],
                                                    w["Wqkv"][:, c, 2 * D:3 * D], start=c == 0, stop=c == 1)
                    last.then_inc(S["values"], 1)
                    pe.wait_ge(S["k_out"], g + 1)
                    for p in range(4):
                        for c in range(2):
                            last = nc.tensor.matmul(ps(j, 2)[0:PAIR, p * PAIR:p * PAIR + PAIR],
                                                    s[f"k{j}"][:, c, p * PAIR:p * PAIR + PAIR],
                                                    s[f"q{j}"][:, c, p * PAIR:p * PAIR + PAIR],
                                                    start=c == 0, stop=c == 1)
                    last.then_inc(S["scores"], 1)
                for j in range(2):
                    g = 2 * i + j
                    pe.wait_ge(S["v_out"], g + 1)
                    pe.wait_ge(S["masked"], g + 1)
                    for c in range(2):
                        for p in range(4):
                            last = nc.tensor.matmul(ps(j, 3 * (1 - c))[0:P, p * PAIR:p * PAIR + PAIR],
                                                    s[f"v{j}"][:, p, c * P:c * P + P], s[f"score{j}"][:, p, :],
                                                    start=True, stop=True)
                    last.then_inc(S["sums"], 1)

        @block.scalar
        def _(act):
            act.wait_ge(m.loaded, m.due)
            with act.Fori(0, GROUPS // 2) as i:
                for q, (done, out, t) in enumerate((("queries", "q_out", "q"), ("keys", "k_out", "k"))):
                    for j in range(2):
                        g = 2 * i + j
                        act.wait_ge(S[done], g + 1)
                        for c in range(2):
                            last = nc.scalar.activation(s[f"{t}{j}"][:, c, :], ps(j, 2 * q + c)[0:P, 0:N],
                                                        ACT.Identity, bias=w["bqk"][:, 2 * q + c:2 * q + c + 1])
                        last.then_inc(S[out], 1)

        @block.vector
        def _(dve):
            dve.sem_inc(S["out"], 2)
            dve.wait_ge(m.loaded, m.due)
            with dve.Fori(0, GROUPS // 2) as i:
                for j in range(2):
                    g = 2 * i + j
                    dve.wait_ge(S["values"], g + 3)
                    for q in range(2):
                        last = nc.vector.tensor_tensor(
                            s[f"v{j}"][:, 2 * q:2 * q + 2, :],
                            ps(j, q)[0:PAIR, 0:2 * D].rearrange("p (a b) -> p a b", a=2),
                            w["bv"].rearrange("p (a b) -> p a b", a=1).broadcast_to([PAIR, 2, D]), ALU.add)
                    last.then_inc(S["v_out"], 1)
                    dve.wait_ge(S["scores"], g + 1)
                    nc.vector.tensor_tensor(s[f"score{j}"], ps(j, 2)[0:PAIR, 0:N].rearrange("p (a b) -> p a b", a=4),
                                            w["decay"].rearrange("p (a b) -> p a b", a=1)
                                            .broadcast_to([PAIR, 4, PAIR]), ALU.mult).then_inc(S["masked"], 1)
                for j in range(2):
                    g = 2 * i + j
                    dve.wait_ge(S["sums"], g + 1)
                    for c in range(2):
                        h = m.h[:, c, span(g, N)]
                        last = nc.vector.tensor_tensor(h, ps(j, 3 * (1 - c))[0:P, 0:N], h, ALU.add)
                    last.then_inc(S["out"], 1)
    finish(nc, sems)


def adapter_block(nc, m, w, load, x, logits, hidden, gates, dram_logits, dram_gates):
    n, E, R = WIDE, 3, 8
    TT = T // 128
    s = carve(m.scratch[:], {"logit": (128, (E, TT), F32), "top": (128, (TT,), F32), "sum": (128, (TT,), F32),
                             "drop": (128, (E, TT), F32), "keep": (128, (E, TT), F32)})
    names = ("product", "acted", "stored", "loaded", "step", "exp", "gates", "gates_stored", "gates_loaded")
    sems = signals(nc, "adapter", *names)
    S = dict(zip(names, sems))
    one = lambda a: a.rearrange("p (a t) -> p a t", a=1).broadcast_to([128, E, TT])
    with nc.Block() as block:
        @block.sync
        def _(sp):
            load(sp)
            sp.wait_ge(S["acted"], T // n + 2)
            sp.dma_start(dram_logits, logits).then_inc(S["stored"], 16)
            sp.wait_ge(S["stored"], 16)
            for e in range(E):
                sp.dma_start(s["logit"][:, e, :], dram_logits[e].rearrange("(p t) -> p t", p=128)
                             ).then_inc(S["loaded"], 16)
            sp.wait_ge(S["gates"], 1)
            for e in range(E):
                sp.dma_start(dram_gates[e].rearrange("(p t) -> p t", p=128), s["keep"][:, e, :]
                             ).then_inc(S["gates_stored"], 16)
            sp.wait_ge(S["gates_stored"], 16 * E)
            for e in range(E):
                sp.dma_start(gates[R * e:R * e + R, :], dram_gates[e:e + 1, :].broadcast_to([R, T])
                             ).then_inc(S["gates_loaded"], 16)

        @block.tensor
        def _(pe):
            pe.wait_ge(m.loaded, m.due)
            with pe.Fori(0, T // n // 2) as i:
                for j in range(2):
                    g = 2 * i + j
                    pe.wait_ge(S["acted"], g + 1)
                    for out, wt in ((m.psum[0:E, 2 * j, 0:n], w["router"]), (m.psum[0:E * R, 2 * j + 1, 0:n], w["down"])):
                        for c in range(2):
                            last = nc.tensor.matmul(out, wt[:, c, :], x[:, c, span(g, n)], start=c == 0, stop=c == 1)
                    last.then_inc(S["product"], 1)

        @block.scalar
        def _(act):
            act.sem_inc(S["acted"], 2)
            act.wait_ge(m.loaded, m.due)
            with act.Fori(0, T // n // 2) as i:
                for j in range(2):
                    g = 2 * i + j
                    act.wait_ge(S["product"], g + 1)
                    nc.scalar.activation(logits[:, span(g, n)], m.psum[0:E, 2 * j, 0:n], ACT.Identity,
                                         bias=w["router_b"])
                    nc.scalar.activation(hidden[:, span(g, n)], m.psum[0:E * R, 2 * j + 1, 0:n],
                                         ACT.Gelu).then_inc(S["acted"], 1)
            act.wait_ge(S["step"], 2)
            nc.scalar.activation(s["logit"], s["logit"], ACT.Exp).then_inc(S["exp"], 1)

        @block.vector
        def _(dve):
            done = [0]

            def step(ins):
                done[0] += 1
                ins.then_inc(S["step"], 1)
                dve.wait_ge(S["step"], done[0])

            dve.wait_ge(S["loaded"], 16 * E)
            te = lambda a: a.rearrange("p e t -> p t e")
            step(nc.vector.tensor_reduce(s["top"], te(s["logit"]), AXX, ALU.max))
            step(nc.vector.tensor_tensor(s["logit"], s["logit"], one(s["top"]), ALU.subtract))
            dve.wait_ge(S["exp"], 1)
            step(nc.vector.tensor_reduce(s["sum"], te(s["logit"]), AXX, ALU.add))
            step(nc.vector.reciprocal(s["sum"], s["sum"]))
            step(nc.vector.tensor_tensor(s["logit"], s["logit"], one(s["sum"]), ALU.mult))
            p = [s["logit"][:, e, :] for e in range(E)]
            d = [s["drop"][:, e, :] for e in range(E)]
            step(nc.vector.tensor_tensor(d[0], p[2], p[0], ALU.is_le))
            step(nc.vector.tensor_tensor(d[2], p[2], p[1], ALU.is_le))
            step(nc.vector.tensor_tensor(d[2], d[2], d[0], ALU.mult))
            step(nc.vector.tensor_scalar(s["sum"], d[2], -1.0, 1.0, ALU.mult, ALU.add))
            step(nc.vector.tensor_tensor(d[1], p[1], p[0], ALU.is_le))
            step(nc.vector.tensor_tensor(d[1], d[1], s["sum"], ALU.mult))
            step(nc.vector.tensor_tensor(d[0], s["sum"], d[1], ALU.subtract))
            step(nc.vector.tensor_scalar(s["drop"], s["drop"], -1.0, 1.0, ALU.mult, ALU.add))
            step(nc.vector.tensor_tensor(s["keep"], s["logit"], s["drop"], ALU.mult))
            step(nc.vector.tensor_reduce(s["sum"], te(s["keep"]), AXX, ALU.add))
            step(nc.vector.tensor_scalar(s["sum"], s["sum"], 1e-6, None, ALU.add))
            step(nc.vector.reciprocal(s["sum"], s["sum"]))
            nc.vector.tensor_tensor(s["keep"], s["keep"], one(s["sum"]), ALU.mult).then_inc(S["gates"], 1)
            dve.wait_ge(S["gates_loaded"], 16 * E)
            dve.wait_ge(S["acted"], T // n + 2)
            nc.vector.tensor_tensor(hidden, hidden, gates, ALU.mult)
    finish(nc, sems)


def mamba_input_block(nc, m, w, load, x, xc, gate):
    C, TAPS = DI // 128, 4
    LP = L + TAPS - 1
    s = carve(m.scratch[:], {f"{k}{j}": v for j in range(2) for k, v in (
        ("pad", (128, (C, GB, LP), F32)), ("conv", (128, (C, GB, L), F32)))})
    names = ("zero", "product", "padded", "tap", "conv", "silu")
    sems = signals(nc, "input", *names)
    S = dict(zip(names, sems))
    bl = lambda t: t.rearrange("p (b l) -> p b l", l=L)
    per = 2 * C
    with nc.Block() as block:
        @block.sync
        def _(sp):
            load(sp)

        @block.tensor
        def _(pe):
            pe.wait_ge(m.loaded, m.due)
            with pe.Fori(0, GROUPS // 2) as i:
                for j in range(2):
                    g = 2 * i + j
                    for k in range(per):
                        pe.wait_ge(S["padded"], per * g + k + 1)
                        for c in range(2):
                            last = nc.tensor.matmul(m.psum[:, k, 0:N], w["Win"][:, c, k * 128:k * 128 + 128],
                                                    x[:, c, span(g, N)], start=c == 0, stop=c == 1)
                        last.then_inc(S["product"], 1)

        @block.scalar
        def _(act):
            nc.scalar.preload_act_table_set(SILU)
            act.sem_inc(S["padded"], per)
            act.wait_ge(m.loaded, m.due)
            act.wait_ge(S["zero"], 2)
            with act.Fori(0, GROUPS // 2) as i:
                for j in range(2):
                    g = 2 * i + j
                    act.wait_ge(S["conv"], C * g + C)
                    for k in range(per):
                        act.wait_ge(S["product"], per * g + k + 1)
                        if k < C:
                            nc.scalar.activation(s[f"pad{j}"][:, k, :, TAPS - 1:LP], bl(m.psum[:, k, 0:N]),
                                                 ACT.Copy).then_inc(S["padded"], 1)
                        else:
                            nc.scalar.activation(gate[:, k - C, span(g, N)], m.psum[:, k, 0:N],
                                                 ACT.Silu).then_inc(S["padded"], 1)
                for j in range(2):
                    g = 2 * i + j
                    for k in range(C):
                        act.wait_ge(S["conv"], C * g + k + 7)
                        nc.scalar.activation(bl(xc[:, k, span(g, N)]), s[f"conv{j}"][:, k, :, :], ACT.Silu,
                                             bias=w["conv_b"][:, k:k + 1]).then_inc(S["silu"], 1)

        @block.vector
        def _(dve):
            dve.sem_inc(S["conv"], 6)
            for j in range(2):
                nc.vector.memset(s[f"pad{j}"][:, :, :, 0:TAPS - 1], 0.0).then_inc(S["zero"], 1)
            dve.wait_ge(m.loaded, m.due)
            dve.sem_inc(S["silu"], 6)
            with dve.Fori(0, GROUPS // 2) as i:
                for j in range(2):
                    g = 2 * i + j
                    dve.wait_ge(S["silu"], C * g + C)
                    for k in range(C):
                        dve.wait_ge(S["padded"], per * g + k + 7)
                        out = s[f"conv{j}"][:, k, :, :]
                        for tap in range(TAPS):
                            src = s[f"pad{j}"][:, k, :, tap:tap + L]
                            wt = w["conv_w"][:, k, tap:tap + 1]
                            if tap:
                                dve.wait_ge(S["tap"], (TAPS - 1) * (C * g + k) + tap)
                                ins = nc.vector.scalar_tensor_tensor(out=out, in0=src, scalar=wt, in1=out,
                                                                     op0=ALU.mult, op1=ALU.add)
                            else:
                                ins = nc.vector.tensor_scalar(out, src, wt, None, ALU.mult)
                            ins.then_inc(S["conv" if tap == TAPS - 1 else "tap"], 1)
    finish(nc, sems)


def mamba_rates_block(nc, m, w, load, xc, dt, coef, rates):
    n, C = N, DI // 128
    s = carve(m.scratch[:], {f"{k}{j}": v for j in range(2) for k, v in (
        ("mag", (128, (C, n), F32)), ("rest", (32, (n,), F32)), ("high", (32, (n,), BF16)),
        ("mid", (32, (n,), BF16)), ("raw", (1, (n,), F32)))})
    names = ("coefs", "raw", "product", "mag", "exp", "log", "max", "out", "high", "rest", "mid", "low", "rates",
             "negated")
    sems = signals(nc, "mrates", *names)
    S = dict(zip(names, sems))
    small = lambda j: m.psum[:, 3 + 4 * j, :]
    with nc.Block() as block:
        @block.sync
        def _(sp):
            load(sp)

        @block.tensor
        def _(pe):
            pe.wait_ge(m.loaded, m.due)
            with pe.Fori(0, T // n // 2) as i:
                for j in range(2):
                    g = 2 * i + j
                    pe.wait_ge(S["low"], g + 1)
                    pe.wait_ge(S["product"], g + 1)
                    pe.wait_ge(S["out"], g + 1)
                    for k in range(C):
                        nc.tensor.matmul(small(j)[0:32, 0:n], w["xproj"][:, k, 0:32], xc[:, k, span(g, n)],
                                         start=k == 0, stop=k == C - 1)
                    for k in range(C):
                        last = nc.tensor.matmul(m.psum[0:1, 4 * j, 0:n], w["xproj"][:, k, 32:33],
                                                xc[:, k, span(g, n)], start=k == 0, stop=k == C - 1)
                    last.then_inc(S["coefs"], 1)
                for j in range(2):
                    g = 2 * i + j
                    pe.wait_ge(S["raw"], g + 1)
                    for k in range(C):
                        last = nc.tensor.matmul(m.psum[:, 4 * j + k, 0:n], w["w_dt"][:, k * 128:k * 128 + 128],
                                                s[f"raw{j}"], start=True, stop=True)
                    last.then_inc(S["product"], 1)

        @block.scalar
        def _(act):
            nc.scalar.preload_act_table_set(LOG_EXP)
            act.wait_ge(m.loaded, m.due)
            nc.scalar.activation(rates, w["A_log"], ACT.Exp).then_inc(S["rates"], 1)
            with act.Fori(0, T // n // 2) as i:
                for j in range(2):
                    g = 2 * i + j
                    act.wait_ge(S["coefs"], g + 1)
                    act.wait_ge(S["product"], g + 1)
                    act.wait_ge(S["low"], g + 1)
                    nc.scalar.activation(s[f"raw{j}"], m.psum[0:1, 4 * j, 0:n], ACT.Copy).then_inc(S["raw"], 1)
                    nc.scalar.activation(s[f"high{j}"], small(j)[0:32, 0:n], ACT.Copy)
                    nc.scalar.activation(coef[0:32, span(g, n)], small(j)[0:32, 0:n], ACT.Copy
                                         ).then_inc(S["high"], 1)
                for j in range(2):
                    g = 2 * i + j
                    act.wait_ge(S["product"], g + 3)
                    act.wait_ge(S["out"], g + 1)
                    for k in range(C):
                        last = nc.scalar.activation(s[f"mag{j}"][:, k, :], m.psum[:, 4 * j + k, 0:n], ACT.Abs,
                                                    bias=w["b_dt"][:, k:k + 1])
                    last.then_inc(S["mag"], 1)
                    act.wait_ge(S["mag"], g + 1)
                    nc.scalar.activation(s[f"mag{j}"], s[f"mag{j}"], ACT.Exp, scale=-1.0).then_inc(S["exp"], 1)
                    act.wait_ge(S["exp"], g + 1)
                    nc.scalar.activation(s[f"mag{j}"], s[f"mag{j}"], ACT.Ln, bias=m.ones[:, 0:1]
                                         ).then_inc(S["log"], 1)
                    act.wait_ge(S["rest"], g + 1)
                    nc.scalar.activation(s[f"mid{j}"], s[f"rest{j}"], ACT.Copy)
                    nc.scalar.activation(coef[32:64, span(g, n)], s[f"rest{j}"], ACT.Copy).then_inc(S["mid"], 1)

        @block.vector
        def _(dve):
            dve.sem_inc(S["out"], 2)
            dve.sem_inc(S["low"], 2)
            dve.sem_inc(S["product"], 2)
            dve.wait_ge(m.loaded, m.due)
            dve.wait_ge(S["rates"], 1)
            nc.vector.tensor_scalar(rates, rates, -1.0, None, ALU.mult).then_inc(S["negated"], 1)
            with dve.Fori(0, T // n // 2) as i:
                for j in range(2):
                    g = 2 * i + j
                    dve.wait_ge(S["high"], g + 1)
                    nc.vector.tensor_tensor(s[f"rest{j}"], small(j)[0:32, 0:n], s[f"high{j}"],
                                            ALU.subtract).then_inc(S["rest"], 1)
                for j in range(2):
                    g = 2 * i + j
                    dve.wait_ge(S["mag"], g + 1)
                    for k in range(C):
                        last = nc.vector.tensor_scalar(dt[:, k, span(g, n)], m.psum[:, 4 * j + k, 0:n],
                                                       w["b_dt"][:, k:k + 1], 0.0, ALU.add, ALU.max)
                    last.then_inc(S["max"], 1)
                    dve.wait_ge(S["log"], g + 1)
                    dve.wait_ge(S["max"], g + 1)
                    d = dt[:, :, span(g, n)]
                    nc.vector.tensor_tensor(d, d, s[f"mag{j}"], ALU.add).then_inc(S["out"], 1)
                    dve.wait_ge(S["mid"], g + 1)
                    nc.vector.tensor_tensor(coef[64:96, span(g, n)], s[f"rest{j}"], s[f"mid{j}"],
                                            ALU.subtract).then_inc(S["low"], 1)
    finish(nc, sems)


def mamba_scan_block(nc, m, w, load, xc, gate, dt, coef, rates, dst):
    C, OWN = DI // 128, 1
    s = carve(m.scratch[:], {f"{k}{j}": (128, (C, N), F32) for j in range(2) for k in ("a", "b", "h", "y")}
              | {f"c{j}": (128, (1, N), F32) for j in range(2)}
              | {"pick": (96, (32,), BF16), "dtx": (128, (C, N), F32),
                 "gated": (128, (C, N), F32)})
    names = ("act_turn", "pick", "zero", "spread", "a", "b", "scan", "c", "y", "pool_y", "sum", "dtx", "skip", "gated", "out", "added")
    sems = signals(nc, "mscan", *names)
    S = dict(zip(names, sems))
    bl = lambda t: t.rearrange("p (b l) -> p b l", l=L)
    flat = lambda t: t.rearrange("p c t -> p (c t)")
    with nc.Block() as block:
        @block.sync
        def _(sp):
            load(sp)

        @block.tensor
        def _(pe):
            pe.wait_ge(m.loaded, m.due)
            pe.wait_ge(S["pick"], 1)

            def out(g, c):
                if c == 0:
                    pe.wait_ge(S["gated"], g + 1)
                pe.wait_ge(S["added"], 2 * g + c + 2)
                for k in range(C):
                    last = nc.tensor.matmul(m.psum[0:P, 7, 0:N], w["Wout"][:, k, c * P:c * P + P],
                                            s["gated"][:, k, :], start=k == 0, stop=k == C - 1)
                last.then_inc(S["out"], 1)

            def group(i, first):
                def spread(q):
                    pe.wait_ge(S["y"], STATES * i + q + 1)
                    pe.wait_ge(S["pool_y"], STATES * i + q + 1)
                    for k in range(2):
                        last = nc.tensor.matmul(m.psum[:, 2 * (q % 2) + k, 0:N],
                                                s["pick"][:, 16 * k + q:16 * k + q + 1].broadcast_to([96, 128]),
                                                coef[:, span(i, N)], start=True, stop=True)
                    last.then_inc(S["spread"], 1)

                def add(q):
                    pe.wait_ge(S["y"], STATES * i + q + 3)
                    pe.wait_ge(S["pool_y"], STATES * i + q + 3)
                    if q == 0 and not first:
                        pe.wait_ge(S["skip"], C * i)
                    for c in range(C):
                        last = nc.tensor.matmul(m.psum[:, 4 + c, 0:N], m.identity[:], s[f"y{q % 2}"][:, c, :],
                                                start=q == 0, stop=q == STATES - 1)
                    last.then_inc(S["sum"], 1)

                spread(0)
                spread(1)
                if not first:
                    out(i - 1, 0)
                for q in range(STATES):
                    if q + 2 < STATES:
                        spread(q + 2)
                    add(q)
                    if q == 0 and not first:
                        out(i - 1, 1)

            group(0, True)
            with pe.Fori(1, GROUPS) as i:
                group(i, False)
            for c in range(2):
                out(GROUPS - 1, c)

        @block.scalar
        def _(act):
            act.sem_inc(S["a"], 2)
            act.wait_ge(S["zero"], 2)
            with act.Fori(0, GROUPS) as i:
                for q in range(STATES):
                    act.wait_ge(S["scan"], STATES * i + q + 1)
                    own_wait(act, S["act_turn"])
                    for c in range(C):
                        last = nc.scalar.activation(bl(s[f"a{q % 2}"][:, c, :])[:, :, 1:L],
                                                    bl(dt[:, c, span(i, N)])[:, :, 1:L],
                                                    ACT.Exp, scale=rates[:, c, q:q + 1])
                    last.then_inc(S["a"], 1)
                    act.wait_ge(S["spread"], STATES * i + q + 1)
                    act.wait_ge(S["pool_y"], STATES * i + q + 1)
                    nc.scalar.activation(s[f"c{q % 2}"][:, 0, :], m.psum[:, 2 * (q % 2) + 1, 0:N],
                                         ACT.Copy).then_inc(S["c"], 1)

        @block.gpsimd
        def _(pool):
            pool.sem_inc(S["pool_y"], 2)
            with pool.Fori(0, GROUPS) as i:
                for q in range(STATES):
                    pool.wait_ge(S["c"], STATES * i + q + 1)
                    pool.wait_ge(S["scan"], STATES * i + q + 3)
                    pool.wait_ge(S["sum"], STATES * i + q + 1)
                    nc.gpsimd.tensor_tensor(s[f"y{q % 2}"][:, OWN:C, :], s[f"h{q % 2}"][:, OWN:C, :],
                                            s[f"c{q % 2}"].broadcast_to([128, C - OWN, N]),
                                            ALU.mult).then_inc(S["pool_y"], 1)

        @block.vector
        def _(dve):
            for k, v in (("y", 2), ("scan", 2), ("sum", 2), ("added", 2), ("out", 2)):
                dve.sem_inc(S[k], v)
            dve.wait_ge(m.loaded, m.due)
            nc.vector.tensor_copy(s["pick"], w["pick"]).then_inc(S["pick"], 1)
            for j in range(2):
                nc.vector.memset(s[f"a{j}"].rearrange("p c (b l) -> p c b l", l=L)[:, :, :, 0:1], 0.0
                                 ).then_inc(S["zero"], 1)

            def skip_and_gate(g):
                dve.wait_ge(S["sum"], STATES * g + STATES + 2)
                dve.wait_ge(S["out"], 2 * g + 2)
                for c in range(C):
                    nc.vector.scalar_tensor_tensor(out=s["gated"][:, c, :], in0=xc[:, c, span(g, N)],
                                                   scalar=w["D"][:, c:c + 1], in1=m.psum[:, 4 + c, 0:N],
                                                   op0=ALU.mult, op1=ALU.add).then_inc(S["skip"], 1)
                dve.wait_ge(S["skip"], C * g + C)
                nc.vector.tensor_tensor(s["gated"], s["gated"], gate[:, :, span(g, N)],
                                        ALU.mult).then_inc(S["gated"], 1)

            def add(g, c):
                dve.wait_ge(S["out"], 2 * g + c + 3)
                d = dst[:, c, span(g, N)]
                nc.vector.tensor_tensor(d, m.psum[0:P, 7, 0:N], d, ALU.add).then_inc(S["added"], 1)

            def group(i, first):
                nc.vector.tensor_tensor(s["dtx"], dt[:, :, span(i, N)], xc[:, :, span(i, N)],
                                        ALU.mult).then_inc(S["dtx"], 1)
                dve.wait_ge(S["dtx"], i + 1)

                def spread_of(q, k, n):
                    return m.psum[:, 2 * (q % 2) + k:2 * (q % 2) + k + 1, 0:N].broadcast_to([128, n, N])

                def inputs(q):
                    dve.wait_ge(S["spread"], STATES * i + q + 1)
                    dve.wait_ge(S["scan"], STATES * i + q + 1)
                    nc.vector.tensor_tensor(s[f"b{q % 2}"], s["dtx"], spread_of(q, 0, C), ALU.mult).then_inc(S["b"], 1)

                inputs(0)
                for q in range(STATES):
                    dve.wait_ge(S["a"], STATES * i + q + 3)
                    dve.wait_ge(S["b"], STATES * i + q + 1)
                    dve.wait_ge(S["y"], STATES * i + q + 1)
                    dve.wait_ge(S["pool_y"], STATES * i + q + 1)
                    nc.vector.tensor_tensor_scan(flat(s[f"h{q % 2}"]), flat(s[f"a{q % 2}"]), flat(s[f"b{q % 2}"]),
                                                 0.0, ALU.mult, ALU.add).then_inc(S["scan"], 1)
                    if q == 0 and not first:
                        skip_and_gate(i - 1)
                    if q + 1 < STATES:
                        inputs(q + 1)
                    dve.wait_ge(S["scan"], STATES * i + q + 3)
                    dve.wait_ge(S["sum"], STATES * i + q + 1)
                    dve.wait_ge(S["c"], STATES * i + q + 1)
                    nc.vector.tensor_tensor(s[f"y{q % 2}"][:, 0:OWN, :], s[f"h{q % 2}"][:, 0:OWN, :], spread_of(q, 1, OWN),
                                            ALU.mult).then_inc(S["y"], 1)
                    if q < 2 and not first:
                        add(i - 1, q)

            group(0, True)
            with dve.Fori(1, GROUPS) as i:
                group(i, False)
            skip_and_gate(GROUPS - 1)
            for c in range(2):
                add(GROUPS - 1, c)
    finish(nc, sems)


def route_block(nc, m, w, load, name, x, r, rows, tokens):
    E, K, STRIDE = r.experts, r.picks, r.stride
    R, TM, NT = STRIDE // TILE, r.steps, RT * K
    s = carve(m.scratch[:], {f"{k}{j}": v for j in range(2) for k, v in (
        ("x", (P, (2, ROWS), F32)), ("row", (128, (D,), F32)), ("score", (128, (E,), F32)),
        ("choice", (128, (E,), F32)), ("best", (128, (8,), F32)), ("index", (128, (8,), U32)),
        ("indexf", (128, (8,), F32)), ("hot", (128, (K, E), F32)), ("picked", (128, (K, E), F32)), ("ranked", (128, (K, E), F32)),
        ("mask", (128, (E,), BF16)), ("total", (128, (E,), BF16)))} | {
        "before": (128, (128,), BF16), "ones": (128, (128,), BF16), "router": (P, (2, E), F32),
        "expert": (128, (RT, K), F32), "rank": (128, (RT, K), F32), "keep": (128, (RT, K), F32),
        "slotf": (128, (RT, K), F32), "value": (128, (RT, K), F32),
        "sum": (128, (RT, 1), F32),
        "count": (128, (1,), F32), "steps": (128, (1,), F32), "over": (128, (R,), F32),
        "end": (128, (1,), F32), "passed": (128, (TM,), F32), "passed_steps": (128, (TM,), F32),
        "tabf": (1, (2 * TM + 8,), F32)})
    names = ("ids", "act_turn", "dve_turn", "copied", "products", "rows_out", "stored0", "stored1", "scores", "choice", "best",
             "index", "indexf", "hot", "mask", "total", "ranks", "picked", "done", "step", "exp", "slots",
             "count", "counted", "ends", "ended", "row_ready", "weighed")
    sems = signals(nc, name, *names)
    S = dict(zip(names, sems))
    stored = S["stored0"], S["stored1"]
    side = Scatter(nc, m, name + "_scatter", r, tokens, m.scratch[:, 10240:10304], S["slots"])
    per_k = lambda a: a.rearrange("p (a e) -> p a e", a=1).broadcast_to([128, K, E])
    with nc.Block() as block:
        @block.sync
        def _(sp):
            load(sp)

            def store(i):
                for j in range(2):
                    sp.wait_ge(S["rows_out"], 2 * i + j + 3)
                    sp.dma_start(rows[bass.ds((2 * i + j) * ROWS, ROWS), :], s[f"row{j}"]).then_inc(stored[j], 16)

            side.start(sp)
            store(0)
            with sp.Fori(1, RT // 2) as i:
                store(i)
                side.release(sp, i - 1)
            side.release(sp, RT // 2 - 1)
            for j in range(2):
                sp.wait_ge(stored[j], 16 * (RT // 2) + 16)

        @block.gpsimd
        def _(pool):
            nc.gpsimd.iota(r.ids, pattern=[[ROWS, RT], [0, 1]], base=0, channel_multiplier=1
                           ).then_inc(S["ids"], 1)
            pool.wait_ge(S["ids"], 1)

            pool.wait_ge(m.filled, m.all_filled)
            with pool.Fori(0, RT // 2) as i:
                side.scatter(pool, i)
            side.wait(pool)

        @block.tensor
        def _(pe):
            pe.sem_inc(S["products"], 2)
            pe.sem_inc(S["ranks"], 1)
            pe.wait_ge(m.loaded, m.due)
            pe.wait_ge(S["row_ready"], 4)

            def products(i):
                for j in range(2):
                    t = 2 * i + j
                    pe.wait_ge(S["copied"], t + 1)
                    pe.wait_ge(S["rows_out"], t + 1)
                    pe.wait_ge(S["scores"], t + 1)
                    for c in range(2):
                        nc.tensor.transpose(m.psum[:, 4 * j, c * P:c * P + P], s[f"x{j}"][:, c, :],
                                            m.identity[0:P, 0:P])
                    for c in range(2):
                        last = nc.tensor.matmul(m.psum[:, 4 * j + 1, 0:E], s[f"x{j}"][:, c, :], s["router"][:, c, :],
                                                start=c == 0, stop=c == 1)
                    last.then_inc(S["products"], 1)

            def ranks(i):
                for j in range(2):
                    t = 2 * i + j
                    pe.wait_ge(S["mask"], t + 1)
                    pe.wait_ge(S["total"], t + 1)
                    nc.tensor.matmul(m.psum[:, 4 * j + 2, 0:E], s["before"], s[f"mask{j}"], start=True, stop=False)
                    nc.tensor.matmul(m.psum[:, 4 * j + 2, 0:E], s["ones"], s[f"total{j}"], start=False, stop=True
                                     ).then_inc(S["ranks"], 1)

            products(0)
            with pe.Fori(0, RT // 2 - 1) as i:
                products(i + 1)
                ranks(i)
            ranks(RT // 2 - 1)
            pe.wait_ge(S["total"], RT + 1)
            nc.tensor.matmul(m.psum[0:E, 3, 0:1], s["total0"], s["ones"][:, 0:1], start=True, stop=True
                             ).then_inc(S["count"], 1)
            pe.wait_ge(S["counted"], 3)
            nc.tensor.matmul(m.psum[0:E, 3, 1:2], w["upto"][0:E, 0:E], s["steps"][0:E, :], start=True, stop=True
                             ).then_inc(S["count"], 1)
            pe.wait_ge(S["ended"], 3)
            one = m.ones[0:E, 0:1]
            nc.tensor.matmul(m.psum[0:1, 7, 0:TM], one, s["passed"][0:E, :], start=True, stop=True)
            nc.tensor.matmul(m.psum[0:1, 7, TM:2 * TM], one, s["passed_steps"][0:E, :], start=True, stop=True)
            nc.tensor.matmul(m.psum[0:1, 7, 2 * TM:2 * TM + 1], one, s["steps"][0:E, :], start=True, stop=True
                             ).then_inc(S["count"], 1)

        @block.scalar
        def _(act):
            def copy(i):
                for j in range(2):
                    t = 2 * i + j
                    act.wait_ge(S["products"], t + 1)
                    own_wait(act, S["act_turn"])
                    nc.scalar.activation(s[f"x{j}"], x[:, :, span(t, ROWS)], ACT.Copy).then_inc(S["copied"], 1)

            nc.scalar.preload_act_table_set(SIGMOID)
            act.sem_inc(stored[0], 16)
            act.sem_inc(stored[1], 16)
            act.sem_inc(S["rows_out"], 2)
            act.sem_inc(S["scores"], 2)

            def evacuate(i):
                for j in range(2):
                    t = 2 * i + j
                    act.wait_ge(S["products"], t + 3)
                    act.wait_ge(stored[j], 16 * i + 16)
                    nc.scalar.activation(s[f"row{j}"], m.psum[:, 4 * j, 0:D], ACT.Copy).then_inc(S["rows_out"], 1)
                    act.wait_ge(S["done"], t + 1)
                    nc.scalar.activation(s[f"score{j}"], m.psum[:, 4 * j + 1, 0:E],
                                         ACT.Sigmoid if r.sigmoid else ACT.Copy).then_inc(S["scores"], 1)

            copy(0)
            with act.Fori(0, RT // 2 - 1) as i:
                evacuate(i)
                copy(i + 1)
            evacuate(RT // 2 - 1)
            if not r.sigmoid:
                act.wait_ge(S["step"], 4)
                nc.scalar.activation(s["value"], s["value"], ACT.Exp).then_inc(S["exp"], 1)

        @block.vector
        def _(dve):
            done = [0]

            def step(ins):
                done[0] += 1
                ins.then_inc(S["step"], 1)
                dve.wait_ge(S["step"], done[0])

            dve.sem_inc(S["done"], 2)
            dve.sem_inc(S["picked"], 4)
            dve.wait_ge(m.loaded, m.due)
            nc.vector.tensor_copy(s["before"], w["before"]).then_inc(S["row_ready"], 1)
            nc.vector.tensor_copy(s["ones"], m.ones[:]).then_inc(S["row_ready"], 1)
            for c in range(2):
                if r.scaled:
                    ins = nc.vector.tensor_scalar(s["router"][:, c, :], w["router"][:, c, :], w["gamma"][:, c:c + 1],
                                                  None, ALU.mult)
                else:
                    ins = nc.vector.tensor_copy(s["router"][:, c, :], w["router"][:, c, :])
                ins.then_inc(S["row_ready"], 1)
            nc.vector.memset(s["total0"], 0.0).then_inc(S["total"], 1)
            with dve.Fori(0, RT // 2) as i:
                tiles = [(j, 2 * i + j) for j in range(2)]
                at = lambda a, t: a[:, bass.ds(t, 1), :].rearrange("p a k -> p (a k)")
                choice = [s[f"choice{j}"] if r.bias else s[f"score{j}"] for j in range(2)]

                def total(j, t):
                    dve.wait_ge(S["mask"], t + 1)
                    dve.wait_ge(S["total"], t + 1)
                    dve.wait_ge(S["ranks"], t + 1)
                    nc.vector.tensor_tensor(s[f"total{1 - j}"], s[f"total{j}"], s[f"mask{j}"], ALU.add
                                            ).then_inc(S["total"], 1)

                for j, t in tiles:
                    dve.wait_ge(S["scores"], t + 3)
                    dve.wait_ge(S["done"], t + 1)
                    if r.bias:
                        nc.vector.tensor_tensor(choice[j], s[f"score{j}"], w["bias"], ALU.add).then_inc(S["choice"], 1)
                for j, t in tiles:
                    if r.bias:
                        dve.wait_ge(S["choice"], t + 1)
                    own_wait(dve, S["dve_turn"])
                    nc.vector.max(s[f"best{j}"], choice[j]).then_inc(S["best"], 1)
                for j, t in tiles:
                    dve.wait_ge(S["best"], t + 1)
                    own_wait(dve, S["dve_turn"])
                    nc.vector.max_index(s[f"index{j}"], s[f"best{j}"], choice[j]).then_inc(S["index"], 1)
                for j, t in tiles:
                    dve.wait_ge(S["index"], t + 1)
                    nc.vector.tensor_copy(s[f"indexf{j}"], s[f"index{j}"]).then_inc(S["indexf"], 1)
                dve.wait_ge(S["picked"], 4 * i + 4)
                for j, t in tiles:
                    dve.wait_ge(S["indexf"], t + 1)
                    nc.vector.tensor_copy(at(s["expert"], t), s[f"indexf{j}"][:, 0:K])
                    nc.vector.tensor_tensor(s[f"hot{j}"], per_k(w["iota"]),
                                            s[f"indexf{j}"][:, 0:K].rearrange("p (k a) -> p k a", a=1)
                                            .broadcast_to([128, K, E]), ALU.is_equal).then_inc(S["hot"], 1)
                for j, t in tiles:
                    dve.wait_ge(S["hot"], t + 1)
                    with nc.allow_low_precision("sums of zeros and ones"):
                        nc.vector.tensor_reduce(s[f"mask{j}"], s[f"hot{j}"].rearrange("p k e -> p e k"), AXX,
                                                ALU.add).then_inc(S["mask"], 1)
                total(*tiles[0])
                if r.sigmoid:
                    for j, t in tiles:
                        nc.vector.tensor_tensor(s[f"picked{j}"], s[f"hot{j}"], per_k(s[f"score{j}"]), ALU.mult
                                                ).then_inc(S["weighed"], 1)
                total(*tiles[1])
                for j, t in tiles:
                    if r.sigmoid:
                        dve.wait_ge(S["weighed"], t + 1)
                        nc.vector.tensor_reduce(at(s["value"], t), s[f"picked{j}"], AXX, ALU.add
                                                ).then_inc(S["done"], 1)
                    else:
                        nc.vector.tensor_copy(at(s["value"], t), s[f"best{j}"][:, 0:K]).then_inc(S["done"], 1)
                for j, t in tiles:
                    dve.wait_ge(S["ranks"], t + 2)
                    nc.vector.tensor_tensor(s[f"ranked{j}"], s[f"hot{j}"], per_k(m.psum[:, 4 * j + 2, 0:E]),
                                            ALU.mult).then_inc(S["picked"], 1)
                for j, t in tiles:
                    dve.wait_ge(S["picked"], 4 * i + 5 + j)
                    nc.vector.tensor_reduce(at(s["rank"], t), s[f"ranked{j}"], AXX, ALU.add).then_inc(S["picked"], 1)
                for j, t in tiles:
                    dve.wait_ge(S["picked"], 4 * i + 7 + j)
                    nc.vector.scalar_tensor_tensor(out=at(r.scatter, t), in0=at(s["expert"], t), scalar=float(T),
                                                   in1=at(s["rank"], t), op0=ALU.mult, op1=ALU.add
                                                   ).then_inc(S["slots"], 1)
            dve.wait_ge(S["done"], RT + 2)
            dve.wait_ge(S["picked"], 2 * RT + 4)
            weight, slot = r.weight, r.slot
            step(nc.vector.tensor_scalar(s["keep"], s["rank"], r.capacity - 0.5, None, ALU.is_lt))
            step(nc.vector.scalar_tensor_tensor(out=s["slotf"], in0=s["expert"], scalar=float(STRIDE), in1=s["rank"],
                                                op0=ALU.mult, op1=ALU.add))
            if r.sigmoid:
                step(nc.vector.tensor_reduce(s["sum"], s["value"], AXX, ALU.add))
                step(nc.vector.tensor_scalar(s["sum"], s["sum"], 1e-20, None, ALU.add))
            else:
                step(nc.vector.tensor_copy(s["sum"], s["value"][:, :, 0:1]))
                step(nc.vector.tensor_tensor(s["value"], s["value"], s["sum"].broadcast_to([128, RT, K]),
                                             ALU.subtract))
                dve.wait_ge(S["exp"], 1)
                step(nc.vector.tensor_reduce(s["sum"], s["value"], AXX, ALU.add))
            step(nc.vector.reciprocal(s["sum"], s["sum"]))
            step(nc.vector.tensor_tensor(s["value"], s["value"], s["sum"].broadcast_to([128, RT, K]), ALU.mult))
            step(nc.vector.scalar_tensor_tensor(out=weight, in0=s["value"], scalar=r.factor, in1=s["keep"],
                                                op0=ALU.mult, op1=ALU.mult))
            step(nc.vector.tensor_tensor(s["slotf"], s["slotf"], s["keep"], ALU.mult))
            step(nc.vector.tensor_scalar(s["keep"], s["keep"], -1.0, 1.0, ALU.mult, ALU.add))
            step(nc.vector.scalar_tensor_tensor(out=slot, in0=s["keep"], scalar=float(r.slots - 1), in1=s["slotf"],
                                                op0=ALU.mult, op1=ALU.add))
            dve.wait_ge(S["count"], 1)
            nc.vector.tensor_scalar(s["count"][0:E, :], m.psum[0:E, 3, 0:1], float(r.capacity), None, ALU.min
                                    ).then_inc(S["counted"], 1)
            dve.wait_ge(S["counted"], 1)
            nc.vector.tensor_scalar(s["over"][0:E, :], w["starts"][0:E, :], s["count"][0:E, :], None, ALU.is_lt
                                    ).then_inc(S["counted"], 1)
            dve.wait_ge(S["counted"], 2)
            nc.vector.tensor_reduce(s["steps"][0:E, :], s["over"][0:E, :], AXX, ALU.add).then_inc(S["counted"], 1)
            dve.wait_ge(S["count"], 2)
            nc.vector.tensor_copy(s["end"][0:E, :], m.psum[0:E, 3, 1:2]).then_inc(S["ended"], 1)
            dve.wait_ge(S["ended"], 1)
            nc.vector.tensor_scalar(s["passed"][0:E, :], w["numbers"][0:E, :], s["end"][0:E, :], None, ALU.is_ge
                                    ).then_inc(S["ended"], 1)
            dve.wait_ge(S["ended"], 2)
            nc.vector.tensor_scalar(s["passed_steps"][0:E, :], s["passed"][0:E, :], s["steps"][0:E, :], None,
                                    ALU.mult).then_inc(S["ended"], 1)
            dve.wait_ge(S["count"], 3)
            ps = m.psum[0:1, 7, :]
            tf = s["tabf"]
            step(nc.vector.tensor_tensor(tf[:, 0:TM], w["numbers"][0:1, :], ps[:, TM:2 * TM], ALU.subtract))
            step(nc.vector.tensor_scalar(tf[:, TM:2 * TM], tf[:, 0:TM], float(TILE), None, ALU.mult))
            step(nc.vector.scalar_tensor_tensor(out=tf[:, TM:2 * TM], in0=ps[:, 0:TM], scalar=float(STRIDE),
                                                in1=tf[:, TM:2 * TM], op0=ALU.mult, op1=ALU.add))
            step(nc.vector.tensor_scalar(tf[:, TM:2 * TM], tf[:, TM:2 * TM], float(E * STRIDE), None, ALU.min))
            step(nc.vector.tensor_scalar(tf[:, 0:TM], ps[:, 0:TM], float(E - 1), None, ALU.min))
            step(nc.vector.tensor_scalar(tf[:, 2 * TM:2 * TM + 1], ps[:, 2 * TM:2 * TM + 1], 0.5, 0.25, ALU.mult,
                                         ALU.add))
            nc.vector.tensor_copy(r.table[:, 0:2 * TM + 1], tf[:, 0:2 * TM + 1])
    finish(nc, sems + side.sems)


class Scatter:

    def __init__(self, nc, m, name, r, tokens, scratch, ready):
        self.nc, self.r, self.tokens = nc, r, tokens
        self.ready = ready
        self.s = carve(scratch, {f"{k}{j}": v for j in range(2) for k, v in (
            ("slots", (128, (r.picks,), U32)), ("token", (128, (1,), U32)))})
        self.sems = signals(nc, name, "staged", "slots_free", "scattered0", "scattered1", "pool_turn")
        self.staged, self.slots_free, *scattered, self.pool_turn = self.sems
        self.scattered = scattered

    def start(self, sp):
        sp.sem_inc(self.slots_free, 2)

    def release(self, sp, i):
        K = self.r.picks
        for j in range(2):
            sp.wait_ge(self.scattered[j], 16 * K * i + 16 * K)
            sp.sem_inc(self.slots_free, 1)

    def scatter(self, pool, i):
        nc, r, s = self.nc, self.r, self.s
        row = lambda a, t: a[:, bass.ds(t, 1), :].rearrange("p a k -> p (a k)")
        for j in range(2):
            t = 2 * i + j
            pool.wait_ge(self.ready, t + 1)
            pool.wait_ge(self.slots_free, t + 1)
            nc.gpsimd.tensor_copy(s[f"slots{j}"], row(r.scatter, t))
            nc.gpsimd.tensor_copy(s[f"token{j}"], row(r.ids, t)).then_inc(self.staged, 1)
            pool.wait_ge(self.staged, t + 1)
            own_wait(pool, self.pool_turn)
            for k in range(r.picks):
                nc.gpsimd.indirect_dma_start(
                    out=self.tokens, in_=s[f"token{j}"], in_offset=None,
                    out_offset=bass.IndirectOffsetOnAxis(ap=s[f"slots{j}"][:, k:k + 1], axis=0)
                ).then_inc(self.scattered[j], 16)

    def wait(self, pool):
        for j in range(2):
            pool.wait_ge(self.scattered[j], 16 * self.r.picks * (RT // 2))


class Gather:

    BUFFERS = 6

    def __init__(self, nc, name, r, y_rows, sums, gathered, scratch):
        self.nc, self.r, self.y_rows, self.sums, self.gathered = nc, r, y_rows, sums, gathered
        self.s = carve(scratch, {f"{k}{j}": (128, (r.picks,), t) for j in range(self.BUFFERS) for k, t in (
            ("slots", U32), ("weights", F32))} | {f"sum{j}": (128, (D,), F32) for j in range(self.BUFFERS)})
        self.sems = signals(nc, name, "staged", *(f"gathered{j}" for j in range(self.BUFFERS)), "weights", "sum", "pool_turn")
        self.staged, *arrived, self.weights, self.sum, self.pool_turn = self.sems
        self.arrived = arrived

    def row(self, a, t):
        return a[:, bass.ds(t, 1), :].rearrange("p a k -> p (a k)")

    def gpsimd(self, pool):
        nc, r, s, K = self.nc, self.r, self.s, self.r.picks
        pool.sem_inc(self.sum, self.BUFFERS * K)
        with pool.Fori(0, RT // self.BUFFERS) as i:
            for j in range(self.BUFFERS):
                t = self.BUFFERS * i + j
                pool.wait_ge(self.sum, K * t + K)
                nc.gpsimd.tensor_copy(s[f"slots{j}"], self.row(r.slot, t)).then_inc(self.staged, 1)
                pool.wait_ge(self.staged, t + 1)
                own_wait(pool, self.pool_turn)
                for k in range(K):
                    nc.gpsimd.indirect_dma_start(
                        out=self.gathered[j][:, k, :], out_offset=None, in_=self.y_rows,
                        in_offset=bass.IndirectOffsetOnAxis(ap=s[f"slots{j}"][:, k:k + 1], axis=0)
                    ).then_inc(self.arrived[j], 16)

    def vector(self, dve, i, j):
        nc, r, s, K = self.nc, self.r, self.s, self.r.picks
        for n in range(3 * j, 3 * j + 3):
            t, b = 6 * i + n, n
            dve.wait_ge(self.sum, K * t + K)
            nc.vector.tensor_copy(s[f"weights{b}"], self.row(r.weight, t)).then_inc(self.weights, 1)
            dve.wait_ge(self.weights, t + 1)
            dve.wait_ge(self.arrived[b], 16 * K * i + 16 * K)
            for k in range(K):
                g, wt, acc = self.gathered[b][:, k, :], s[f"weights{b}"][:, k:k + 1], s[f"sum{b}"]
                if k == 0:
                    ins = nc.vector.tensor_scalar(acc, g, wt, None, ALU.mult)
                else:
                    dve.wait_ge(self.sum, K * t + self.BUFFERS * K + k)
                    dst = self.row(self.sums, t) if k == K - 1 else acc
                    ins = nc.vector.scalar_tensor_tensor(out=dst, in0=g, scalar=wt, in1=acc, op0=ALU.mult,
                                                         op1=ALU.add)
                ins.then_inc(self.sum, 1)


def output_block(nc, m, name, load, sums, h, out):
    s = carve(m.scratch[:], {f"{k}{j}": v for j in range(2) for k, v in (
        ("h", (P, (2, ROWS), F32)), ("row", (128, (D,), F32)))})
    sems = signals(nc, name, "copied", "turned", "added", "stored0", "stored1")
    s_copied, s_turned, s_added, *s_stored = sems
    with nc.Block() as block:
        @block.sync
        def _(sp):
            load(sp)
            with sp.Fori(0, RT // 2) as i:
                for j in range(2):
                    t = 2 * i + j
                    sp.wait_ge(s_added, t + 3)
                    sp.dma_start(out[bass.ds(t * ROWS, ROWS), :], s[f"row{j}"]).then_inc(s_stored[j], 16)
            for j in range(2):
                sp.wait_ge(s_stored[j], 16 * (RT // 2) + 16)

        @block.scalar
        def _(act):
            with act.Fori(0, RT // 2) as i:
                for j in range(2):
                    t = 2 * i + j
                    act.wait_ge(s_turned, t + 1)
                    nc.scalar.activation(s[f"h{j}"], h[:, :, span(t, ROWS)], ACT.Copy).then_inc(s_copied, 1)

        @block.tensor
        def _(pe):
            pe.sem_inc(s_turned, 2)
            with pe.Fori(0, RT // 2) as i:
                for j in range(2):
                    t = 2 * i + j
                    pe.wait_ge(s_added, t + 1)
                    pe.wait_ge(s_copied, t + 1)
                    for c in range(2):
                        last = nc.tensor.transpose(m.psum[:, j, c * P:c * P + P], s[f"h{j}"][:, c, :],
                                                   m.identity[0:P, 0:P])
                    last.then_inc(s_turned, 1)

        @block.vector
        def _(dve):
            dve.sem_inc(s_added, 2)
            for j in range(2):
                dve.sem_inc(s_stored[j], 16)
            with dve.Fori(0, RT // 2) as i:
                for j in range(2):
                    t = 2 * i + j
                    dve.wait_ge(s_turned, t + 3)
                    dve.wait_ge(s_stored[j], 16 * i + 16)
                    nc.vector.tensor_tensor(s[f"row{j}"], sums[:, bass.ds(t, 1), :].rearrange("p a d -> p (a d)"),
                                            m.psum[:, j, 0:D], ALU.add).then_inc(s_added, 1)
    finish(nc, sems)


def expert_block(nc, m, load, name, r, rows, tokens, y_rows, wg, wu, wd, chunk, chunks, scale=None):
    E, TM = r.experts, r.steps
    F = chunk * chunks
    s = carve(m.scratch[:], {f"{k}{j}": v for j in range(2) for k, v in (
        ("index", (P, (2,), U32)), ("gathered", (P, (2, D), F32)), ("x", (P, (2, TILE), F32)),
        ("silu", (chunk, (TILE,), F32)), ("hidden", (chunk, (chunks, TILE), F32)), ("y", (P, (2, D), F32)),
        ("scale", (P, (2,), F32)))})
    wb = carve(m.full[:, 4:10, :].rearrange("p a t -> p (a t)"), {f"{k}{j}": v for j in range(2) for k, v in (
        ("wg", (P, (2, F), F32)), ("wu", (P, (2, F), F32)), ("wd", (chunk, (chunks, D), F32)))})
    names = ("index0", "index1", "weights0", "weights1", "gathered0", "gathered1", "turned", "x", "up", "silu",
             "hidden", "down", "y", "stored0", "stored1", "down_weights0", "down_weights1", "pool_turn", "act_turn", "sp_turn")
    sems = signals(nc, name, *names)
    S = dict(zip(names, sems))
    pair = lambda k: (S[k + "0"], S[k + "1"])
    s_index, s_weights, s_down_weights, s_gathered, s_stored = map(
        pair, ("index", "weights", "down_weights", "gathered", "stored"))
    loads = 16 * (2 if scale is None else 3)
    trips = lambda eng: eng.value_load(r.table[0:1, 2 * TM:2 * TM + 1], min_val=1, max_val=TM // 2)
    first_slot = lambda eng, t: eng.value_load(r.table[0:1, bass.ds(t + TM, 1)], min_val=0, max_val=E * r.stride)
    with nc.Block() as block:
        @block.sync
        def _(sp):
            load(sp)
            with sp.Fori(0, trips(sp)) as i:
                for j in range(2):
                    t = 2 * i + j
                    at = first_slot(sp, t)
                    sp.wait_ge(S["turned"], t + 1)
                    own_wait(sp, S["sp_turn"])
                    sp.dma_start(s[f"index{j}"], tokens[bass.ds(at * (T // r.stride), TILE), :].rearrange("(p h) a -> p (h a)", h=2)
                                 ).then_inc(s_index[j], 16)
                for j in range(2):
                    t = 2 * i + j
                    e = sp.value_load(r.table[0:1, bass.ds(t, 1)], min_val=0, max_val=E - 1)
                    sp.wait_ge(S["up"], chunks * t + chunks)
                    own_wait(sp, S["sp_turn"])
                    for k, src in ((wb[f"wg{j}"], wg), (wb[f"wu{j}"], wu)):
                        sp.dma_start(k, src[bass.ds(e, 1)].rearrange("e p c f -> p (e c) f")
                                     ).then_inc(s_weights[j], 16)
                    if scale is not None:
                        sp.dma_start(s[f"scale{j}"], scale[bass.ds(e, 1)].rearrange("e p c -> p (e c)")
                                     ).then_inc(s_weights[j], 16)
                for j in range(2):
                    t = 2 * i + j
                    e = sp.value_load(r.table[0:1, bass.ds(t, 1)], min_val=0, max_val=E - 1)
                    sp.wait_ge(S["down"], t + 1)
                    own_wait(sp, S["sp_turn"])
                    sp.dma_start(wb[f"wd{j}"], wd[bass.ds(e, 1)].rearrange("e p c f -> p (e c) f")
                                 ).then_inc(s_down_weights[j], 16)

        @block.gpsimd
        def _(pool):
            with pool.Fori(0, trips(pool)) as i:
                for j in range(2):
                    t = 2 * i + j
                    pool.wait_ge(s_index[j], 16 * i + 16)
                    pool.wait_ge(S["turned"], t + 1)
                    own_wait(pool, S["pool_turn"])
                    for h in range(2):
                        nc.gpsimd.indirect_dma_start(
                            out=s[f"gathered{j}"][:, h, :], out_offset=None, in_=rows,
                            in_offset=bass.IndirectOffsetOnAxis(ap=s[f"index{j}"][:, h:h + 1], axis=0)
                        ).then_inc(s_gathered[j], 16)

        @block.tensor
        def _(pe):
            pe.sem_inc(S["down"], 2)
            pe.sem_inc(S["up"], 2 * chunks)
            pe.sem_inc(S["turned"], 2)
            with pe.Fori(0, trips(pe)) as i:
                for j in range(2):
                    t = 2 * i + j
                    pe.wait_ge(s_gathered[j], 32 * i + 32)
                    pe.wait_ge(S["x"], t + 1)
                    for c in range(2):
                        for h in range(2):
                            last = nc.tensor.transpose(m.psum[0:P, 4 + j, c * TILE + h * HALF:c * TILE + h * HALF + HALF],
                                                       s[f"gathered{j}"][:, h, c * P:c * P + P],
                                                       m.identity[0:P, 0:P])
                    last.then_inc(S["turned"], 1)
                for j in range(2):
                    t = 2 * i + j
                    pe.wait_ge(S["x"], t + 3)
                    pe.wait_ge(s_weights[j], loads * i + loads)
                    for k in range(chunks):
                        pe.wait_ge(S["hidden"], chunks * t + k + 1)
                        for q, wt in enumerate((wb[f"wg{j}"], wb[f"wu{j}"])):
                            for c in range(2):
                                last = nc.tensor.matmul(m.psum[0:chunk, (j * chunks + k) % 4, q * TILE:q * TILE + TILE],
                                                        wt[:, c, k * chunk:k * chunk + chunk], s[f"x{j}"][:, c, :],
                                                        start=c == 0, stop=c == 1)
                        last.then_inc(S["up"], 1)
                for j in range(2):
                    t = 2 * i + j
                    pe.wait_ge(S["hidden"], chunks * t + chunks + 4)
                    pe.wait_ge(S["y"], t + 1)
                    pe.wait_ge(s_down_weights[j], 16 * i + 16)
                    for h in range(2):
                        for k in range(chunks):
                            last = nc.tensor.matmul(m.psum[0:P, 6 + j, h * D:h * D + D],
                                                    s[f"hidden{j}"][:, k, h * HALF:h * HALF + HALF],
                                                    wb[f"wd{j}"][:, k, :], start=k == 0, stop=k == chunks - 1)
                    last.then_inc(S["down"], 1)

        @block.scalar
        def _(act):
            nc.scalar.preload_act_table_set(SILU)
            act.sem_inc(S["x"], 2)
            act.sem_inc(S["y"], 2)
            for j in range(2):
                act.sem_inc(s_stored[j], 16)
            n = trips(act)
            with act.Fori(0, n) as i:
                for j in range(2):
                    t = 2 * i + j
                    act.wait_ge(S["turned"], t + 3)
                    act.wait_ge(S["down"], t + 1)
                    act.wait_ge(s_weights[j], loads * i + loads)
                    for c in range(2):
                        last = nc.scalar.activation(s[f"x{j}"][:, c, :], m.psum[0:P, 4 + j, c * TILE:c * TILE + TILE],
                                                    ACT.Copy if scale is None else ACT.Identity,
                                                    **({} if scale is None else {"scale": s[f"scale{j}"][:, c:c + 1]}))
                    last.then_inc(S["x"], 1)
                for j in range(2):
                    t = 2 * i + j
                    for k in range(chunks):
                        nth = j * chunks + k
                        act.wait_ge(S["up"], chunks * t + k + 1 + 2 * chunks)
                        act.wait_ge(S["hidden"], chunks * t + k + 3)
                        nc.scalar.activation(s[f"silu{nth % 2}"], m.psum[0:chunk, nth % 4, 0:TILE], ACT.Silu
                                             ).then_inc(S["silu"], 1)
                for j in range(2):
                    t = 2 * i + j
                    at = first_slot(act, t)
                    act.wait_ge(S["down"], t + 3)
                    act.wait_ge(s_stored[j], 16 * i + 16)
                    nc.scalar.activation(s[f"y{j}"], m.psum[0:P, 6 + j, 0:2 * D].rearrange("p (h d) -> p h d", h=2),
                                         ACT.Copy).then_inc(S["y"], 1)
                    act.wait_ge(S["y"], t + 3)
                    act.dma_start(y_rows[bass.ds(at, TILE), :].rearrange("(p h) d -> p h d", h=2), s[f"y{j}"]
                                  ).then_inc(s_stored[j], 16)
            for j in range(2):
                act.wait_ge(s_stored[j], 16 * n + 16)
            own_wait(act, S["act_turn"])

        @block.vector
        def _(dve):
            dve.sem_inc(S["hidden"], 4)
            with dve.Fori(0, trips(dve)) as i:
                for j in range(2):
                    t = 2 * i + j
                    dve.wait_ge(S["down"], t + 1)
                    for k in range(chunks):
                        nth = j * chunks + k
                        dve.wait_ge(S["silu"], chunks * t + k + 1)
                        nc.vector.tensor_tensor(s[f"hidden{j}"][:, k, :], s[f"silu{nth % 2}"],
                                                m.psum[0:chunk, nth % 4, TILE:2 * TILE], ALU.mult
                                                ).then_inc(S["hidden"], 1)
    finish(nc, sems)


def combine_block(nc, m, load, name, r, y_rows, h):
    K = r.picks
    s = carve(m.scratch[:], {f"{k}{j}": v for j in range(2) for k, v in (
        ("slots", (128, (K,), U32)), ("weights", (128, (K,), F32)), ("gathered", (128, (K, D), F32)),
        ("sum", (128, (D,), F32)))})
    names = ("pool_turn", "staged", "gathered0", "gathered1", "weights", "sum", "turned", "added")
    sems = signals(nc, name, *names)
    S = dict(zip(names, sems))
    s_gathered = (S["gathered0"], S["gathered1"])
    row = lambda a, t: a[:, bass.ds(t, 1), :].rearrange("p a k -> p (a k)")
    with nc.Block() as block:
        @block.sync
        def _(sp):
            load(sp)

        @block.gpsimd
        def _(pool):
            with pool.Fori(0, RT // 2) as i:
                for j in range(2):
                    t = 2 * i + j
                    pool.wait_ge(S["sum"], K * t + K)
                    nc.gpsimd.tensor_copy(s[f"slots{j}"], row(r.slot, t)).then_inc(S["staged"], 1)
                    pool.wait_ge(S["staged"], t + 1)
                    own_wait(pool, S["pool_turn"])
                    for k in range(K):
                        nc.gpsimd.indirect_dma_start(
                            out=s[f"gathered{j}"][:, k, :], out_offset=None, in_=y_rows,
                            in_offset=bass.IndirectOffsetOnAxis(ap=s[f"slots{j}"][:, k:k + 1], axis=0)
                        ).then_inc(s_gathered[j], 16)

        @block.tensor
        def _(pe):
            pe.sem_inc(S["turned"], 2)
            with pe.Fori(0, RT // 2) as i:
                for j in range(2):
                    t = 2 * i + j
                    pe.wait_ge(S["added"], t + 1)
                    pe.wait_ge(S["sum"], K * t + 3 * K)
                    for c in range(2):
                        last = nc.tensor.transpose(m.psum[0:P, j, c * ROWS:c * ROWS + ROWS],
                                                   s[f"sum{j}"][:, c * P:c * P + P], m.identity[:])
                    last.then_inc(S["turned"], 1)

        @block.vector
        def _(dve):
            dve.sem_inc(S["sum"], 2 * K)
            dve.sem_inc(S["added"], 2)
            with dve.Fori(0, RT // 2) as i:
                for j in range(2):
                    t = 2 * i + j
                    dve.wait_ge(S["sum"], K * t + K)
                    nc.vector.tensor_copy(s[f"weights{j}"], row(r.weight, t)).then_inc(S["weights"], 1)
                    dve.wait_ge(S["weights"], t + 1)
                    dve.wait_ge(s_gathered[j], 16 * K * i + 16 * K)
                    dve.wait_ge(S["turned"], t + 1)
                    for k in range(K):
                        g, wt = s[f"gathered{j}"][:, k, :], s[f"weights{j}"][:, k:k + 1]
                        if k == 0:
                            ins = nc.vector.tensor_scalar(s[f"sum{j}"], g, wt, None, ALU.mult)
                        else:
                            dve.wait_ge(S["sum"], K * t + 2 * K + k)
                            ins = nc.vector.scalar_tensor_tensor(out=s[f"sum{j}"], in0=g, scalar=wt, in1=s[f"sum{j}"],
                                                                 op0=ALU.mult, op1=ALU.add)
                        ins.then_inc(S["sum"], 1)
                for j in range(2):
                    t = 2 * i + j
                    dve.wait_ge(S["turned"], t + 3)
                    d = h[:, :, span(t, ROWS)]
                    nc.vector.tensor_tensor(d, m.psum[0:P, j, 0:2 * ROWS].rearrange("p (c t) -> p c t", c=2), d,
                                            ALU.add).then_inc(S["added"], 1)
    finish(nc, sems)



def program(nc, a, out):
    with ExitStack() as ctx:
        m = Memory(nc, ctx)
        blocks = []

        def stage(weights, block):
            blocks.append((weights, block))

        ln = lambda name, src, dst, **k: stage({}, lambda w, load: norm_block(nc, m, name, load, src, dst, 1e-5, **k))
        x0, x = m.act(0), m.act(2)

        def dram(name, shape, dt=F32):
            return nc.dram_tensor(name, shape, dt).ap()

        def matrix(name, parts, *shape, dt=F32):
            return {name.split("_", 2)[-1]: (parts, shape, dt, a[name])}

        def add_bias_and(dst, bias, n):
            return lambda dve, c, g, product: nc.vector.scalar_tensor_tensor(
                out=dst[:, c, span(g, n)], in0=product, scalar=bias[:, c:c + 1], in1=dst[:, c, span(g, n)],
                op0=ALU.add, op1=ALU.add)

        stage({"W": (128, (6, D), F32, a["tok_W"]), "b": (P, (2,), F32, a["tok_b"]),
               "pos": (P, (2, L), F32, a["tok_pos"])},
              lambda w, load: patch_block(nc, m, w, load, a["patches"]))

        ln("ln0a", m.h, x)
        stage({"Wqk": (P, (2, 128), F32, a["a0_Wqk"]), "Wff": (P, (2, 128), F32, a["a0_Wff"]),
               "Wv": (P, (2, D), F32, a["a0_Wv"]), "bf": (128, (1,), F32, a["a0_bf"]),
               "sign": (128, (1,), F32, a["c_sign"]), "carry": (128, (N,), F32, a["c_carry"]),
               "causal": (PAIR, (PAIR,), F32, a["c_causal"])},
              lambda w, load: decay_attention_block(nc, m, w, load, x, m.act(4)))
        stage({"gamma": (P, (2,), F32, a["a0_gamma"]), "beta": (P, (2,), F32, a["a0_beta"])},
              lambda w, load: norm_block(nc, m, "ln0h", load, m.act(4), m.act(4), 1e-5,
                                         gamma=w["gamma"], beta=w["beta"]))
        stage({"Wo": (P, (2, D), F32, a["a0_Wo"])},
              lambda w, load: project_block(nc, m, "out0", load, m.act(4), w["Wo"], m.h))

        f = "f0_"
        mask_rows = m.full[0:2, 10, :]
        stage({"gamma": (P, (2,), F32, a[f + "g1"]), "beta": (P, (2,), F32, a[f + "b1"])},
              lambda w, load: norm_block(nc, m, "ln0b", load, m.h, x0, 1e-5, gamma=w["gamma"], beta=w["beta"],
                                         twice=(x, 1e-5)))
        stage({"Wr": (P, (2,), F32, a[f + "Wr"]), "br": (P, (1,), F32, a[f + "br"].broadcast_to([P, 1])),
               "before": (B, (L, L), F32, a["c_before"].broadcast_to([B, L * L])
                          .rearrange("p (a b) -> p a b", a=L))},
              lambda w, load: mix_block(nc, m, w, load, x, m.act(4), m.act(6), m.full[0:P, 8, :],
                                        m.full[0:P, 9, :], mask_rows, dram("score_rows", (1, T)),
                                        dram("mask_dram", (2, T))))
        stage({**{k: (P, (2, D), F32, a[f + k]) for k in ("Wq", "Wk", "Wv", "Wo", "Wm")},
               **{k: (P, (2,), F32, a[f + k]) for k in ("bq", "bk", "bv")},
               "bom": (2, (D,), F32, a[f + "bom"]), "head": (P, (6,), F32, a["c_head"]),
               "rows": (3 * L, (2, P), F32, a["c_rows"])},
              lambda w, load: softmax_attention_block(nc, m, w, load, x, x0, m.act(4), m.full[0:P, 9, :],
                                                      mask_rows, m.act(6)))
        stage({"gamma": (P, (2,), F32, a[f + "g2"]), "beta": (P, (2,), F32, a[f + "b2"])},
              lambda w, load: norm_block(nc, m, "ln0g", load, m.act(6), x, 1e-5, gamma=w["gamma"],
                                         beta=w["beta"], add_to=m.h[:]))

        def layer0_mlp(w, load):
            mlp_block(nc, m, "mlp0", load, x, w["W1"], w["bf1"], w["W2"], add_bias_and(m.h, w["bf2"], WIDE),
                      ACT.Gelu)

        stage({"W1": (P, (2, HID), F32, a[f + "W1"]), "bf1": (128, (6,), F32, a[f + "bf1"]),
               "W2": (128, (6, D), F32, a[f + "W2"]), "bf2": (P, (2,), F32, a[f + "bf2"])}, layer0_mlp)

        coef, rates = m.coef[:], m.rates[:, 0:24]
        ln("ln1a", m.h, x)
        stage({"Wd": (P, (2, 256), F32, a["a1_Wd"]), "WBC": (P, (2, 32), F32, a["a1_WBC"]),
               "bd": (128, (2,), F32, a["a1_bd"]), "loglam": (128, (24,), F32, a["a1_loglam"])},
              lambda w, load: rates_block(nc, m, w, load, x, m.act(4, 2, 128), coef, rates))
        stage({"Wout": (128, (24, D), F32, a["a1_Wout"]), "bout": (P, (2,), F32, a["a1_bout"]),
               "pick": (96, (32,), F32, a["c_pick"])},
              lambda w, load: scan_block(nc, m, w, load, m.act(4, 2, 128), coef, rates))

        places = IMAGE_GROUPS * GB
        factor = m.full[0:P, 9, 0:places]
        table = m.full[0:1, 9, 128:128 + places + IMAGE_GROUPS + 1].bitcast(I32)
        ln("ln1b", m.h, x)
        stage({"Wg": (P, (2, 3), F32, a["f1_Wg"]), "before": (B, (B,), F32, a["c_tokens_before"][0:B, 0:B]),
               "numbers": (B, (places,), F32, a["c_numbers"][:, 0:places].broadcast_to([B, places])),
               "token": (B, (1,), F32, a["c_first_token"])},
              lambda w, load: image_route_block(nc, m, w, load, x, table, factor))
        stage({}, lambda w, load: image_expert_block(nc, m, load, x, table, factor, a["f1_W1"], a["f1_b1"],
                                                     a["f1_W2"], a["f1_b2"]))

        ln("ln2a", m.h, x)
        stage({"Wqkv": (P, (2, 3 * D), F32, a["a2_Wqkv"]), "bqk": (P, (4,), F32, a["a2_bqk"]),
               "bv": (PAIR, (D,), F32, a["a2_bv"].broadcast_to([PAIR, D])),
               "decay": (PAIR, (PAIR,), F32, a["c_decay"])},
              lambda w, load: retention_block(nc, m, w, load, x))

        hidden = m.full[0:24, 9, :]
        ln("ln2b", m.h, x)
        stage({"router": (P, (2, 3), F32, a["f2_router_w"]), "router_b": (3, (1,), F32, a["f2_router_b"]),
               "down": (P, (2, 24), F32, a["f2_down"])},
              lambda w, load: adapter_block(nc, m, w, load, x, m.full[0:3, 8, :], hidden, m.full[0:24, 10, :],
                                            dram("adapter_logits", (3, T)), dram("adapter_gates", (3, T))))

        def layer2_mlp(w, load):
            mlp_block(nc, m, "mlp2", load, x, w["w1"], w["b1"], w["w2"], add_bias_and(m.h, w["b2"], WIDE),
                      ACT.Gelu, extra=(w["up"], hidden))

        stage({"w1": (P, (2, HID), F32, a["f2_w1"]), "b1": (128, (6,), F32, a["f2_b1"]),
               "w2": (128, (6, D), F32, a["f2_w2"]), "b2": (P, (2,), F32, a["f2_b2"]),
               "up": (24, (D,), F32, a["f2_up"])}, layer2_mlp)

        xc, gate, dt = m.full[:, 5:8, :], m.full[:, 8:11, :], m.full[:, 2:5, :]
        coef3 = m.coef[0:96, :]
        rates3 = m.rates[:].rearrange("p (c n) -> p c n", n=STATES)
        stage({"gamma": (P, (2,), F32, a["a3_g_mamba"])},
              lambda w, load: norm_block(nc, m, "ln3a", load, m.h, x0, 1e-5, gamma=w["gamma"], twice=(x, 1e-6)))
        stage({"Win": (P, (2, 2 * DI), F32, a["a3_w_in"]), "conv_w": (128, (3, 4), F32, a["a3_conv_w"]),
               "conv_b": (128, (3,), F32, a["a3_conv_b"])},
              lambda w, load: mamba_input_block(nc, m, w, load, x, xc, gate))
        stage({"xproj": (128, (3, 33), F32, a["a3_w_xproj"]), "w_dt": (1, (DI,), F32, a["a3_w_dt"]),
               "b_dt": (128, (3,), F32, a["a3_b_dt"]), "A_log": (128, (3, STATES), F32, a["a3_A_log"])},
              lambda w, load: mamba_rates_block(nc, m, w, load, xc, dt, coef3, rates3))
        stage({"Wout": (128, (3, D), F32, a["a3_w_out"]), "D": (128, (3,), F32, a["a3_D_skip"]),
               "pick": (96, (32,), F32, a["c_pick"])},
              lambda w, load: mamba_scan_block(nc, m, w, load, xc, gate, dt, coef3, rates3, x0))
        stage({}, lambda w, load: add_block(nc, m, "addm", load, x0, m.h))
        r3 = Routing(m, E1, K1, STRIDE1, T, 32, False, 1.0)
        rows3, tokens3 = dram("rows3", (T, D)), dram("tokens3", (r3.token_slots, 1), U32)
        y3 = dram("y3", (r3.slots, D))
        m.zeroing(tokens3, 1)
        m.zeroing(y3, D)
        stage({}, lambda w, load: norm_block(nc, m, "rms3b", load, x0, x, 1e-6, centre=False))
        stage({"router": (P, (2, E1), F32, a["a3_w_router"]), "gamma": (P, (2,), F32, a["a3_g_moe"]),
               **route_constants(a, r3)},
              lambda w, load: route_block(nc, m, w, load, "route3", x, r3, rows3, tokens3))
        stage({}, lambda w, load: expert_block(nc, m, load, "experts3", r3, rows3, tokens3, y3, a["a3_w1"],
                                               a["a3_w3"], a["a3_w2"], 128, HID // 128, a["a3_g_exp"]))
        stage({}, lambda w, load: combine_block(nc, m, load, "combine3", r3, y3, m.h))

        r4 = Routing(m, E2, K2, STRIDE2, STRIDE2, E2 + 2, True, 2.5)
        rows4, tokens4 = dram("rows4", (T, D)), dram("tokens4", (r4.token_slots, 1), U32)
        y4 = dram("y4", (r4.slots, D))
        m.zeroing(tokens4, 1)
        m.zeroing(y4, D)
        ln("ln3b", m.h, x)
        stage({"router": (P, (2, E2), F32, a["f3_Wg"]), "bias": (128, (E2,), F32, a["f3_e_bias"].broadcast_to([128, E2])),
               **route_constants(a, r4)},
              lambda w, load: route_block(nc, m, w, load, "route4", x, r4, rows4, tokens4))
        flat = lambda t: t.rearrange("p a t -> p (a t)")
        sums = flat(m.full[:, 4:6, :])[:, 0:RT * D].rearrange("p (t d) -> p t d", d=D)
        gathered = [flat(m.full[:, 6:9, :])[:, j * K2 * D:(j + 1) * K2 * D].rearrange("p (k d) -> p k d", d=D)
                    for j in range(Gather.BUFFERS)]
        sides = (lambda: None, lambda: Gather(nc, "gather4", r4, y4, sums, gathered, m.scratch[:, 8192:9600]))

        def shared(part):
            n, chunks = SHARED // 2, 4
            return ({"Wsg": (P, (2, n), F32, a["f3_Wsg"][:, :, part * n:part * n + n]),
                     "Wsu": (P, (2, n), F32, a["f3_Wsu"][:, :, part * n:part * n + n]),
                     "Wsd": (n // chunks, (chunks, D), F32, a["f3_Wsd"][:, chunks * part:chunks * part + chunks, :])},
                    lambda w, load: gated_block(nc, m, f"shared{part}", load, x, w["Wsg"], w["Wsu"], w["Wsd"],
                                                n // chunks, chunks, sides[part]()))

        stage(*shared(0))
        stage({}, lambda w, load: expert_block(nc, m, load, "experts4", r4, rows4, tokens4, y4, a["f3_Wgate"],
                                               a["f3_Wup"], a["f3_Wdown"], 116, F2 // 116))
        stage(*shared(1))
        stage({}, lambda w, load: output_block(nc, m, "output", load, sums, m.h, out))

        share = -(-len(m.fills) // 14)
        m.all_filled = 16 * len(m.fills)
        placed = [carve(m.half[k % 2][:], {n: s[:3] for n, s in weights.items()})
                  for k, (weights, _) in enumerate(blocks)]

        def loader(k):
            def load(sp):
                for table, words in m.fills[(k - 1) * share:k * share] if k else []:
                    sp.dma_start(table, words).then_inc(m.filled, 16)
                if k < len(blocks):
                    for name, (_, _, _, source) in blocks[k][0].items():
                        sp.dma_start(placed[k][name], source).then_inc(m.arrived[k % 2], 16)
            return load

        def first_load(sp):
            loader(0)(sp)
            sp.dma_start(m.identity[:], a["c_identity"]).then_inc(m.setup, 16)
            sp.wait_ge(m.setup, 16)
        start_block(nc, m, first_load)
        dues = [0, 0]
        for k, (weights, block) in enumerate(blocks):
            dues[k % 2] += 16 * len(weights)
            m.loaded, m.due = m.arrived[k % 2], dues[k % 2]
            block(placed[k], loader(k + 1))


def route_constants(a, r):
    R = r.stride // TILE
    return {"before": (128, (128,), F32, a["c_tokens_before"]), "upto": (128, (128,), F32, a["c_upto"]),
            "iota": (128, (r.experts,), F32, a["c_numbers"][:, 0:r.experts].broadcast_to([128, r.experts])),
            "numbers": (128, (r.steps,), F32, a["c_numbers"][:, 0:r.steps].broadcast_to([128, r.steps])),
            "starts": (128, (R,), F32, a["c_starts"][:, 0:R].broadcast_to([128, R]))}


def add_block(nc, m, name, load, x, dst):
    with nc.Block() as block:
        @block.sync
        def _(sp):
            load(sp)

        @block.vector
        def _(dve):
            nc.vector.tensor_tensor(dst[:, 0, :], x[:, 0, :], dst[:, 0, :], ALU.add)

        @block.gpsimd
        def _(pool):
            nc.gpsimd.tensor_tensor(dst[:, 1, :], x[:, 1, :], dst[:, 1, :], ALU.add)



def layout(v):
    f32 = lambda x: np.ascontiguousarray(x, dtype=np.float32)
    rows = lambda x, k=2: f32(x.reshape(k, x.shape[0] // k, -1).transpose(1, 0, 2))
    col = lambda x, k=2: f32(x.reshape(k, -1).T)
    o = {}
    x = v["x"].reshape(B, 3, 6, 16, 6, 16).transpose(0, 2, 4, 1, 3, 5).reshape(GROUPS, N, PD // 128, 128)
    o["patches"] = f32(x.transpose(0, 3, 2, 1))
    o["tok_W"] = rows(v["L0_tok_W"].reshape(D, PD).T, PD // 128)
    o["tok_b"] = col(v["L0_tok_b"])
    i = np.arange(L, dtype=np.float32)[:, None]
    j = np.arange(D)
    angle = i / np.power(np.float32(10000.0), (2 * (j // 2)).astype(np.float32) / np.float32(D))
    angle = angle + np.where(j % 2 == 1, np.float32(np.pi / 2), np.float32(0))
    o["tok_pos"] = f32(np.sin(angle).astype(np.float32).T.reshape(2, P, L).transpose(1, 0, 2))
    t, u = np.arange(PAIR)[:, None], np.arange(PAIR)[None, :]
    o["c_causal"] = f32((t // L == u // L) & (t <= u))
    o["c_sign"] = f32(np.where(np.arange(128) < 64, -1, 1)[:, None])
    o["c_carry"] = f32(np.broadcast_to(np.arange(N) % L != 0, (128, N)))
    a, b = np.arange(L)[:, None], np.arange(L)[None, :]
    o["c_before"] = f32(b < a).reshape(1, L * L)
    o["c_head"] = f32(np.arange(P)[:, None] // DH == np.arange(6)[None, :])
    r, q, f = np.arange(3 * L)[:, None, None] // L, np.arange(2)[None, :, None], np.arange(P)[None, None, :]
    o["c_rows"] = f32(f // DH == 3 * q + r)
    o["c_identity"] = f32(np.eye(128))
    A = "L0_attn_"
    o["a0_Wqk"] = rows(np.concatenate([v[A + "Wq"], v[A + "Wk"]], 1))
    o["a0_Wff"] = rows(np.concatenate([v[A + "Wf"], v[A + "Wf"]], 1))
    o["a0_Wv"], o["a0_Wo"] = rows(v[A + "Wv"]), rows(v[A + "Wo"])
    o["a0_bf"] = f32(np.concatenate([v[A + "bf"], v[A + "bf"]])[:, None])
    o["a0_gamma"], o["a0_beta"] = col(v[A + "gamma"]), col(v[A + "beta"])
    A = "L0_ffn_"
    for k in ("Wq", "Wk", "Wv", "Wo", "Wm", "W1"):
        o["f0_" + k] = rows(v[A + k])
    for k in ("g1", "b1", "g2", "b2", "Wr", "bq", "bk", "bv", "bf2"):
        o["f0_" + k] = col(v[A + k])
    o["f0_br"] = f32(v[A + "br"].reshape(1, 1))
    o["f0_bom"] = f32(np.stack([v[A + "bo"], v[A + "bm"]]))
    o["f0_bf1"], o["f0_W2"] = col(v[A + "bf1"], 6), rows(v[A + "W2"], 6)
    A = "L1_attn_"
    twice = lambda x: np.concatenate([x[0:128], x[128:D], x[128:D]])
    o["a1_Wd"], o["a1_bd"] = rows(twice(v[A + "Wd"]).T), col(twice(v[A + "bd"]))
    o["a1_WBC"] = rows(np.concatenate([v[A + "WB"], v[A + "WC"]]).T)

    def by_chunk(x):
        tail = x[128:D].reshape(64, 8, 2, *x.shape[2:]).swapaxes(1, 2).swapaxes(0, 1)
        return f32(np.concatenate([x[0:128], tail.reshape(128, 8, *x.shape[2:])], 1))

    o["a1_loglam"] = by_chunk(v[A + "log_lambda"])
    o["a1_Wout"] = by_chunk(v[A + "Wout"].T.reshape(D, STATES, D))
    o["a1_bout"] = col(v[A + "bout"])
    k, n = np.arange(96)[:, None] % 32, np.arange(32)[None, :]
    o["c_pick"] = f32(k == n)
    A = "L1_ffn_"
    o["f1_Wg"] = rows(v[A + "Wg"].T)
    for key, cut, k in (("W1", rows, 2), ("W2", rows, 6), ("b1", col, 6), ("b2", col, 2)):
        o["f1_" + key] = f32(np.stack([cut(v[A + key][e], k) for e in range(3)]))
    A = "L2_attn_"
    o["a2_Wqkv"] = rows(v[A + "W_qkv"].T)
    o["a2_bqk"] = col(v[A + "b_qkv"][0:2 * D], 4)
    o["a2_bv"] = f32(v[A + "b_qkv"][None, 2 * D:])
    o["c_decay"] = f32(np.where((t // L == u // L) & (t <= u), 0.99 ** np.maximum(u - t, 0), 0) / np.sqrt(D))
    A = "L2_ffn_"
    o["f2_w1"], o["f2_b1"] = rows(v[A + "w1"]), col(v[A + "b1"], 6)
    o["f2_w2"], o["f2_b2"] = rows(v[A + "w2"], 6), col(v[A + "b2"])
    o["f2_router_w"], o["f2_router_b"] = rows(v[A + "router_w"]), f32(v[A + "router_b"][:, None])
    o["f2_down"] = rows(v[A + "w_down"].transpose(1, 0, 2).reshape(D, 24))
    o["f2_up"] = f32(v[A + "w_up"].reshape(24, D))
    A = "L3_attn_"
    for k in ("g_mamba", "g_moe"):
        o["a3_" + k] = col(v[A + k])
    for k in ("conv_b", "b_dt", "D_skip"):
        o["a3_" + k] = col(v[A + k], 3)
    for k in ("conv_w", "w_xproj", "A_log", "w_out"):
        o["a3_" + k] = rows(v[A + k], 3)
    o["a3_w_router"] = rows(v[A + "w_router"])
    per_expert = lambda x, k: f32(np.stack([rows(e, k) for e in x]))
    o["a3_w1"], o["a3_w3"], o["a3_w2"] = per_expert(v[A + "w1"], 2), per_expert(v[A + "w3"], 2), per_expert(v[A + "w2"], 6)
    o["a3_g_exp"] = f32(v[A + "g_exp"].reshape(E1, 2, P).transpose(0, 2, 1))
    A2 = "L3_ffn_"
    o["f3_Wg"], o["f3_e_bias"] = rows(v[A2 + "Wg"].T), f32(v[A2 + "e_bias"][None])
    o["f3_Wgate"], o["f3_Wup"] = (per_expert(v[A2 + "W_gate_up"][:, :, k * F2:k * F2 + F2], 2) for k in range(2))
    o["f3_Wdown"] = per_expert(v[A2 + "W_down"], 4)
    o["f3_Wsg"], o["f3_Wsu"], o["f3_Wsd"] = rows(v[A2 + "Wsg"]), rows(v[A2 + "Wsu"]), rows(v[A2 + "Wsd"], 8)
    q = np.arange(128)
    o["c_tokens_before"], o["c_upto"] = f32(q[:, None] < q[None, :]), f32(q[:, None] <= q[None, :])
    o["c_first_token"] = f32(np.arange(B) * L)[:, None]
    o["c_numbers"] = f32(np.arange(E2 + 2))[None]
    o["c_starts"] = f32(np.arange(STRIDE1 // TILE) * TILE)[None]
    o["a3_w_in"], o["a3_w_dt"] = rows(v[A + "w_in"]), f32(v[A + "w_dt"])
    return o

def kernel(**inputs):
    import concourse.bacc as bacc
    from concourse.bass_utils import run_bass_kernel_spmd

    arrays = layout({name: np.asarray(x) for name, x in inputs.items()})
    nc = bacc.Bacc("TRN2", target_bir_lowering=False, num_devices=1)
    dram = {name: nc.dram_tensor(name, x.shape, mybir.dt.from_np(x.dtype), kind="ExternalInput").ap()
            for name, x in arrays.items()}
    out = nc.dram_tensor("out", (T, D), F32, kind="ExternalOutput").ap()
    program(nc, dram, out)
    result = run_bass_kernel_spmd(nc, [arrays], core_ids=[0])
    return result.results[0]["out"].reshape(B, L, D)
```
